# Optimizing a Trainium2 kernel written in Bass

```python
import numpy as np
import jax
import jax.numpy as jnp

def _softmax(x, axis=-1):
    return jax.nn.softmax(x, axis=axis)

def _gelu(x):
    return jax.nn.gelu(x, approximate=True)

def _silu(x):
    return jax.nn.silu(x)

def _sigmoid(x):
    return jax.nn.sigmoid(x)

def _layernorm(x, axis=-1, eps=1e-05):
    m = jnp.mean(x, axis=axis, keepdims=True)
    v = jnp.var(x, axis=axis, keepdims=True)
    return (x - m) / jnp.sqrt(v + eps)

def _scatter_add(tgt, idx, src, axis=0):
    return tgt.at[idx].add(src)

def _segment_sum(src, seg, n):
    return jax.ops.segment_sum(src, seg, n)
kernel_name = 'mk_adaln_d1_jaxref_r4_5ee368'

def setup_inputs(seed: int=0):
    np.random.seed(seed)
    _w = jnp.asarray

    def _L0_attn_setup():
        import jax, jax.numpy as jnp
        import numpy as np
        B, S, D = (2, 512, 512)
        H, NOPE, ROPE, VD, LORA = (16, 128, 64, 128, 128)
        GS, BASE = (128, 10000.0)

        def _fp4_fakequant(w):
            wt = w.T
            K, N = wt.shape
            g = wt.reshape(K // GS, GS, N)
            amax = jnp.clip(jnp.max(jnp.abs(g), axis=1, keepdims=True), 1e-08, None)
            ws = jnp.clip(g / amax * 6.0, -6.0, 6.0)
            q = jnp.round(ws * 2.0)
            deq = q / 2.0 * (amax / 6.0)
            return deq.reshape(K, N)

        def _apply_rope(x, cos, sin):
            xe, xo = (x[..., ::2], x[..., 1::2])
            re = xe * cos - xo * sin
            ro = xo * cos + xe * sin
            return jnp.stack([re, ro], axis=-1).reshape(x.shape)
        key = jax.random.key(seed)
        ks = jax.random.split(key, 6)
        std = 0.02
        x = jax.random.normal(ks[0], (B, S, D), dtype=jnp.float32)
        wq = _fp4_fakequant(jax.random.normal(ks[1], (H * (NOPE + ROPE), D), dtype=jnp.float32) * std)
        wkv_a = _fp4_fakequant(jax.random.normal(ks[2], (LORA + ROPE, D), dtype=jnp.float32) * std)
        wkv_b = _fp4_fakequant(jax.random.normal(ks[3], (H * (NOPE + VD), LORA), dtype=jnp.float32) * std)
        wo = _fp4_fakequant(jax.random.normal(ks[4], (D, H * VD), dtype=jnp.float32) * std)
        return {'x': x, 'wq': wq, 'wkv_a': wkv_a, 'wkv_b': wkv_b, 'wo': wo}
    _L0_attn_in = _L0_attn_setup()

    def _L0_ffn_setup():
        import jax, jax.numpy as jnp
        import numpy as np
        B, S, D, F, E, SH, K = (2, 512, 512, 256, 16, 2, 2)

        def _experts_all(x, g, gb, w1, b1, w2, b2):
            y = jax.nn.gelu(jnp.einsum('bsd,edf->bsef', x, g) + gb, approximate=False)
            y = y * (jnp.einsum('bsd,edf->bsef', x, w1) + b1)
            return jnp.einsum('bsef,efd->bsed', y, w2) + b2
        key = jax.random.key(seed)
        ks = jax.random.split(key, 8)
        std = 0.02
        mk = lambda k, sh: jax.random.normal(k, sh, jnp.float32) * std
        return {'x': jax.random.normal(ks[0], (B, S, D), jnp.float32), 'wa': mk(ks[1], (D, E)), 'rg': mk(ks[2], (E, D, F)), 'rgb': jnp.zeros((E, F), jnp.float32), 'rw1': mk(ks[3], (E, D, F)), 'rb1': jnp.zeros((E, F), jnp.float32), 'rw2': mk(ks[4], (E, F, D)), 'rb2': jnp.zeros((E, D), jnp.float32), 'sg': mk(ks[5], (SH, D, F)), 'sgb': jnp.zeros((SH, F), jnp.float32), 'sw1': mk(ks[6], (SH, D, F)), 'sb1': jnp.zeros((SH, F), jnp.float32), 'sw2': mk(ks[7], (SH, F, D)), 'sb2': jnp.zeros((SH, D), jnp.float32)}
    _L0_ffn_in = _L0_ffn_setup()
    _L0_c = _w((lambda *s: np.random.randn(*s).astype(np.float32) * 0.05)(4, 512))
    _L0_wmod = _w((lambda *s: np.random.randn(*s).astype(np.float32) * 0.05)(512, 6 * 512) * 512 ** (-0.5))
    _d = {'L0_attn_x': _L0_attn_in['x'], 'L0_attn_wq': _L0_attn_in['wq'], 'L0_attn_wkv_a': _L0_attn_in['wkv_a'], 'L0_attn_wkv_b': _L0_attn_in['wkv_b'], 'L0_attn_wo': _L0_attn_in['wo'], 'L0_ffn_wa': _L0_ffn_in['wa'], 'L0_ffn_rg': _L0_ffn_in['rg'], 'L0_ffn_rgb': _L0_ffn_in['rgb'], 'L0_ffn_rw1': _L0_ffn_in['rw1'], 'L0_ffn_rb1': _L0_ffn_in['rb1'], 'L0_ffn_rw2': _L0_ffn_in['rw2'], 'L0_ffn_rb2': _L0_ffn_in['rb2'], 'L0_ffn_sg': _L0_ffn_in['sg'], 'L0_ffn_sgb': _L0_ffn_in['sgb'], 'L0_ffn_sw1': _L0_ffn_in['sw1'], 'L0_ffn_sb1': _L0_ffn_in['sb1'], 'L0_ffn_sw2': _L0_ffn_in['sw2'], 'L0_ffn_sb2': _L0_ffn_in['sb2'], 'L0_c': _L0_c, 'L0_wmod': _L0_wmod}
    _x0 = _d['L0_attn_x']
    _d['L0_attn_x'] = jax.random.normal(jax.random.fold_in(jax.random.key(seed), 1), (4, 512, 512), dtype=_x0.dtype)
    del _x0
    return _d

def reference(L0_attn_x, L0_attn_wq, L0_attn_wkv_a, L0_attn_wkv_b, L0_attn_wo, L0_ffn_wa, L0_ffn_rg, L0_ffn_rgb, L0_ffn_rw1, L0_ffn_rb1, L0_ffn_rw2, L0_ffn_rb2, L0_ffn_sg, L0_ffn_sgb, L0_ffn_sw1, L0_ffn_sb1, L0_ffn_sw2, L0_ffn_sb2, L0_c, L0_wmod):

    def _L0_attn_ref(x, wq, wkv_a, wkv_b, wo):
        import jax, jax.numpy as jnp
        import numpy as np
        B, S, D = (2, 512, 512)
        H, NOPE, ROPE, VD, LORA = (16, 128, 64, 128, 128)
        GS, BASE = (128, 10000.0)

        def _fp4_fakequant(w):
            wt = w.T
            K, N = wt.shape
            g = wt.reshape(K // GS, GS, N)
            amax = jnp.clip(jnp.max(jnp.abs(g), axis=1, keepdims=True), 1e-08, None)
            ws = jnp.clip(g / amax * 6.0, -6.0, 6.0)
            q = jnp.round(ws * 2.0)
            deq = q / 2.0 * (amax / 6.0)
            return deq.reshape(K, N)

        def _apply_rope(x, cos, sin):
            xe, xo = (x[..., ::2], x[..., 1::2])
            re = xe * cos - xo * sin
            ro = xo * cos + xe * sin
            return jnp.stack([re, ro], axis=-1).reshape(x.shape)
        b, s, _ = x.shape
        q = (x @ wq).reshape(b, s, H, NOPE + ROPE)
        q_nope, q_pe = (q[..., :NOPE], q[..., NOPE:])
        ckv = x @ wkv_a
        c, k_pe = (ckv[..., :LORA], ckv[..., LORA:])
        half = ROPE // 2
        inv_freq = 1.0 / BASE ** (jnp.arange(half, dtype=jnp.float32) * 2.0 / ROPE)
        freqs = jnp.arange(s, dtype=jnp.float32)[:, None] * inv_freq[None, :]
        cos, sin = (jnp.cos(freqs), jnp.sin(freqs))
        q_pe = _apply_rope(q_pe, cos[None, :, None, :], sin[None, :, None, :])
        k_pe = _apply_rope(k_pe, cos[None, :, :], sin[None, :, :])
        kv = (c @ wkv_b).reshape(b, s, H, NOPE + VD)
        k_nope, v = (kv[..., :NOPE], kv[..., NOPE:])
        k = jnp.concatenate([k_nope, jnp.broadcast_to(k_pe[:, :, None, :], (b, s, H, ROPE))], axis=-1)
        qf = jnp.concatenate([q_nope, q_pe], axis=-1)
        scale = 1.0 / np.sqrt(NOPE + ROPE)
        scores = jnp.einsum('bqhd,bkhd->bhqk', qf, k) * scale
        causal = jnp.tril(jnp.ones((s, s), dtype=bool))
        scores = jnp.where(causal[None, None], scores, jnp.float32(-1e+30))
        attn = jax.nn.softmax(scores, axis=-1)
        o = jnp.einsum('bhqk,bkhd->bqhd', attn, v).reshape(b, s, H * VD)
        return o @ wo

    def _L0_ffn_ref(x, wa, rg, rgb, rw1, rb1, rw2, rb2, sg, sgb, sw1, sb1, sw2, sb2):
        import jax, jax.numpy as jnp
        import numpy as np
        B, S, D, F, E, SH, K = (2, 512, 512, 256, 16, 2, 2)

        def _experts_all(x, g, gb, w1, b1, w2, b2):
            y = jax.nn.gelu(jnp.einsum('bsd,edf->bsef', x, g) + gb, approximate=False)
            y = y * (jnp.einsum('bsd,edf->bsef', x, w1) + b1)
            return jnp.einsum('bsef,efd->bsed', y, w2) + b2
        aff = jax.nn.sigmoid(jnp.einsum('bsd,de->bse', x, wa))
        topk_p, topk_i = jax.lax.top_k(aff, K)
        topk_p = topk_p / jnp.sum(topk_p, axis=-1, keepdims=True)
        combine = jnp.sum(jax.nn.one_hot(topk_i, E, dtype=x.dtype) * topk_p[..., None], axis=2)
        routed = jnp.einsum('bsed,bse->bsd', _experts_all(x, rg, rgb, rw1, rb1, rw2, rb2), combine)
        shared = jnp.sum(_experts_all(x, sg, sgb, sw1, sb1, sw2, sb2), axis=2)
        return x + shared + routed
    x = L0_attn_x
    mod = (_silu(L0_c) @ L0_wmod).reshape(L0_c.shape[0], 6, 1, -1)
    sa, ca, ga, sb, cb, gb = (mod[:, 0], mod[:, 1], mod[:, 2], mod[:, 3], mod[:, 4], mod[:, 5])
    ga = (2 * (ga >= 0) - 1) * jnp.maximum(jnp.abs(ga), 0.25)
    gb = (2 * (gb >= 0) - 1) * jnp.maximum(jnp.abs(gb), 0.25)
    h = _layernorm(x, axis=-1) * (1 + ca) + sa
    x = x + ga * _L0_attn_ref(h, L0_attn_wq, L0_attn_wkv_a, L0_attn_wkv_b, L0_attn_wo)
    h = _layernorm(x, axis=-1) * (1 + cb) + sb
    x = x + gb * _L0_ffn_ref(h, L0_ffn_wa, L0_ffn_rg, L0_ffn_rgb, L0_ffn_rw1, L0_ffn_rb1, L0_ffn_rw2, L0_ffn_rb2, L0_ffn_sg, L0_ffn_sgb, L0_ffn_sw1, L0_ffn_sb1, L0_ffn_sw2, L0_ffn_sb2)
    return x

_drawn_inputs = setup_inputs


def setup_inputs(seed=0):
    import zlib

    import numpy as np

    out = dict(_drawn_inputs(seed))
    spreads = {'L0_ffn_rgb': (0.0, 0.8),
     'L0_ffn_rb1': (0.0, 0.8),
     'L0_ffn_rb2': (0.0, 2.0),
     'L0_ffn_sgb': (0.0, 0.8),
     'L0_ffn_sb1': (0.0, 0.8),
     'L0_ffn_sb2': (0.0, 2.0)}
    factors = {'L0_attn_wq': 8.0,
     'L0_attn_wkv_a': 8.0,
     'L0_attn_wkv_b': 8.0,
     'L0_attn_wo': 8.0,
     'L0_ffn_wa': 3.321,
     'L0_ffn_rg': 8.0,
     'L0_ffn_rw1': 8.0,
     'L0_ffn_rw2': 8.0,
     'L0_ffn_sg': 4.516,
     'L0_ffn_sw1': 4.335,
     'L0_ffn_sw2': 4.233}
    for name, (base, spread) in spreads.items():
        noise = np.random.default_rng([zlib.crc32(name.encode()), seed]).standard_normal(out[name].shape)
        drawn = base * np.exp(spread * noise) if base else spread * noise
        out[name] = jnp.asarray(drawn.astype(out[name].dtype))
    for name, factor in factors.items():
        out[name] = (out[name] * factor).astype(out[name].dtype)
    return out
```

```python
from contextlib import ExitStack

import numpy as np
import concourse.bass as bass
from concourse import mybir

ALU = mybir.AluOpType
ACT = mybir.ActivationFunctionType
AX = mybir.AxisListType
F32 = mybir.dt.float32
F32R = mybir.dt.float32r
BF16 = mybir.dt.bfloat16
I32 = mybir.dt.int32
U32 = mybir.dt.uint32

B, S, D = 4, 512, 512
H, NOPE, ROPE, VD, LORA = 16, 128, 64, 128, 128
E, SH, F = 16, 2, 256
P = 128
DC = D // P
FC = F // P
TB = S // P
NT = B * TB
QD = NOPE + ROPE
KVD = NOPE + VD
SCALE = 1.0 / float(np.sqrt(NOPE + ROPE))
EPS = 1e-5
HALF = ROPE // 2
TOP = 2
NBLK = (B * S * TOP) // P + E
VECS = 6


class Chain:

    def __init__(self, eng, sem, base=0):
        self.eng, self.sem, self.base, self.n = eng, sem, base, 0

    def after(self, ins):
        ins.then_inc(self.sem, 1)
        self.wait()

    def wait(self):
        self.n += 1
        self.eng.wait_ge(self.sem, self.base + self.n)


class Kernel:

    def __init__(self, nc, ctx, ins, out):
        self.nc, self.ctx, self.out = nc, ctx, out
        self.ins = ins
        d = lambda name, shape, dt: nc.dram_tensor(name, shape, dt, kind="Internal").ap()
        self.mod_d = d("mod_d", [B, VECS * D], F32)
        self.wqk_d = d("wqk_d", [H, P, 2, DC, P], F32)
        self.hT_d = d("hT_d", [B, P, DC, 2, S], F32)
        self.cT_d = d("cT_d", [B, P, 2, S], F32)
        self.kpe_d = d("kpe_d", [B, P, 2, S], F32)
        self.c_d = d("c_d", [B, P, TB, 2, P], F32)
        self.qpe_d = d("qpe_d", [B, H, P, S], F32)
        self.attn_d = d("attn_d", [NT, P, D], F32)
        self.h2_d = d("h2_d", [B * S, D], F32)
        self.y_d = d("y_d", [NBLK * P, D], F32)
        self.idx_d = d("idx_d", [NBLK * P, 1], I32)
        self.ident = self.sb("ident", [P, P], F32)
        self.identb = self.sb("identb", [P, P], BF16)
        self.maskb = self.sb("maskb", [P, P], BF16)

    def sb(self, name, shape, dt, ctx=None):
        return (ctx or self.ctx).enter_context(self.nc.sbuf_tensor(name, shape, dt))

    def ps(self, name, shape, dt, ctx):
        return ctx.enter_context(self.nc.psum_tensor(name, shape, dt))

    def sem(self, name):
        return self.ctx.enter_context(self.nc.semaphore(name))


def split3(nc, out, pairs):
    last = None
    for n, (sh, sl, mh, ml) in enumerate(pairs):
        nc.tensor.matmul(out, sh, mh, start=n == 0, stop=False)
        nc.tensor.matmul(out, sh, ml, start=False, stop=False)
        last = nc.tensor.matmul(out, sl, mh, start=False, stop=n == len(pairs) - 1)
    return last


def stage_weights(K, Mhl, modcol):
    nc = K.nc
    with ExitStack() as ctx:
        sb = lambda n, s, d: K.sb(n, s, d, ctx)
        constf = sb("w_constf", [P, 2, P], F32)
        cs = sb("w_c", [B, D], F32)
        csg = sb("w_csg", [B, D], F32)
        csT = sb("w_csT", [P, DC, B], F32)
        wm = sb("w_wm", [P, 2, DC, D], F32)
        mrow = sb("w_mrow", [B, VECS, D], F32)
        msgn = sb("w_msgn", [B, 2, D], F32)
        wq = sb("w_wq", [P, 2, DC, P], F32)
        wkv = sb("w_wkv", [P, 2, KVD], F32)
        wo = sb("w_wo", [P, 2, D], F32)
        wqT = sb("w_wqT", [P, 2, D], F32)
        kvT = sb("w_kvT", [P, 2, KVD], F32)
        hl = sb("w_hl", [P, 2, 2, D], F32R)
        pq = K.ps("w_pq", [P, 2, D], F32, ctx)
        pk = K.ps("w_pk", [P, 2, D], F32, ctx)
        pw = K.ps("w_pw", [P, 2, D], F32, ctx)
        pm = K.ps("w_pm", [P, 2, D], F32, ctx)
        const_in, c_in, const_ok = K.sem("w_const_in"), K.sem("w_c_in"), K.sem("w_const_ok")
        silu, mod_t, mod_tc = K.sem("w_silu"), K.sem("w_mod_t"), K.sem("w_mod_tc")
        wm_in = [K.sem("w_wm_in0"), K.sem("w_wm_in1")]
        mod_mm, mod_ev, dch = K.sem("w_mod_mm"), K.sem("w_mod_ev"), K.sem("w_dch")
        mod_ok, col_t, col_ok, mod_out = K.sem("w_mod_ok"), K.sem("w_col_t"), K.sem("w_col_ok"), K.sem("w_mod_out")
        in_s = [K.sem("w_in0"), K.sem("w_in1")]
        out_s = [K.sem("w_out0"), K.sem("w_out1")]
        tr, ev_q, ev_k, mm = K.sem("w_tr"), K.sem("w_ev_q"), K.sem("w_ev_k"), K.sem("w_mm")
        hi_w, lo_w = K.sem("w_hi"), K.sem("w_lo")

        with nc.Block() as block:

            @block.sync
            def _(sp):
                sp.dma_start(constf[:, :, :], K.ins["c_const"][0:2].rearrange("a p c -> p a c")).then_inc(const_in, 16)
                sp.dma_start(cs[:, :], K.ins["L0_c"]).then_inc(c_in, 16)
                wmv = K.ins["L0_wmod"].rearrange("(c p) (v n) -> v p c n", p=P, n=D)
                for v in range(VECS):
                    if v >= 2:
                        sp.wait_ge(mod_mm, v - 1)
                    sp.dma_start(wm[:, v % 2], wmv[v]).then_inc(wm_in[v % 2], 16)
                def load(h, u):
                    sp.dma_start(wq[:, u], K.ins["L0_attn_wq"].rearrange("(c p) n -> p c n", p=P)[
                        :, :, bass.ds(h * QD, NOPE)]).then_inc(in_s[u], 16)
                    sp.dma_start(wkv[:, u], K.ins["L0_attn_wkv_b"][:, bass.ds(h * KVD, KVD)]).then_inc(in_s[u], 16)
                    sp.dma_start(wo[:, u], K.ins["L0_attn_wo"][bass.ds(h * VD, VD), :]).then_inc(in_s[u], 16)

                def heads(j, more):
                    for u in range(2):
                        h = j * 2 + u
                        if more:
                            sp.wait_ge(mm, h + 1)
                            load(h + 2, u)
                        sp.wait_ge(hi_w, h * 2 + 1)
                        sp.wait_ge(lo_w, h * 2 + 1)
                        sp.dma_start(K.wqk_d[bass.ds(h, 1)].rearrange("a p s c n -> p (a s) (c n)"),
                                     hl[:, u].bitcast(F32)).then_inc(out_s[u], 16)

                load(0, 0)
                load(1, 1)
                with sp.Fori(0, H // 2 - 1) as j:
                    heads(j, True)
                heads(H // 2 - 1, False)
                for u in range(2):
                    sp.wait_ge(out_s[u], 16 * (H // 2 + 1))
                sp.wait_ge(mod_ok, 1)
                sp.dma_start(K.mod_d.rearrange("b (v n) -> b v n", n=D), mrow[:, :, :]).then_inc(mod_out, 16)
                sp.wait_ge(mod_out, 16)

            @block.scalar
            def _(act):
                act.wait_ge(c_in, 16)
                nc.scalar.activation(csg[:, :], cs[:, :], ACT.Sigmoid).then_inc(silu, 1)
                act.sem_inc(out_s[0], 16)
                act.sem_inc(out_s[1], 16)
                with act.Fori(0, H // 2) as j:
                    for u in range(2):
                        h = j * 2 + u
                        act.wait_ge(tr, h + 1)
                        nc.scalar.activation(wqT[:, u], pq[:, u], ACT.Copy).then_inc(ev_q, 1)
                        act.wait_ge(mm, h + 1)
                        act.wait_ge(out_s[u], j * 16 + 16)
                        nc.scalar.activation(hl[:, u, 0], pw[:, u], ACT.Copy).then_inc(hi_w, 1)
                        nc.scalar.activation(Mhl[:, bass.ds(h, 1), 0, :].rearrange("p a n -> p (a n)"),
                                             pm[:, u], ACT.Copy).then_inc(hi_w, 1)

            @block.vector
            def _(dve):
                dve.wait_ge(const_in, 16)
                nc.vector.tensor_copy(K.ident[:, :], constf[:, 0]).then_inc(const_ok, 1)
                nc.vector.tensor_copy(K.identb[:, :], constf[:, 0]).then_inc(const_ok, 1)
                nc.vector.tensor_copy(K.maskb[:, :], constf[:, 1]).then_inc(const_ok, 1)
                dve.wait_ge(silu, 1)
                nc.vector.tensor_tensor(csg[:, :], csg[:, :], cs[:, :], ALU.mult).then_inc(silu, 1)
                dve.wait_ge(mod_t, 1)
                nc.vector.tensor_copy(csT[:, :, :], pk[:, 0, 0:DC * B].rearrange("p (c b) -> p c b", b=B)).then_inc(mod_tc, 1)
                for v in range(VECS):
                    dve.wait_ge(mod_mm, v + 1)
                    nc.vector.tensor_copy(mrow[:, v], pm[0:B, v % 2]).then_inc(mod_ev, 1)
                dve.wait_ge(mod_ev, VECS)
                ch = Chain(dve, dch)
                for v in (1, 4):
                    nc.vector.tensor_scalar(mrow[:, v], mrow[:, v], 1.0, None, ALU.add).then_inc(mod_ev, 1)
                for n, v in enumerate((2, 5)):
                    ch.after(nc.vector.tensor_scalar(msgn[:, n], mrow[:, v], 0.0, 2.0, ALU.is_ge, ALU.mult))
                    ch.after(nc.vector.tensor_scalar(msgn[:, n], msgn[:, n], -1.0, None, ALU.add))
                    ch.after(nc.vector.tensor_tensor(mrow[:, v], mrow[:, v], msgn[:, n], ALU.mult))
                    ch.after(nc.vector.tensor_scalar(mrow[:, v], mrow[:, v], 0.25, None, ALU.max))
                    ch.after(nc.vector.tensor_tensor(mrow[:, v], mrow[:, v], msgn[:, n], ALU.mult))
                dve.wait_ge(mod_ev, VECS + 2)
                nc.vector.tensor_scalar(msgn[:, 0], msgn[:, 0], 1.0, None, ALU.mult).then_inc(mod_ok, 1)
                dve.wait_ge(col_t, 1)
                nc.vector.tensor_copy(modcol[:, :, :, :], pk[:, 1, 0:2 * DC * B].rearrange(
                    "p (v c b) -> p b v c", v=2, c=DC)).then_inc(col_ok, 1)
                with dve.Fori(0, H // 2) as j:
                    for u in range(2):
                        h = j * 2 + u
                        dve.wait_ge(tr, h + 1)
                        nc.vector.tensor_copy(kvT[:, u], pk[:, u, 0:KVD]).then_inc(ev_k, 1)
                        dve.wait_ge(hi_w, h * 2 + 1)
                        nc.vector.tensor_tensor(hl[:, u, 1], pw[:, u], hl[:, u, 0].bitcast(F32),
                                                ALU.subtract).then_inc(lo_w, 1)
                        dve.wait_ge(hi_w, h * 2 + 2)
                        nc.vector.tensor_tensor(Mhl[:, bass.ds(h, 1), 1, :].rearrange("p a n -> p (a n)"), pm[:, u],
                                                Mhl[:, bass.ds(h, 1), 0, :].rearrange("p a n -> p (a n)").bitcast(F32),
                                                ALU.subtract).then_inc(lo_w, 1)

            @block.tensor
            def _(pe):
                pe.wait_ge(const_ok, 3)
                pe.wait_ge(silu, 2)
                for c in range(DC):
                    t = nc.tensor.transpose(pk[:, 0, c * B:(c + 1) * B], csg[:, c * P:(c + 1) * P], K.ident[0:B, 0:B])
                t.then_inc(mod_t, 1)
                pe.wait_ge(mod_tc, 1)
                for v in range(VECS):
                    pe.wait_ge(wm_in[v % 2], 16 * (v // 2 + 1))
                    if v >= 2:
                        pe.wait_ge(mod_ev, v - 1)
                    for c in range(DC):
                        m = nc.tensor.matmul(pm[0:B, v % 2], csT[:, c], wm[:, v % 2, c], start=c == 0, stop=c == DC - 1)
                    m.then_inc(mod_mm, 1)
                pe.wait_ge(mod_ok, 1)
                for v in range(2):
                    for c in range(DC):
                        o = (v * DC + c) * B
                        t = nc.tensor.transpose(pk[:, 1, o:o + B], mrow[:, v, c * P:(c + 1) * P], K.ident[0:B, 0:B])
                t.then_inc(col_t, 1)
                pe.wait_ge(col_ok, 1)
                with pe.Fori(0, H // 2) as j:
                    for u in range(2):
                        h = j * 2 + u
                        pe.wait_ge(in_s[u], j * 48 + 48)
                        for c in range(DC):
                            nc.tensor.transpose(pq[:, u, c * P:(c + 1) * P], wq[:, u, c], K.ident[:, :])
                        for n in range(2):
                            t = nc.tensor.transpose(pk[:, u, n * P:(n + 1) * P], wkv[:, u, n * P:(n + 1) * P], K.ident[:, :])
                        t.then_inc(tr, 1)
                    for u in range(2):
                        h = j * 2 + u
                        pe.wait_ge(ev_q, h + 1)
                        pe.wait_ge(ev_k, h + 1)
                        for c in range(DC):
                            nc.tensor.matmul(pw[:, u, c * P:(c + 1) * P], wqT[:, u, c * P:(c + 1) * P],
                                             kvT[:, u, 0:P], start=True, stop=True)
                        nc.tensor.matmul(pm[:, u], kvT[:, u, P:2 * P], wo[:, u], start=True, stop=True).then_inc(mm, 1)
                    pe.wait_ge(lo_w, j * 4 + 4)


def stage_project(K, modcol):
    nc = K.nc
    NQ = H * ROPE
    NC = LORA + ROPE
    with ExitStack() as ctx:
        sb = lambda n, s, d: K.sb(n, s, d, ctx)
        wst = sb("p_wst", [P, DC, NQ], F32)
        wpe = sb("p_wpe", [P, DC, 2, NQ], F32R)
        wcst = sb("p_wcst", [P, DC, NC], F32)
        wc = sb("p_wc", [P, DC, 2, NC], F32R)
        rope = sb("p_rope", [P, TB, ROPE], F32)
        half = sb("p_half", [P, 1], F32)
        x = sb("p_x", [P, 2, D], F32)
        st = sb("p_st", [P, 2, 6], F32)
        mv = sb("p_mv", [P, 2, 4], F32)
        hf = sb("p_hf", [P, 2, DC, P], F32)
        hT = sb("p_hT", [P, 2, DC, 2, P], F32R)
        cf = sb("p_cf", [P, 2, P], F32)
        chl = sb("p_chl", [P, 2, 2, P], F32R)
        qk = sb("p_qk", [P, 2, H + 1, ROPE], F32)
        rt = sb("p_rt", [P, 2, 4, H + 1, HALF], F32)
        qr = sb("p_qr", [P, 2, H + 1, ROPE], F32)
        qs = sb("p_qs", [P, 2, H, P], F32R)
        ck = sb("p_ck", [P, 2, 2, 2, P], F32R)
        px = K.ps("p_px", [P, 2, DC * P], F32, ctx)
        pc = K.ps("p_pc", [P, 512], F32, ctx)
        pq = K.ps("p_pq", [P, NQ], F32, ctx)
        pt = K.ps("p_pt", [P, 2, 4 * P], F32, ctx)
        pk = K.ps("p_pk", [P, 512], F32, ctx)
        w_in, w_hi, w_lo = K.sem("p_w_in"), K.sem("p_w_hi"), K.sem("p_w_lo")
        x_in = [K.sem("p_x_in0"), K.sem("p_x_in1")]
        pch, dch = K.sem("p_pch"), K.sem("p_dch")
        step_v, step_e = K.sem("p_step_v"), K.sem("p_step_e")
        var_ok, rstd_ok, x_n, x_t = K.sem("p_var_ok"), K.sem("p_rstd_ok"), K.sem("p_x_n"), K.sem("p_x_t")
        h_full, h_hi, h_lo = K.sem("p_h_full"), K.sem("p_h_hi"), K.sem("p_h_lo")
        proj, pev = K.sem("p_proj"), K.sem("p_pev")
        c_hi, c_lo = K.sem("p_c_hi"), K.sem("p_c_lo")
        rot_p, rot = K.sem("p_rot_p"), K.sem("p_rot")
        qt, q_hi, q_lo = K.sem("p_qt"), K.sem("p_q_hi"), K.sem("p_q_lo")
        kt, k_hi, k_lo = K.sem("p_kt"), K.sem("p_k_hi"), K.sem("p_k_lo")
        out_s = [K.sem("p_out0"), K.sem("p_out1")]
        NOUT = 5

        with nc.Block() as block:

            @block.sync
            def _(sp):
                xv = K.ins["L0_attn_x"].rearrange("b (t p) n -> (b t) p n", p=P)
                wqv = K.ins["L0_attn_wq"].rearrange("(c p) (h q) -> p c h q", p=P, q=QD)
                for c in range(DC):
                    sp.dma_start(wst[:, c].rearrange("p (h q) -> p h q", q=ROPE), wqv[:, c, :, NOPE:QD]).then_inc(w_in, 16)
                sp.dma_start(wcst[:, :, :], K.ins["L0_attn_wkv_a"].rearrange("(c p) n -> p c n", p=P)).then_inc(w_in, 16)
                sp.dma_start(rope[:, :, :], K.ins["c_rope"].rearrange("(t p) n -> p t n", p=P)).then_inc(w_in, 16)
                for u in range(2):
                    sp.dma_start(x[:, u], xv[u]).then_inc(x_in[u], 16)
                def tiles(j, more):
                    b = j // 2
                    for u in range(2):
                        t = j * 2 + u
                        ti = (j % 2) * 2 + u
                        tok = ti * P
                        if more:
                            sp.wait_ge(x_t, t + 1)
                            sp.dma_start(x[:, u], xv[bass.ds(t + 2, 1)].rearrange("a p n -> p (a n)")).then_inc(x_in[u], 16)
                        sp.wait_ge(h_hi, t + 1)
                        sp.wait_ge(h_lo, t + 1)
                        sp.dma_start(K.hT_d[bass.ds(b, 1), :, :, :, bass.ds(tok, P)].rearrange("a p c s n -> (a p) c s n"),
                                     hT[:, u].bitcast(F32)).then_inc(out_s[u], 16)
                        sp.wait_ge(c_hi, t + 1)
                        sp.wait_ge(c_lo, t + 1)
                        sp.dma_start(K.c_d[bass.ds(b, 1), :, bass.ds(ti, 1)].rearrange("a p t s n -> (a p) (t s) n"),
                                     chl[:, u].bitcast(F32)).then_inc(out_s[u], 16)
                        sp.wait_ge(k_hi, t + 1)
                        sp.wait_ge(k_lo, t + 1)
                        sp.dma_start(K.cT_d[bass.ds(b, 1), :, :, bass.ds(tok, P)].rearrange("a p s n -> (a p) s n"),
                                     ck[:, u, :, 0].bitcast(F32)).then_inc(out_s[u], 16)
                        sp.dma_start(K.kpe_d[bass.ds(b, 1), :, :, bass.ds(tok, P)].rearrange("a p s n -> (a p) s n"),
                                     ck[:, u, :, 1].bitcast(F32)).then_inc(out_s[u], 16)
                        sp.wait_ge(q_hi, t * 4 + 4)
                        sp.wait_ge(q_lo, t * 4 + 4)
                        sp.dma_start(K.qpe_d[bass.ds(b, 1), :, :, bass.ds(tok, P)].rearrange("a h p n -> p (a h) n"),
                                     qs[:, u].bitcast(F32)).then_inc(out_s[u], 16)

                with sp.Fori(0, NT // 2 - 1) as j:
                    tiles(j, True)
                tiles(NT // 2 - 1, False)
                for u in range(2):
                    sp.wait_ge(out_s[u], 16 * NOUT * (NT // 2 + 1))

            @block.gpsimd
            def _(pool):
                nc.gpsimd.memset(half[:, :], -0.5).then_inc(pch, 1)
                pool.wait_ge(pch, 1)
                with pool.Fori(0, NT // 2) as j:
                    for u in range(2):
                        t = j * 2 + u
                        ti = (j % 2) * 2 + u
                        pool.wait_ge(var_ok, t + 1)
                        nc.gpsimd.tensor_tensor(mv[:, u, 3:4], mv[:, u, 2:3], half[:, :], ALU.pow).then_inc(rstd_ok, 1)
                        pool.wait_ge(pev, t * 2 + 2)
                        sin = rope[:, bass.ds(ti, 1), HALF:ROPE].broadcast_to([P, H + 1, HALF])
                        nc.gpsimd.tensor_tensor(rt[:, u, 0], qk[:, u, :, 1::2], sin, ALU.mult)
                        nc.gpsimd.tensor_tensor(rt[:, u, 1], qk[:, u, :, 0::2], sin, ALU.mult).then_inc(rot_p, 1)

            @block.scalar
            def _(act):
                act.wait_ge(w_in, 96)
                nc.scalar.activation(wc[:, :, 0], wcst[:, :, :], ACT.Copy).then_inc(w_hi, 1)
                for c in range(DC):
                    nc.scalar.activation(wpe[:, c, 0], wst[:, c], ACT.Copy).then_inc(w_hi, 1)
                for u in range(2):
                    act.sem_inc(out_s[u], 16 * NOUT)
                with act.Fori(0, NT // 2) as j:
                    for u in range(2):
                        t = j * 2 + u
                        act.wait_ge(h_full, t + 1)
                        act.wait_ge(out_s[u], j * (16 * NOUT) + 16 * NOUT)
                        nc.scalar.activation(hT[:, u, :, 0], hf[:, u], ACT.Copy).then_inc(h_hi, 1)
                        act.wait_ge(proj, t * 2 + 1)
                        nc.scalar.activation(cf[:, u], pc[:, 0:LORA], ACT.Copy).then_inc(pev, 1)
                        nc.scalar.activation(qk[:, u, H], pc[:, LORA:NC], ACT.Copy)
                        nc.scalar.activation(chl[:, u, 0], pc[:, 0:LORA], ACT.Copy).then_inc(c_hi, 1)
                        act.wait_ge(proj, t * 2 + 2)
                        nc.scalar.activation(qk[:, u, 0:H].rearrange("p h q -> p (h q)"), pq[:, :], ACT.Copy).then_inc(pev, 1)
                        act.wait_ge(kt, t + 1)
                        nc.scalar.activation(ck[:, u, 0, 0], pk[:, 0:P], ACT.Copy)
                        nc.scalar.activation(ck[0:ROPE, u, 0, 1], pk[0:ROPE, P:2 * P], ACT.Copy)
                        nc.scalar.activation(ck[ROPE:P, u, 0, 1], pk[0:ROPE, P:2 * P], ACT.Copy).then_inc(k_hi, 1)
                        for g in range(4):
                            act.wait_ge(qt, t * 4 + g + 1)
                            nc.scalar.activation(qs[0:ROPE, u, 4 * g:4 * g + 4].rearrange("p h n -> p (h n)"), pt[0:ROPE, g % 2],
                                                 ACT.Copy, scale=SCALE).then_inc(q_hi, 1)

            @block.vector
            def _(dve):
                dve.wait_ge(w_hi, 1)
                nc.vector.tensor_tensor(wc[:, :, 1], wcst[:, :, :], wc[:, :, 0].bitcast(F32), ALU.subtract).then_inc(w_lo, 1)
                for c in range(DC):
                    dve.wait_ge(w_hi, c + 2)
                    nc.vector.tensor_tensor(wpe[:, c, 1], wst[:, c], wpe[:, c, 0].bitcast(F32), ALU.subtract).then_inc(w_lo, 1)

                def norm(j, u):
                    t = j * 2 + u
                    dve.wait_ge(x_in[u], j * 16 + 16)
                    ch = Chain(dve, dch, t * 4)
                    nc.vector.bn_stats(st[:, u], x[:, u]).then_inc(ch.sem, 1)
                    ch.wait()
                    dve.sem_inc(step_v, 1)
                    ch.after(nc.vector.bn_aggr(mv[:, u, 0:2], st[:, u]))
                    nc.vector.tensor_scalar(mv[:, u, 2:3], mv[:, u, 1:2], EPS, None, ALU.add).then_inc(var_ok, 1)
                    dve.wait_ge(rstd_ok, t + 1)
                    nc.vector.tensor_scalar(x[:, u], x[:, u], mv[:, u, 0:1], mv[:, u, 3:4], ALU.subtract, ALU.mult).then_inc(x_n, 1)
                    return ch

                with dve.Fori(0, NT // 2) as j:
                    b = j // 2
                    for u in range(2):
                        t = j * 2 + u
                        ti = (j % 2) * 2 + u
                        ch = norm(j, u)
                        dve.wait_ge(x_t, t + 1)
                        ca = modcol[:, bass.ds(b, 1), 1, :].rearrange("p a c -> p (a c)").unsqueeze(2).broadcast_to([P, DC, P])
                        sa = modcol[:, bass.ds(b, 1), 0, :].rearrange("p a c -> p (a c)").unsqueeze(2).broadcast_to([P, DC, P])
                        pxv = px[:, u].rearrange("p (c n) -> p c n", c=DC)
                        ch.after(nc.vector.tensor_tensor(hf[:, u], pxv, ca, ALU.mult))
                        nc.vector.tensor_tensor(hf[:, u], hf[:, u], sa, ALU.add).then_inc(h_full, 1)
                        dve.wait_ge(h_hi, t + 1)
                        nc.vector.tensor_tensor(hT[:, u, :, 1], hf[:, u], hT[:, u, :, 0].bitcast(F32), ALU.subtract).then_inc(h_lo, 1)
                        dve.wait_ge(c_hi, t + 1)
                        nc.vector.tensor_tensor(chl[:, u, 1], cf[:, u], chl[:, u, 0].bitcast(F32), ALU.subtract).then_inc(c_lo, 1)
                        dve.wait_ge(pev, t * 2 + 2)
                        cos = rope[:, bass.ds(ti, 1), 0:HALF].broadcast_to([P, H + 1, HALF])
                        nc.vector.tensor_tensor(rt[:, u, 2], qk[:, u, :, 0::2], cos, ALU.mult)
                        ch.after(nc.vector.tensor_tensor(rt[:, u, 3], qk[:, u, :, 1::2], cos, ALU.mult))
                        dve.wait_ge(rot_p, t + 1)
                        nc.vector.tensor_tensor(qr[:, u, :, 0:HALF], rt[:, u, 2], rt[:, u, 0], ALU.subtract)
                        nc.vector.tensor_tensor(qr[:, u, :, HALF:ROPE], rt[:, u, 3], rt[:, u, 1], ALU.add).then_inc(rot, 1)
                        dve.wait_ge(k_hi, t + 1)
                        nc.vector.tensor_tensor(ck[:, u, 1, 0], pk[:, 0:P], ck[:, u, 0, 0].bitcast(F32), ALU.subtract)
                        for r in (slice(0, ROPE), slice(ROPE, P)):
                            m = nc.vector.tensor_tensor(ck[r, u, 1, 1], pk[0:ROPE, P:2 * P],
                                                        ck[0:ROPE, u, 0, 1].bitcast(F32), ALU.subtract)
                        m.then_inc(k_lo, 1)
                        for g in range(4):
                            dve.wait_ge(q_hi, t * 4 + g + 1)
                            part = lambda r: qs[r, u, 4 * g:4 * g + 4].rearrange("p h n -> p (h n)")
                            nc.vector.scalar_tensor_tensor(out=part(slice(ROPE, P)), in0=pt[0:ROPE, g % 2], scalar=SCALE,
                                                           in1=part(slice(0, ROPE)).bitcast(F32),
                                                           op0=ALU.mult, op1=ALU.subtract).then_inc(q_lo, 1)
                        assert ch.n == 4

            @block.tensor
            def _(pe):
                pe.wait_ge(w_lo, DC + 1)
                with pe.Fori(0, NT // 2) as j:
                    for u in range(2):
                        t = j * 2 + u
                        pe.wait_ge(x_n, t + 1)
                        for c in range(DC):
                            m = nc.tensor.transpose(px[:, u, c * P:(c + 1) * P], x[:, u, c * P:(c + 1) * P], K.ident[:, :])
                        m.then_inc(x_t, 1)
                        pe.wait_ge(h_lo, t + 1)
                        hs = [(hT[:, u, c, 0], hT[:, u, c, 1]) for c in range(DC)]
                        split3(nc, pc[:, 0:NC], [(*hs[c], wc[:, c, 0], wc[:, c, 1]) for c in range(DC)]).then_inc(proj, 1)
                        for n in range(NQ // 512):
                            w = slice(n * 512, (n + 1) * 512)
                            m = split3(nc, pq[:, w], [(*hs[c], wpe[:, c, 0, w], wpe[:, c, 1, w]) for c in range(DC)])
                        m.then_inc(proj, 1)
                        pe.wait_ge(rot, t + 1)
                        nc.tensor.transpose(pk[:, 0:P], cf[:, u], K.ident[:, :])
                        nc.tensor.transpose(pk[0:ROPE, P:2 * P], qr[:, u, H], K.ident[:, :]).then_inc(kt, 1)
                        for g in range(4):
                            if g >= 2:
                                pe.wait_ge(q_lo, t * 4 + g - 1)
                                pe.sem_inc(step_e, 1)
                            for i in range(4):
                                m = nc.tensor.transpose(pt[0:ROPE, g % 2, i * P:(i + 1) * P], qr[:, u, 4 * g + i], K.ident[:, :])
                            m.then_inc(qt, 1)
                        pe.wait_ge(k_lo, t + 1)
                        pe.wait_ge(q_lo, t * 4 + 4)


def stage_attention(K, Mhl):
    nc = K.nc
    PAIRS = H // 2
    OFF = {0: 0, 3: 5 * P, 1: 6 * P, 2: 9 * P}
    ZERO = 4 * P
    NPT = 11 * P
    with ExitStack() as ctx:
        sb = lambda n, s, d: K.sb(n, s, d, ctx)
        hT = sb("a_hT", [P, 2, DC, 2, S], F32R)
        cT = sb("a_cT", [P, 2, 2, S], F32R)
        kpe = sb("a_kpe", [P, 2, 2, S], F32R)
        cv = sb("a_cv", [P, TB, 2, P], F32R)
        wqk = sb("a_wqk", [P, 2, 2, DC, P], F32R)
        qpe = sb("a_qpe", [P, 2, S], F32R)
        qT = sb("a_qT", [P, 2, S], F32R)
        pr = sb("a_pr", [P, TB, S], F32)
        pT = sb("a_pT", [P, 2, NPT], F32R)
        oT = sb("a_oT", [P, 2, 2, S], F32R)
        acc = sb("a_acc", [P, TB, D], F32)
        nmax = sb("a_nmax", [P, TB], F32)
        rsum = sb("a_rsum", [P, TB], F32)
        rinv = sb("a_rinv", [P, TB], F32)
        psS = K.ps("a_psS", [P, 3, 512], F32, ctx)
        psX = K.ps("a_psX", [P, 512], F32, ctx)
        psY = K.ps("a_psY", [P, 512], F32, ctx)
        psZ = K.ps("a_psZ", [P, 512], F32, ctx)
        psT = K.ps("a_psT", [P, 2, 512], F32, ctx)
        b_in = [K.sem("a_b_in0"), K.sem("a_b_in1")]
        c_in, landed = K.sem("a_c_in"), K.sem("a_landed")
        w_in = [K.sem("a_w_in0"), K.sem("a_w_in1")]
        q_in = [K.sem("a_q_in0"), K.sem("a_q_in1")]
        qp, q_hi, q_lo = K.sem("a_qp"), K.sem("a_q_hi"), K.sem("a_q_lo")
        sc, mx, ex, rc, nr = K.sem("a_sc"), K.sem("a_mx"), K.sem("a_ex"), K.sem("a_rc"), K.sem("a_nr")
        pt, p_hi, p_lo = K.sem("a_pt"), K.sem("a_p_hi"), K.sem("a_p_lo")
        pv, o_hi, o_lo = K.sem("a_pv"), K.sem("a_o_hi"), K.sem("a_o_lo")
        ot, ac, acc_out, zero = K.sem("a_ot"), K.sem("a_ac"), K.sem("a_acc_out"), K.sem("a_zero")
        score = [psS[:, 0, 0:2 * P], psS[:, 0, 2 * P:4 * P], psS[:, 1, 0:3 * P], psS[:, 2, :]]
        groups = [(psT[:, 0], slice(0, 4 * P), [(0, 0)]),
                  (psT[:, 1], slice(OFF[3], OFF[3] + 4 * P), [(3, 0), (1, P)]),
                  (psX[:, 0:2 * P], slice(OFF[2], OFF[2] + 2 * P), [(2, 0)])]

        with nc.Block() as block:

            @block.sync
            def _(sp):
                def load_w(g, u):
                    sp.dma_start(wqk[:, u].rearrange("p s c n -> p (s c n)").bitcast(F32),
                                 K.wqk_d[bass.ds(g % H, 1)].rearrange("a p s c n -> p (a s c n)")).then_inc(w_in[u], 16)

                def load_q(g, u):
                    sp.dma_start(qpe[:, u].bitcast(F32), K.qpe_d.rearrange("b h p n -> (b h) p n")[bass.ds(g, 1)]
                                 .rearrange("a p n -> p (a n)")).then_inc(q_in[u], 16)

                for u in range(2):
                    load_w(u, u)
                    load_q(u, u)
                with sp.Fori(0, B * PAIRS - 1) as n:
                    for u in range(2):
                        g = n * 2 + u
                        sp.wait_ge(qp, g + 1)
                        load_w(g + 2, u)
                        sp.wait_ge(sc, g * 4 + 4)
                        load_q(g + 2, u)

            @block.gpsimd
            def _(pool):
                def load(b):
                    s = b % 2
                    pool.dma_start(hT[:, s].rearrange("p c s n -> p (c s n)").bitcast(F32),
                                   K.hT_d[b].rearrange("p c s n -> p (c s n)")).then_inc(b_in[s], 16)
                    pool.dma_start(cT[:, s].rearrange("p s n -> p (s n)").bitcast(F32),
                                   K.cT_d[b].rearrange("p s n -> p (s n)")).then_inc(b_in[s], 16)
                    pool.dma_start(kpe[:, s].rearrange("p s n -> p (s n)").bitcast(F32),
                                   K.kpe_d[b].rearrange("p s n -> p (s n)")).then_inc(b_in[s], 16)

                def load_c(b):
                    pool.dma_start(cv[:, :, :, :].rearrange("p t s n -> p (t s n)").bitcast(F32),
                                   K.c_d[b].rearrange("p t s n -> p (t s n)")).then_inc(c_in, 16)

                load(0)
                load_c(0)
                load(1)
                for b in range(B):
                    if b:
                        pool.wait_ge(pv, H * b)
                        load_c(b)
                        if b + 1 < B:
                            pool.wait_ge(qp, H * b)
                            pool.wait_ge(sc, 4 * H * b)
                            load(b + 1)
                    pool.wait_ge(c_in, 16 * (b + 1))
                    pool.wait_ge(b_in[b % 2], 48 * (b // 2 + 1))
                    pool.sem_inc(landed, 1)

            @block.scalar
            def _(act):
                act.sem_inc(acc_out, 16)

                def exps(g):
                    for i in range(TB):
                        act.wait_ge(mx, g * 4 + max(i + 1, 2))
                        w = (i + 1) * P
                        nc.scalar.activation(pr[:, i, 0:w], score[i][:, 0:w], ACT.Exp, bias=nmax[:, i:i + 1],
                                             accum_out=rsum[:, i:i + 1]).then_inc(ex, 1)

                def q_high(g):
                    act.wait_ge(qp, g + 1)
                    nc.scalar.activation(qT[:, 0], psX[:, :], ACT.Copy, scale=SCALE).then_inc(q_hi, 1)

                def o_high(g, n, u):
                    act.wait_ge(pv, g + 1)
                    act.wait_ge(ot, n * 4 + 1)
                    nc.scalar.activation(oT[:, u, 0], psY[:, :], ACT.Copy).then_inc(o_hi, 1)

                def p_high(g):
                    for k, (src, dst, _) in enumerate(groups):
                        act.wait_ge(pt, g * 3 + k + 1)
                        nc.scalar.activation(pT[:, 0, dst], src, ACT.Copy).then_inc(p_hi, 1)

                def pair(b, i, first, last):
                    n = b * PAIRS + i
                    for u in range(2):
                        g = n * 2 + u
                        exps(g)
                        if not (last and u):
                            q_high(g + 1)
                        if not (first and not u):
                            o_high(g - 1, n - 1 if not u else n, 1 - u)
                        p_high(g)

                with act.Fori(0, B) as b:
                    q_high(b * H)
                    pair(b, 0, True, False)
                    with act.Fori(1, PAIRS - 1) as i:
                        pair(b, i, False, False)
                    pair(b, PAIRS - 1, False, True)
                    o_high(b * H + H - 1, b * PAIRS + PAIRS - 1, 1)
                    act.wait_ge(ac, b * (PAIRS * TB) + PAIRS * TB + 1)
                    act.dma_start(K.attn_d[bass.ds(b * TB, TB)].rearrange("t p n -> p t n"),
                                  acc[:, :, :]).then_inc(acc_out, 16)
                act.wait_ge(acc_out, 16 * B + 16)

            @block.vector
            def _(dve):
                for credit in (o_lo, p_lo, ac):
                    dve.sem_inc(credit, 1)
                for s in range(2):
                    nc.vector.memset(pT[:, s, ZERO:ZERO + P].bitcast(U32), 0).then_inc(zero, 1)

                def softmax(g):
                    for i in range(TB):
                        dve.wait_ge(sc, g * 4 + max(i + 1, 2))
                        nc.vector.tensor_reduce(nmax[:, i:i + 1], score[i][:, 0:(i + 1) * P], AX.X, ALU.max,
                                                negate=True).then_inc(mx, 1)
                    dve.wait_ge(ex, g * 4 + 4)
                    nc.vector.reciprocal(rinv[:, :], rsum[:, :]).then_inc(rc, 1)
                    dve.wait_ge(rc, g + 1)
                    for i in range(TB):
                        w = (i + 1) * P
                        nc.vector.tensor_scalar(pr[:, i, 0:w], pr[:, i, 0:w], rinv[:, i:i + 1], None, ALU.mult).then_inc(nr, 1)

                def q_low(g):
                    dve.wait_ge(q_hi, g + 1)
                    nc.vector.scalar_tensor_tensor(out=qT[:, 1], in0=psX[:, :], scalar=SCALE, in1=qT[:, 0].bitcast(F32),
                                                   op0=ALU.mult, op1=ALU.subtract).then_inc(q_lo, 1)

                def o_low(g, u):
                    dve.wait_ge(o_hi, g + 1)
                    nc.vector.tensor_tensor(oT[:, u, 1], psY[:, :], oT[:, u, 0].bitcast(F32), ALU.subtract).then_inc(o_lo, 1)

                def p_low(g):
                    for k, (src, dst, _) in enumerate(groups):
                        dve.wait_ge(p_hi, g * 3 + k + 1)
                        nc.vector.tensor_tensor(pT[:, 1, dst], src, pT[:, 0, dst].bitcast(F32), ALU.subtract).then_inc(p_lo, 1)

                def add_out(b, n, t, first):
                    dve.wait_ge(ot, n * 4 + t + 2)
                    part = acc[:, t]
                    if first:
                        nc.vector.tensor_copy(part, psZ[:, :]).then_inc(ac, 1)
                    else:
                        dve.wait_ge(ac, n * 4 + t - 2)
                        nc.vector.tensor_tensor(part, psZ[:, :], part, ALU.add).then_inc(ac, 1)

                def pair(b, i, first, last, second=False):
                    n = b * PAIRS + i
                    for u in range(2):
                        g = n * 2 + u
                        softmax(g)
                        if u and not first:
                            add_out(b, n - 1, 1, second)
                        if not (last and u):
                            q_low(g + 1)
                        if u and not first:
                            add_out(b, n - 1, 2, second)
                            add_out(b, n - 1, 3, second)
                        if not (first and not u):
                            o_low(g - 1, 1 - u)
                        p_low(g)
                        if not u and not first:
                            add_out(b, n - 1, 0, second)

                with dve.Fori(0, B) as b:
                    q_low(b * H)
                    pair(b, 0, True, False)
                    dve.wait_ge(acc_out, b * 16 + 16)
                    pair(b, 1, False, False, True)
                    with dve.Fori(2, PAIRS - 1) as i:
                        pair(b, i, False, False)
                    pair(b, PAIRS - 1, False, True)
                    o_low(b * H + H - 1, 1)
                    for t in range(TB):
                        add_out(b, b * PAIRS + PAIRS - 1, t, False)

            @block.tensor
            def _(pe):
                def qproj(b, g, u, transposed):
                    pe.wait_ge(w_in[u], (g // 2) * 16 + 16)
                    pe.wait_ge(p_lo, transposed * 3 + 1)
                    h_ = lambda c, s: hT[:, bass.ds(b % 2, 1), c, s].rearrange("p a n -> p (a n)")
                    split3(nc, psX[:, :], [(wqk[:, u, 0, c], wqk[:, u, 1, c], h_(c, 0), h_(c, 1))
                                           for c in range(DC)]).then_inc(qp, 1)

                def scores(b, g, u):
                    pe.wait_ge(q_lo, g + 1)
                    pe.wait_ge(q_in[u], (g // 2) * 16 + 16)
                    for i in range(TB):
                        w = max(i + 1, 2) * P
                        q = slice(i * P, (i + 1) * P)
                        out = score[i][:, 0:w]
                        k_ = lambda src, s: src[:, bass.ds(b % 2, 1), s, 0:w].rearrange("p a n -> p (a n)")
                        nc.tensor.matmul(out, qT[:, 0, q], k_(cT, 0), start=True, stop=False)
                        nc.tensor.matmul(out, qT[:, 0, q], k_(cT, 1), start=False, stop=False)
                        nc.tensor.matmul(out, qT[:, 1, q], k_(cT, 0), start=False, stop=False)
                        nc.tensor.matmul(out, qpe[:, u, q], k_(kpe, 0), start=False, stop=False)
                        nc.tensor.matmul(out, qpe[:, u, q], k_(kpe, 1), start=False, stop=False)
                        nc.tensor.matmul(out[:, q], K.identb[:, :], K.maskb[:, :], start=False, stop=True).then_inc(sc, 1)

                def values(g):
                    pe.wait_ge(p_lo, g * 3 + 4)
                    pe.wait_ge(o_lo, g + 1)
                    n = 0
                    for j in range(TB):
                        q0 = min(j, 2) * P
                        o = OFF[j] - (j * P - q0)
                        w = S - q0
                        for cs, ps in ((0, 0), (0, 1), (1, 0)):
                            m = nc.tensor.matmul(psY[:, q0:S], cv[:, j, cs], pT[:, ps, o:o + w], start=n == 0, stop=n == 11)
                            n += 1
                    m.then_inc(pv, 1)

                def transposes(g):
                    pe.wait_ge(nr, g * 4 + 4)
                    for k, (dst, _, parts) in enumerate(groups):
                        for j, o in parts:
                            for i in range(j, TB):
                                m = nc.tensor.transpose(dst[:, o + (i - j) * P:o + (i - j + 1) * P],
                                                        pr[:, i, j * P:(j + 1) * P], K.ident[:, :])
                        m.then_inc(pt, 1)

                def output(n, i, t):
                    pe.wait_ge(o_lo, n * 2 + 3)
                    pe.wait_ge(ac, n * 4 + t + 1)
                    q = slice(t * P, (t + 1) * P)
                    M_ = lambda u, s: Mhl[:, bass.ds(i * 2 + u, 1), s].rearrange("p a n -> p (a n)")
                    split3(nc, psZ[:, :], [(oT[:, u, 0, q], oT[:, u, 1, q], M_(u, 0), M_(u, 1))
                                           for u in range(2)]).then_inc(ot, 1)

                def pair(b, i, first, last):
                    n = b * PAIRS + i
                    for u in range(2):
                        g = n * 2 + u
                        scores(b, g, u)
                        if u and not first:
                            output(n - 1, i - 1, 1)
                        if not (last and u):
                            qproj(b, g + 1, 1 - u, g)
                        if u and not first:
                            output(n - 1, i - 1, 2)
                        if not (first and not u):
                            values(g - 1)
                        if u and not first:
                            output(n - 1, i - 1, 3)
                        if not (last and u):
                            pe.wait_ge(q_lo, g + 2)
                        transposes(g)
                        if not u and not first:
                            output(n - 1, i - 1, 0)

                pe.wait_ge(zero, 2)
                pe.sem_inc(ot, 1)
                with pe.Fori(0, B) as b:
                    pe.wait_ge(landed, b + 1)
                    qproj(b, b * H, 0, b * H)
                    pair(b, 0, True, False)
                    with pe.Fori(1, PAIRS - 1) as i:
                        pair(b, i, False, False)
                    pair(b, PAIRS - 1, False, True)
                    values(b * H + H - 1)
                    for t in range(TB):
                        output(b * PAIRS + PAIRS - 1, PAIRS - 1, t)


def stage_shared(K, M):
    nc = K.nc
    with ExitStack() as ctx:
        sb = lambda n, s, d: K.sb(n, s, d, ctx)
        st1 = sb("s_st1", [P, DC, 2, F], F32)
        st2 = sb("s_st2", [P, FC, D], F32)
        w1 = sb("s_w1", [P, SH, DC, 2, 2 * F], F32R)
        w2 = sb("s_w2", [P, SH, FC, 2, D], F32R)
        b1 = sb("s_b1", [P, SH, 2 * F], F32)
        b2 = sb("s_b2", [P, SH, D], F32)
        wa = sb("s_wa", [P, DC, E], F32)
        half = sb("s_half", [P, 1], F32)
        x = sb("s_x", [P, 2, D], F32)
        at = sb("s_at", [P, 2, D], F32)
        x1 = sb("s_x1", [P, 2, D], F32)
        h2 = sb("s_h2", [P, 2, D], F32)
        st = sb("s_st", [P, 2, 6], F32)
        mv = sb("s_mv", [P, 2, 4], F32)
        hf = sb("s_hf", [P, 2, D], F32)
        hT = sb("s_hT", [P, 2, 2, D], F32R)
        z = sb("s_z", [P, 2, 2 * F], F32)
        y = sb("s_y", [P, 2, F], F32)
        yT = sb("s_yT", [P, 2, 2, F], F32R)
        so = sb("s_so", [P, 2, D], F32)
        px = K.ps("s_px", [P, D], F32, ctx)
        pg = K.ps("s_pg", [P, 2, 2 * F], F32, ctx)
        py = K.ps("s_py", [P, 2, 512], F32, ctx)
        po = K.ps("s_po", [P, 2, D], F32, ctx)
        pl = K.ps("s_pl", [P, 512], F32, ctx)
        w_in, w_hi, w_lo, c_in = K.sem("s_w_in"), K.sem("s_w_hi"), K.sem("s_w_lo"), K.sem("s_c_in")
        x_in = [K.sem("s_x_in0"), K.sem("s_x_in1")]
        h_out = [K.sem("s_h_out0"), K.sem("s_h_out1")]
        step_v, step_p = K.sem("s_step_v"), K.sem("s_step_p")
        dch, pch, b2_ok = K.sem("s_dch"), K.sem("s_pch"), K.sem("s_b2_ok")
        var_ok, rstd, xn, x_used = K.sem("s_var_ok"), K.sem("s_rstd"), K.sem("s_xn"), K.sem("s_x_used")
        h2_ok, tr, h_hi, h_lo = K.sem("s_h2_ok"), K.sem("s_tr"), K.sem("s_h_hi"), K.sem("s_h_lo")
        lg, lg_ok = K.sem("s_lg"), K.sem("s_lg_ok")
        gu, z_ok, ge, y_ok = K.sem("s_gu"), K.sem("s_z_ok"), K.sem("s_ge"), K.sem("s_y_ok")
        yt, y_hi, y_lo, oo, so_ok, base_ok = (K.sem("s_yt"), K.sem("s_y_hi"), K.sem("s_y_lo"), K.sem("s_oo"),
                                              K.sem("s_so_ok"), K.sem("s_base_ok"))

        with nc.Block() as block:

            @block.sync
            def _(sp):
                for b in range(B):
                    sp.dma_start(M.rows[:, b].rearrange("p v n -> p (v n)"),
                                 K.mod_d[b:b + 1, 2 * D:6 * D].broadcast_to([P, 4 * D])).then_inc(c_in, 16)
                sp.dma_start(wa[:, :, :], K.ins["L0_ffn_wa"].rearrange("(c p) e -> p c e", p=P)).then_inc(c_in, 16)
                for e in range(SH):
                    for n, bias in enumerate((K.ins["L0_ffn_sgb"], K.ins["L0_ffn_sb1"])):
                        sp.dma_start(b1[:, e, n * F:(n + 1) * F], bias[e:e + 1, :].broadcast_to([P, F])).then_inc(c_in, 16)
                    sp.dma_start(b2[:, e], K.ins["L0_ffn_sb2"][e:e + 1, :].broadcast_to([P, D])).then_inc(c_in, 16)
                xv = K.ins["L0_attn_x"].rearrange("b (t p) n -> (b t) p n", p=P)

                def load(t, u):
                    sp.dma_start(x[:, u], xv[bass.ds(t, 1)].rearrange("a p n -> p (a n)")).then_inc(x_in[u], 16)
                    sp.dma_start(at[:, u], K.attn_d[bass.ds(t, 1)].rearrange("a p n -> p (a n)")).then_inc(x_in[u], 16)

                load(0, 0)
                load(1, 1)
                for e in range(SH):
                    if e:
                        sp.wait_ge(w_lo, 2 * e)
                    sp.dma_start(st1[:, :, 0], K.ins["L0_ffn_sg"][e].rearrange("(c p) f -> p c f", p=P)).then_inc(w_in, 16)
                    sp.dma_start(st1[:, :, 1], K.ins["L0_ffn_sw1"][e].rearrange("(c p) f -> p c f", p=P)).then_inc(w_in, 16)
                    sp.dma_start(st2[:, :, :], K.ins["L0_ffn_sw2"][e].rearrange("(c p) n -> p c n", p=P)).then_inc(w_in, 16)

                def tiles(j, more):
                    for u in range(2):
                        t = j * 2 + u
                        if more:
                            sp.wait_ge(x_used, t + 1)
                            load(t + 2, u)
                        sp.wait_ge(h2_ok, t + 1)
                        sp.dma_start(K.h2_d[bass.ds(t * P, P), :], h2[:, u]).then_inc(h_out[u], 16)

                with sp.Fori(0, NT // 2 - 1) as j:
                    tiles(j, True)
                tiles(NT // 2 - 1, False)
                for u in range(2):
                    sp.wait_ge(h_out[u], 16 * (NT // 2))

            @block.gpsimd
            def _(pool):
                nc.gpsimd.memset(half[:, :], -0.5).then_inc(pch, 1)
                pool.wait_ge(pch, 1)
                pool.wait_ge(c_in, 16 * (B + 1 + 3 * SH))
                nc.gpsimd.tensor_tensor(b2[:, 0], b2[:, 0], b2[:, 1], ALU.add).then_inc(b2_ok, 1)

                def scale(b, t, u):
                    pool.wait_ge(var_ok, t + 1)
                    nc.gpsimd.tensor_tensor(mv[:, u, 3:4], mv[:, u, 2:3], half[:, :], ALU.pow).then_inc(rstd, 1)
                    pool.wait_ge(xn, t + 1)
                    pool.sem_inc(step_p, 1)
                    row = lambda v: M.rows[:, bass.ds(b, 1), v].rearrange("p a n -> p (a n)")
                    nc.gpsimd.tensor_tensor(h2[:, u], h2[:, u], row(2), ALU.mult).then_inc(pch, 1)
                    pool.wait_ge(pch, t + 2)
                    pool.sem_inc(step_p, 1)
                    nc.gpsimd.tensor_tensor(h2[:, u], h2[:, u], row(1), ALU.add).then_inc(h2_ok, 1)

                def base(b, t, u):
                    row = M.rows[:, bass.ds(b, 1), 3].rearrange("p a n -> p (a n)")
                    bt = M.base[:, bass.ds(t, 1)].rearrange("p a n -> p (a n)")
                    pool.wait_ge(so_ok, t + 1)
                    pool.sem_inc(step_p, 1)
                    nc.gpsimd.tensor_tensor(so[:, u], so[:, u], h2[:, u], ALU.add).then_inc(base_ok, 1)
                    pool.wait_ge(base_ok, t * 3 + 1)
                    pool.sem_inc(step_p, 1)
                    nc.gpsimd.tensor_tensor(so[:, u], so[:, u], row, ALU.mult).then_inc(base_ok, 1)
                    pool.wait_ge(base_ok, t * 3 + 2)
                    pool.sem_inc(step_p, 1)
                    nc.gpsimd.tensor_tensor(bt, so[:, u], x1[:, u], ALU.add).then_inc(base_ok, 1)

                def tiles(j, more):
                    for u in range(2):
                        t = j * 2 + u
                        if more or not u:
                            scale((t + 1) // TB, t + 1, 1 - u)
                        base(j // 2, t, u)

                scale(0, 0, 0)
                with pool.Fori(0, NT // 2 - 1) as j:
                    tiles(j, True)
                tiles(NT // 2 - 1, False)

            @block.scalar
            def _(act):
                for e in range(SH):
                    act.wait_ge(w_in, 48 * (e + 1))
                    nc.scalar.activation(w1[:, e, :, 0].rearrange("p c (a f) -> p c a f", a=2), st1[:, :, :, :], ACT.Copy).then_inc(w_hi, 1)
                    nc.scalar.activation(w2[:, e, :, 0], st2[:, :, :], ACT.Copy).then_inc(w_hi, 1)

                def h_high(t, u):
                    act.wait_ge(tr, t + 1)
                    nc.scalar.activation(hf[:, u], px[:, :], ACT.Copy)
                    nc.scalar.activation(hT[:, u, 0], px[:, :], ACT.Copy).then_inc(h_hi, 1)

                def logits(t):
                    act.wait_ge(lg, t + 1)
                    nc.scalar.activation(M.aff[:, bass.ds(t, 1)].rearrange("p a e -> p (a e)"), pl[:, 0:E], ACT.Copy).then_inc(lg_ok, 1)

                def gelu(t, e):
                    act.wait_ge(z_ok, t * 2 + e + 1)
                    nc.scalar.activation(y[:, e], z[:, e, 0:F], ACT.Gelu).then_inc(ge, 1)

                def y_high(t, e):
                    act.wait_ge(yt, t * 2 + e + 1)
                    nc.scalar.activation(yT[:, e, 0], py[:, e, 0:F], ACT.Copy).then_inc(y_hi, 1)

                def tiles(j, more):
                    for u in range(2):
                        t = j * 2 + u
                        gelu(t, 0)
                        gelu(t, 1)
                        y_high(t, 0)
                        if more or not u:
                            h_high(t + 1, 1 - u)
                        y_high(t, 1)
                        if more or not u:
                            logits(t + 1)

                h_high(0, 0)
                logits(0)
                with act.Fori(0, NT // 2 - 1) as j:
                    tiles(j, True)
                tiles(NT // 2 - 1, False)

            @block.vector
            def _(dve):
                for e in range(SH):
                    dve.wait_ge(w_hi, 2 * e + 1)
                    nc.vector.tensor_tensor(w1[:, e, :, 1].rearrange("p c (a f) -> p c a f", a=2), st1[:, :, :, :],
                                            w1[:, e, :, 0].rearrange("p c (a f) -> p c a f", a=2).bitcast(F32),
                                            ALU.subtract).then_inc(w_lo, 1)
                    dve.wait_ge(w_hi, 2 * e + 2)
                    nc.vector.tensor_tensor(w2[:, e, :, 1], st2[:, :, :], w2[:, e, :, 0].bitcast(F32), ALU.subtract).then_inc(w_lo, 1)

                def norm(b, t, u, slot_loads, former):
                    ch = Chain(dve, dch, t * 4)
                    dve.wait_ge(x_in[u], slot_loads * 32)
                    row = M.rows[:, bass.ds(b, 1), 0].rearrange("p a n -> p (a n)")
                    ch.after(nc.vector.tensor_tensor(at[:, u], at[:, u], row, ALU.mult))
                    if former is not None:
                        dve.wait_ge(base_ok, former * 3 + 3)
                    nc.vector.tensor_tensor(x1[:, u], x[:, u], at[:, u], ALU.add).then_inc(x_used, 1)
                    dve.wait_ge(x_used, t + 1)
                    nc.vector.bn_stats(st[:, u], x1[:, u]).then_inc(ch.sem, 1)
                    ch.wait()
                    dve.sem_inc(step_v, 1)
                    ch.after(nc.vector.bn_aggr(mv[:, u, 0:2], st[:, u]))
                    nc.vector.tensor_scalar(mv[:, u, 2:3], mv[:, u, 1:2], EPS, None, ALU.add).then_inc(var_ok, 1)
                    dve.wait_ge(rstd, t + 1)
                    dve.wait_ge(h_out[u], (slot_loads - 1) * 16)
                    nc.vector.tensor_scalar(h2[:, u], x1[:, u], mv[:, u, 0:1], mv[:, u, 3:4], ALU.subtract, ALU.mult).then_inc(xn, 1)
                    dve.wait_ge(xn, t + 1)
                    ch.after(nc.vector.tensor_copy(mv[:, u, 2:3], mv[:, u, 1:2]))
                    assert ch.n == 4

                def h_low(t, u):
                    dve.wait_ge(h_hi, t + 1)
                    nc.vector.tensor_tensor(hT[:, u, 1], px[:, :], hT[:, u, 0].bitcast(F32), ALU.subtract).then_inc(h_lo, 1)

                def bias(t, e):
                    dve.wait_ge(gu, t * 2 + e + 1)
                    nc.vector.tensor_tensor(z[:, e], pg[:, e], b1[:, e], ALU.add).then_inc(z_ok, 1)

                def gate(t, e):
                    dve.wait_ge(ge, t * 2 + e + 1)
                    nc.vector.tensor_tensor(y[:, e], y[:, e], z[:, e, F:2 * F], ALU.mult).then_inc(y_ok, 1)

                def y_low(t, e):
                    dve.wait_ge(y_hi, t * 2 + e + 1)
                    nc.vector.tensor_tensor(yT[:, e, 1], py[:, e, 0:F], yT[:, e, 0].bitcast(F32), ALU.subtract).then_inc(y_lo, 1)

                def tiles(j, more, fresh=False):
                    for u in range(2):
                        t = j * 2 + u
                        if more or not u:
                            norm((t + 1) // TB, t + 1, 1 - u, j + 1 + u, None if fresh and not u else t - 1)
                        bias(t, 0)
                        gate(t, 0)
                        bias(t, 1)
                        gate(t, 1)
                        y_low(t, 0)
                        if more or not u:
                            h_low(t + 1, 1 - u)
                        y_low(t, 1)
                        dve.wait_ge(oo, t + 1)
                        nc.vector.tensor_tensor(so[:, u], po[:, u], b2[:, 0], ALU.add).then_inc(so_ok, 1)

                dve.wait_ge(c_in, 16 * (B + 1 + 3 * SH))
                dve.wait_ge(b2_ok, 1)
                norm(0, 0, 0, 1, None)
                h_low(0, 0)
                tiles(0, True, True)
                with dve.Fori(1, NT // 2 - 1) as j:
                    tiles(j, True)
                tiles(NT // 2 - 1, False)

            @block.tensor
            def _(pe):
                def transposes(t, u):
                    pe.wait_ge(h2_ok, t + 1)
                    for c in range(DC):
                        m = nc.tensor.transpose(px[:, c * P:(c + 1) * P], h2[:, u, c * P:(c + 1) * P], K.ident[:, :])
                    m.then_inc(tr, 1)

                def router(t, u):
                    pe.wait_ge(h_hi, t + 1)
                    pe.wait_ge(lg_ok, t)
                    for c in range(DC):
                        m = nc.tensor.matmul(pl[:, 0:E], hf[:, u, c * P:(c + 1) * P], wa[:, c], start=c == 0, stop=c == DC - 1)
                    m.then_inc(lg, 1)

                def first(t, u, e):
                    pe.wait_ge(h_lo, t + 1)
                    c_ = lambda c: slice(c * P, (c + 1) * P)
                    split3(nc, pg[:, e], [(hT[:, u, 0, c_(c)], hT[:, u, 1, c_(c)], w1[:, e, c, 0], w1[:, e, c, 1])
                                          for c in range(DC)]).then_inc(gu, 1)

                def y_trans(t, e):
                    pe.wait_ge(y_ok, t * 2 + e + 1)
                    for c in range(FC):
                        m = nc.tensor.transpose(py[:, e, c * P:(c + 1) * P], y[:, e, c * P:(c + 1) * P], K.ident[:, :])
                    m.then_inc(yt, 1)

                def second(t, u, e):
                    pe.wait_ge(y_lo, t * 2 + e + 1)
                    n = 0
                    for c in range(FC):
                        for s, w in ((0, 0), (0, 1), (1, 0)):
                            m = nc.tensor.matmul(po[:, u], yT[:, e, s, c * P:(c + 1) * P], w2[:, e, c, w],
                                                 start=e == 0 and n == 0, stop=e == SH - 1 and n == 3 * FC - 1)
                            n += 1
                    if e == SH - 1:
                        m.then_inc(oo, 1)

                def tiles(j, more):
                    for u in range(2):
                        t = j * 2 + u
                        first(t, u, 0)
                        first(t, u, 1)
                        y_trans(t, 0)
                        if more or not u:
                            transposes(t + 1, 1 - u)
                        second(t, u, 0)
                        y_trans(t, 1)
                        if more or not u:
                            router(t + 1, 1 - u)
                        second(t, u, 1)

                pe.wait_ge(c_in, 16 * (B + 1 + 3 * SH))
                pe.wait_ge(w_lo, 2 * SH)
                transposes(0, 0)
                router(0, 0)
                with pe.Fori(0, NT // 2 - 1) as j:
                    tiles(j, True)
                tiles(NT // 2 - 1, False)


def stage_route(K, M):
    nc = K.nc
    NS = E + E * E + NBLK
    with ExitStack() as ctx:
        sb = lambda n, s, d: K.sb(n, s, d, ctx)
        small = sb("r_small", [P, NS], F32)
        tok = sb("r_tok", [P, NT], I32)
        trif = sb("r_trif", [P, P], F32)
        tri = sb("r_tri", [P, P], BF16)
        ones = sb("r_ones", [P, P], BF16)
        zeros = sb("r_zeros", [P, NBLK], I32)
        wide = lambda n: sb(n, [P, NT, E], F32)
        af, oh1, oh2, t1, rank = wide("r_af"), wide("r_oh1"), wide("r_oh2"), wide("r_t1"), wide("r_rank")
        mb = sb("r_mb", [P, NT, E], BF16)
        m1, m2, mt = sb("r_m1", [P, NT], F32), sb("r_m2", [P, NT], F32), sb("r_mt", [P, NT], F32)
        cnt, cnti = sb("r_cnt", [P, E], F32), sb("r_cnti", [P, 2, E], I32)
        nb, first, base = sb("r_nb", [P, E], F32), sb("r_first", [P, E], F32), sb("r_base", [P, E], F32)
        tt = sb("r_tt", [P, E, E], F32)
        cmp = sb("r_cmp", [P, NBLK, E], F32)
        bef = sb("r_bef", [P, NBLK], F32)
        pr = K.ps("r_pr", [P, NT * E], F32, ctx)
        pn = K.ps("r_pn", [P, 512], F32, ctx)
        c_in, z_out, sc_out = K.sem("r_c_in"), K.sem("r_z_out"), K.sem("r_sc_out")
        dch, sig, mb_ok, ranks, zero = K.sem("r_dch"), K.sem("r_sig"), K.sem("r_mb_ok"), K.sem("r_ranks"), K.sem("r_zero")
        pos_ok = K.sem("r_pos_ok")
        rev = small[:, 0:E]
        before = small[:, E:E + E * E].rearrange("p (e f) -> p e f", f=E)
        blk = small[:, E + E * E:NS]

        with nc.Block() as block:

            @block.sync
            def _(sp):
                sp.dma_start(small[:, :], K.ins["c_small"].broadcast_to([P, NS])).then_inc(c_in, 16)
                sp.dma_start(tok[:, :], K.ins["c_tok"]).then_inc(c_in, 16)
                sp.dma_start(trif[:, :], K.ins["c_const"][2]).then_inc(c_in, 16)
                sp.wait_ge(zero, 1)
                sp.dma_start(K.idx_d.rearrange("(p k) o -> p (k o)", p=P), zeros[:, :]).then_inc(z_out, 16)

            @block.scalar
            def _(act):
                nc.scalar.activation(af[:, :, :], M.aff[:, :, :], ACT.Sigmoid).then_inc(sig, 1)

            @block.gpsimd
            def _(pool):
                nc.gpsimd.memset(zeros[:, :], 0).then_inc(zero, 1)
                nc.gpsimd.memset(ones[:, :], 1.0).then_inc(zero, 1)
                pool.wait_ge(c_in, 48)
                pool.wait_ge(z_out, 16)
                pool.wait_ge(pos_ok, 1)
                for t in range(NT):
                    for k in range(TOP):
                        pool.indirect_dma_start(
                            out=K.idx_d, out_offset=bass.IndirectOffsetOnAxis(ap=M.pos[:, k, t:t + 1], axis=0),
                            in_=tok[:, t:t + 1], in_offset=None).then_inc(sc_out, 16)
                pool.wait_ge(sc_out, 16 * NT * TOP)

            @block.vector
            def _(dve):
                ch = Chain(dve, dch)
                dve.wait_ge(c_in, 48)
                dve.wait_ge(sig, 1)
                over = lambda a: a.unsqueeze(2).broadcast_to([P, NT, E])
                under = lambda a: a.unsqueeze(1).broadcast_to([P, NT, E])
                tt_, v = nc.vector.tensor_tensor, nc.vector
                ch.after(v.tensor_copy(tri[:, :], trif[:, :]))
                for m, oh in ((m1, oh1), (m2, oh2)):
                    ch.after(v.tensor_reduce(m[:, :], af[:, :, :], AX.X, ALU.max))
                    ch.after(tt_(t1[:, :, :], af[:, :, :], over(m[:, :]), ALU.is_equal))
                    ch.after(tt_(t1[:, :, :], t1[:, :, :], under(rev), ALU.mult))
                    ch.after(v.tensor_reduce(mt[:, :], t1[:, :, :], AX.X, ALU.max))
                    ch.after(tt_(oh[:, :, :], t1[:, :, :], over(mt[:, :]), ALU.is_equal))
                    if oh is oh1:
                        ch.after(v.scalar_tensor_tensor(out=af[:, :, :].rearrange("p t e -> p (t e)"),
                                                        in0=oh[:, :, :].rearrange("p t e -> p (t e)"), scalar=-2.0,
                                                        in1=af[:, :, :].rearrange("p t e -> p (t e)"),
                                                        op0=ALU.mult, op1=ALU.add))
                tt_(mb[:, :, :], oh1[:, :, :], oh2[:, :, :], ALU.add).then_inc(mb_ok, 1)
                ch.after(tt_(mt[:, :], m1[:, :], m2[:, :], ALU.add))
                ch.after(v.reciprocal(mt[:, :], mt[:, :]))
                tt_(M.wt[:, 0], m1[:, :], mt[:, :], ALU.mult)
                tt_(M.wt[:, 1], m2[:, :], mt[:, :], ALU.mult)
                dve.wait_ge(ranks, 1)
                ch.after(v.tensor_scalar(cnti[:, 0], pn[:, 0:E], float(P - 1), None, ALU.add))
                ch.after(v.tensor_scalar(cnti[:, 1], cnti[:, 0], P.bit_length() - 1, None, ALU.logical_shift_right))
                ch.after(v.tensor_copy(nb[:, :], cnti[:, 1]))
                ch.after(tt_(tt[:, :, :], before, nb[:, :].unsqueeze(1).broadcast_to([P, E, E]), ALU.mult))
                ch.after(v.tensor_reduce(first[:, :], tt[:, :, :], AX.X, ALU.add))
                ch.after(v.tensor_scalar(base[:, :], first[:, :], float(P), None, ALU.mult))
                ch.after(tt_(rank[:, :, :], pr[:, :].rearrange("p (t e) -> p t e", e=E), under(base[:, :]), ALU.add))
                for k, oh in enumerate((oh1, oh2)):
                    ch.after(tt_(t1[:, :, :], rank[:, :, :], oh[:, :, :], ALU.mult))
                    ch.after(v.tensor_reduce(mt[:, :], t1[:, :, :], AX.X, ALU.add))
                    ch.after(v.tensor_copy(M.pos[:, k], mt[:, :]))
                ch.after(tt_(first[:, :], first[:, :], nb[:, :], ALU.add))
                v.tensor_scalar(m1[:, :], m1[:, :], 1.0, None, ALU.mult).then_inc(pos_ok, 1)
                ch.after(tt_(cmp[:, :, :], first[:, :].unsqueeze(1).broadcast_to([P, NBLK, E]),
                             blk.unsqueeze(2).broadcast_to([P, NBLK, E]), ALU.is_le))
                ch.after(v.tensor_reduce(bef[:, :], cmp[:, :, :], AX.X, ALU.add))
                ch.after(v.tensor_scalar(M.be[:, :], bef[:, :], float(E - 1), None, ALU.min))

            @block.tensor
            def _(pe):
                pe.wait_ge(mb_ok, 1)
                pe.wait_ge(zero, 2)
                nc.tensor.matmul(pr[:, :], tri[:, :], mb[:, :, :].rearrange("p t e -> p (t e)"), start=True, stop=False)
                for t in range(NT - 1):
                    nc.tensor.matmul(pr[:, (t + 1) * E:].rearrange("p (t e) -> p t e", e=E), ones[:, :],
                                     mb[:, t:t + 1].broadcast_to([P, NT - 1 - t, E]), start=False, stop=t == NT - 2)
                for t in range(NT):
                    m = nc.tensor.matmul(pn[:, 0:E], ones[:, :], mb[:, t], start=t == 0, stop=t == NT - 1)
                m.then_inc(ranks, 1)


def stage_routed(K, M):
    nc = K.nc
    LB = NBLK // 2
    PW = 2
    with ExitStack() as ctx:
        sb = lambda n, s, d: K.sb(n, s, d, ctx)
        st1 = sb("e_st1", [P, 2, DC, 2, F], F32)
        st2 = sb("e_st2", [P, 2, FC, D], F32)
        w1 = sb("e_w1", [P, 2, DC, 2, 2 * F], F32R)
        w2 = sb("e_w2", [P, 2, FC, 2, D], F32R)
        b1 = sb("e_b1", [P, 2, 2 * F], F32)
        b2 = sb("e_b2", [P, 2, D], F32)
        idx = sb("e_idx", [P, 2, 1], I32)
        xg = sb("e_xg", [P, 2, D], F32)
        xT = sb("e_xT", [P, 2, 2, D], F32R)
        z = sb("e_z", [P, 2, 2 * F], F32)
        y = sb("e_y", [P, 2, F], F32)
        yT = sb("e_yT", [P, 2, 2, F], F32R)
        yo = sb("e_yo", [P, 2, D], F32)
        px = K.ps("e_px", [P, D], F32, ctx)
        pg = K.ps("e_pg", [P, 2, 2 * F], F32, ctx)
        py = K.ps("e_py", [P, 2, 512], F32, ctx)
        po = K.ps("e_po", [P, 2, D], F32, ctx)
        w_in = [K.sem("e_w_in0"), K.sem("e_w_in1")]
        b_in = [K.sem("e_b_in0"), K.sem("e_b_in1")]
        i_in = [K.sem("e_i_in0"), K.sem("e_i_in1")]
        x_in = [K.sem("e_x_in0"), K.sem("e_x_in1")]
        y_out = [K.sem("e_y_out0"), K.sem("e_y_out1")]
        step_p = K.sem("e_step_p")
        w_hi, w_lo, w_lop = K.sem("e_w_hi"), K.sem("e_w_lo"), K.sem("e_w_lop")
        tr, x_hi, x_lo = K.sem("e_tr"), K.sem("e_x_hi"), K.sem("e_x_lo")
        gu, z_ok, ge, y_ok = K.sem("e_gu"), K.sem("e_z_ok"), K.sem("e_ge"), K.sem("e_y_ok")
        yt, y_hi, y_lo, oo, yo_ok = K.sem("e_yt"), K.sem("e_y_hi"), K.sem("e_y_lo"), K.sem("e_oo"), K.sem("e_yo_ok")

        def run(eng, head, body, tail):
            head()
            body(0, True, False)
            with eng.Fori(1, LB - 1) as j:
                body(j, False, False)
            body(LB - 1, False, True)
            tail()

        with nc.Block() as block:

            @block.sync
            def _(sp):
                rg = K.ins["L0_ffn_rg"].rearrange("e (c p) f -> e p c f", p=P)
                rw1 = K.ins["L0_ffn_rw1"].rearrange("e (c p) f -> e p c f", p=P)
                rw2 = K.ins["L0_ffn_rw2"].rearrange("e (c p) n -> e p c n", p=P)

                def load(k, u):
                    e = sp.value_load(M.be[0:1, bass.ds(k, 1)], min_val=0, max_val=E - 1)
                    one = bass.ds(e, 1)
                    sp.dma_start(st1[:, u, :, 0], rg[one].rearrange("a p c f -> (a p) c f")).then_inc(w_in[u], 16)
                    sp.dma_start(st1[:, u, :, 1], rw1[one].rearrange("a p c f -> (a p) c f")).then_inc(w_in[u], 16)
                    sp.dma_start(st2[:, u], rw2[one].rearrange("a p c n -> (a p) c n")).then_inc(w_in[u], 16)
                    return one

                def load_bias(one, u):
                    sp.dma_start(b1[:, u, 0:F], K.ins["L0_ffn_rgb"][one, :].broadcast_to([P, F])).then_inc(b_in[u], 16)
                    sp.dma_start(b1[:, u, F:2 * F], K.ins["L0_ffn_rb1"][one, :].broadcast_to([P, F])).then_inc(b_in[u], 16)
                    sp.dma_start(b2[:, u], K.ins["L0_ffn_rb2"][one, :].broadcast_to([P, D])).then_inc(b_in[u], 16)

                def load_idx(k, u):
                    sp.dma_start(idx[:, u], K.idx_d[bass.ds(k * P, P), :]).then_inc(i_in[u], 16)

                def store(k, u):
                    sp.wait_ge(yo_ok, k + 1)
                    sp.dma_start(K.y_d[bass.ds(k * P, P), :], yo[:, u]).then_inc(y_out[u], 16)

                def body(j, first, last):
                    for u in range(2):
                        k = j * 2 + u
                        if not last:
                            sp.wait_ge(w_lo, k + 1)
                            sp.wait_ge(w_lop, k + 1)
                            one = load(k + 2, u)
                            sp.wait_ge(tr, k + 1)
                            load_idx(k + 2, u)
                            sp.wait_ge(yo_ok, k + 1)
                            load_bias(one, u)
                        store(k, u)

                for u in range(2):
                    load_idx(u, u)
                    load_bias(load(u, u), u)
                with sp.Fori(0, LB - 1) as j:
                    body(j, False, False)
                body(LB - 1, False, True)
                for u in range(2):
                    sp.wait_ge(y_out[u], 16 * LB + 16)

            @block.gpsimd
            def _(pool):
                def gather(k, j, u):
                    pool.wait_ge(i_in[u], j * 16 + 16)
                    pool.sem_inc(step_p, 1)
                    pool.indirect_dma_start(out=xg[:, u], out_offset=None, in_=K.h2_d,
                                            in_offset=bass.IndirectOffsetOnAxis(ap=idx[:, u], axis=0)).then_inc(x_in[u], 16)

                def low(k, u):
                    pool.wait_ge(w_hi, k * 2 + 1)
                    nc.gpsimd.tensor_tensor(w1[:, u, 0:PW, 1].rearrange("p c (a f) -> p c a f", a=2), st1[:, u, 0:PW],
                                            w1[:, u, 0:PW, 0].rearrange("p c (a f) -> p c a f", a=2).bitcast(F32),
                                            ALU.subtract).then_inc(w_lop, 1)

                gather(0, 0, 0)
                low(0, 0)

                def body(j, last):
                    for u in range(2):
                        k = j * 2 + u
                        if not (last and u):
                            pool.wait_ge(tr, k)
                            gather(k + 1, j + u, 1 - u)
                            low(k + 1, 1 - u)

                body(0, False)
                with pool.Fori(1, LB - 1) as j:
                    body(j, False)
                body(LB - 1, True)

            @block.scalar
            def _(act):
                def w_high(k, j, u):
                    act.wait_ge(w_in[u], j * 48 + 48)
                    act.wait_ge(gu, k - 1)
                    nc.scalar.activation(w1[:, u, :, 0].rearrange("p c (a f) -> p c a f", a=2), st1[:, u], ACT.Copy).then_inc(w_hi, 1)
                    act.wait_ge(oo, k - 1)
                    nc.scalar.activation(w2[:, u, :, 0], st2[:, u], ACT.Copy).then_inc(w_hi, 1)

                def x_high(k, u):
                    act.wait_ge(tr, k + 1)
                    nc.scalar.activation(xT[:, u, 0], px[:, :], ACT.Copy).then_inc(x_hi, 1)

                def gelu(k, u):
                    act.wait_ge(z_ok, k + 1)
                    nc.scalar.activation(y[:, u], z[:, u, 0:F], ACT.Gelu).then_inc(ge, 1)

                def y_high(k, u):
                    act.wait_ge(yt, k + 1)
                    nc.scalar.activation(yT[:, u, 0], py[:, u, 0:F], ACT.Copy).then_inc(y_hi, 1)

                def head():
                    act.wait_ge(w_in[0], 48)
                    nc.scalar.activation(w1[:, 0, :, 0].rearrange("p c (a f) -> p c a f", a=2), st1[:, 0], ACT.Copy).then_inc(w_hi, 1)
                    nc.scalar.activation(w2[:, 0, :, 0], st2[:, 0], ACT.Copy).then_inc(w_hi, 1)
                    x_high(0, 0)

                def body(j, first, last):
                    for u in range(2):
                        k = j * 2 + u
                        if not (first and not u):
                            y_high(k - 1, 1 - u)
                        if not (last and u):
                            w_high(k + 1, j + u, 1 - u)
                            x_high(k + 1, 1 - u)
                        gelu(k, u)

                run(act, head, body, lambda: y_high(NBLK - 1, 1))

            @block.vector
            def _(dve):
                def w_low(k, u):
                    dve.wait_ge(w_hi, k * 2 + 1)
                    nc.vector.tensor_tensor(w1[:, u, PW:DC, 1].rearrange("p c (a f) -> p c a f", a=2), st1[:, u, PW:DC],
                                            w1[:, u, PW:DC, 0].rearrange("p c (a f) -> p c a f", a=2).bitcast(F32), ALU.subtract)
                    dve.wait_ge(w_hi, k * 2 + 2)
                    nc.vector.tensor_tensor(w2[:, u, :, 1], st2[:, u], w2[:, u, :, 0].bitcast(F32), ALU.subtract).then_inc(w_lo, 1)

                def x_low(k, u):
                    dve.wait_ge(x_hi, k + 1)
                    nc.vector.tensor_tensor(xT[:, u, 1], px[:, :], xT[:, u, 0].bitcast(F32), ALU.subtract).then_inc(x_lo, 1)

                def y_low(k, u):
                    dve.wait_ge(y_hi, k + 1)
                    nc.vector.tensor_tensor(yT[:, u, 1], py[:, u, 0:F], yT[:, u, 0].bitcast(F32), ALU.subtract).then_inc(y_lo, 1)

                def store(k, j, u):
                    dve.wait_ge(oo, k + 1)
                    dve.wait_ge(y_out[u], j * 16 + 16)
                    nc.vector.tensor_tensor(yo[:, u], po[:, u], b2[:, u], ALU.add).then_inc(yo_ok, 1)

                def body(j, first, last):
                    for u in range(2):
                        k = j * 2 + u
                        if not (first and not u):
                            y_low(k - 1, 1 - u)
                        if not (last and u):
                            w_low(k + 1, 1 - u)
                            x_low(k + 1, 1 - u)
                        dve.wait_ge(gu, k + 1)
                        dve.wait_ge(b_in[u], j * 48 + 48)
                        nc.vector.tensor_tensor(z[:, u], pg[:, u], b1[:, u], ALU.add).then_inc(z_ok, 1)
                        if not (first and not u):
                            store(k - 1, j - 1 + u, 1 - u)
                        dve.wait_ge(ge, k + 1)
                        nc.vector.tensor_tensor(y[:, u], y[:, u], z[:, u, F:2 * F], ALU.mult).then_inc(y_ok, 1)

                def head():
                    for u in range(2):
                        dve.sem_inc(y_out[u], 16)
                    w_low(0, 0)
                    x_low(0, 0)

                def tail():
                    y_low(NBLK - 1, 1)
                    store(NBLK - 1, LB - 1, 1)

                run(dve, head, body, tail)

            @block.tensor
            def _(pe):
                def x_trans(k, j, u):
                    pe.wait_ge(x_in[u], j * 16 + 16)
                    for c in range(DC):
                        m = nc.tensor.transpose(px[:, c * P:(c + 1) * P], xg[:, u, c * P:(c + 1) * P], K.ident[:, :])
                    m.then_inc(tr, 1)

                def first_(k, u):
                    pe.wait_ge(x_lo, k + 1)
                    pe.wait_ge(w_lo, k + 1)
                    pe.wait_ge(w_lop, k + 1)
                    c_ = lambda c: slice(c * P, (c + 1) * P)
                    split3(nc, pg[:, u], [(xT[:, u, 0, c_(c)], xT[:, u, 1, c_(c)], w1[:, u, c, 0], w1[:, u, c, 1])
                                          for c in range(DC)]).then_inc(gu, 1)

                def y_trans(k, u):
                    pe.wait_ge(y_ok, k + 1)
                    for c in range(FC):
                        m = nc.tensor.transpose(py[:, u, c * P:(c + 1) * P], y[:, u, c * P:(c + 1) * P], K.ident[:, :])
                    m.then_inc(yt, 1)

                def second(k, u):
                    pe.wait_ge(y_lo, k + 1)
                    c_ = lambda c: slice(c * P, (c + 1) * P)
                    split3(nc, po[:, u], [(yT[:, u, 0, c_(c)], yT[:, u, 1, c_(c)], w2[:, u, c, 0], w2[:, u, c, 1])
                                          for c in range(FC)]).then_inc(oo, 1)

                def body(j, first, last):
                    for u in range(2):
                        k = j * 2 + u
                        first_(k, u)
                        if not (first and not u):
                            y_trans(k - 1, 1 - u)
                        if not (last and u):
                            x_trans(k + 1, j + u, 1 - u)
                        if not (first and not u):
                            second(k - 1, 1 - u)

                def tail():
                    y_trans(NBLK - 1, 1)
                    second(NBLK - 1, 1)

                run(pe, lambda: x_trans(0, 0, 0), body, tail)


def stage_combine(K, M):
    nc = K.nc
    with ExitStack() as ctx:
        sb = lambda n, s, d: K.sb(n, s, d, ctx)
        at = sb("f_at", [P, 2, TOP], I32)
        r = sb("f_r", [P, 2, TOP, D], F32)
        o = sb("f_o", [P, 2, D], F32)
        step_p = K.sem("f_step_p")
        at_ok, dch, o_ok = K.sem("f_at_ok"), K.sem("f_dch"), K.sem("f_o_ok")
        r_in = [K.sem("f_r_in0"), K.sem("f_r_in1")]
        o_out = [K.sem("f_o_out0"), K.sem("f_o_out1")]

        with nc.Block() as block:

            @block.sync
            def _(sp):
                ov = K.out.rearrange("b (t p) n -> (b t) p n", p=P)
                with sp.Fori(0, NT // 2) as j:
                    for u in range(2):
                        t = j * 2 + u
                        sp.wait_ge(o_ok, t + 1)
                        sp.dma_start(ov[bass.ds(t, 1)].rearrange("a p n -> p (a n)"), o[:, u]).then_inc(o_out[u], 16)
                for u in range(2):
                    sp.wait_ge(o_out[u], 16 * (NT // 2))

            @block.gpsimd
            def _(pool):
                with pool.Fori(0, NT // 2) as j:
                    for u in range(2):
                        t = j * 2 + u
                        pool.wait_ge(at_ok, t + 1)
                        pool.sem_inc(step_p, 1)
                        for k in range(TOP):
                            pool.indirect_dma_start(out=r[:, u, k], out_offset=None, in_=K.y_d,
                                                    in_offset=bass.IndirectOffsetOnAxis(ap=at[:, u, k:k + 1], axis=0)
                                                    ).then_inc(r_in[u], 16)

            @block.vector
            def _(dve):
                def places(t, u):
                    nc.vector.tensor_copy(at[:, u], M.pos[:, :, bass.ds(t, 1)].rearrange("p k a -> p (k a)")).then_inc(at_ok, 1)

                def tiles(j, more):
                    for u in range(2):
                        t = j * 2 + u
                        ch = Chain(dve, dch, t * 3)
                        dve.wait_ge(r_in[u], j * 32 + 32)
                        dve.wait_ge(o_out[u], j * 16)
                        w = lambda k: M.wt[:, k, bass.ds(t, 1)]
                        ch.after(nc.vector.tensor_scalar(r[:, u, 0], r[:, u, 0], w(0), None, ALU.mult))
                        ch.after(nc.vector.scalar_tensor_tensor(out=r[:, u, 0], in0=r[:, u, 1], scalar=w(1), in1=r[:, u, 0],
                                                                op0=ALU.mult, op1=ALU.add))
                        row = M.rows[:, bass.ds(j // 2, 1), 3].rearrange("p a n -> p (a n)")
                        ch.after(nc.vector.tensor_tensor(r[:, u, 0], r[:, u, 0], row, ALU.mult))
                        nc.vector.tensor_tensor(o[:, u], r[:, u, 0], M.base[:, bass.ds(t, 1)].rearrange("p a n -> p (a n)"),
                                                ALU.add).then_inc(o_ok, 1)
                        if more:
                            dve.wait_ge(o_ok, t + 1)
                            places(t + 2, u)

                places(0, 0)
                places(1, 1)
                tiles(0, True)
                with dve.Fori(1, NT // 2 - 1) as j:
                    tiles(j, True)
                tiles(NT // 2 - 1, False)


class Kept:

    def __init__(self, K, ctx):
        self.rows = K.sb("rows", [P, B, 4, D], F32, ctx)
        self.base = K.sb("base", [P, NT, D], F32, ctx)
        self.aff = K.sb("aff", [P, NT, E], F32, ctx)
        self.wt = K.sb("wt", [P, TOP, NT], F32, ctx)
        self.pos = K.sb("pos", [P, TOP, NT], I32, ctx)
        self.be = K.sb("be", [P, NBLK], I32, ctx)


def program(nc, ins, out):
    with ExitStack() as ctx:
        K = Kernel(nc, ctx, ins, out)
        with ExitStack() as att:
            Mhl = K.sb("Mhl", [P, H, 2, D], F32R, att)
            modcol = K.sb("modcol", [P, B, 2, DC], F32, att)
            stage_weights(K, Mhl, modcol)
            stage_project(K, modcol)
            stage_attention(K, Mhl)
        with ExitStack() as moe:
            M = Kept(K, moe)
            stage_shared(K, M)
            stage_route(K, M)
            stage_routed(K, M)
            stage_combine(K, M)


_INS = ["L0_attn_x", "L0_attn_wq", "L0_attn_wkv_a", "L0_attn_wkv_b", "L0_attn_wo", "L0_ffn_wa", "L0_ffn_rg",
        "L0_ffn_rgb", "L0_ffn_rw1", "L0_ffn_rb1", "L0_ffn_rw2", "L0_ffn_rb2", "L0_ffn_sg", "L0_ffn_sgb",
        "L0_ffn_sw1", "L0_ffn_sb1", "L0_ffn_sw2", "L0_ffn_sb2", "L0_c", "L0_wmod"]


def constants():
    inv = (np.float32(1.0) / np.float32(10000.0) ** (np.arange(HALF, dtype=np.float32) * np.float32(2.0)
                                                     / np.float32(ROPE))).astype(np.float32)
    ang = (np.arange(S, dtype=np.float32)[:, None] * inv[None, :]).astype(np.float32)
    rope = np.concatenate([np.cos(ang), np.sin(ang)], axis=1).astype(np.float32)
    k, m = np.arange(P)[:, None], np.arange(P)[None, :]
    const = np.stack([k == m, np.where(m > k, -1e30, 0.0), k < m]).astype(np.float32)
    e, f = np.arange(E)[:, None], np.arange(E)[None, :]
    small = np.concatenate([E - np.arange(E), (f < e).ravel(), np.arange(NBLK)]).astype(np.float32)[None, :]
    tok = (np.arange(P)[:, None] + P * np.arange(NT)[None, :]).astype(np.int32)
    return {"c_rope": rope, "c_const": const, "c_small": small, "c_tok": tok}


def kernel(**inputs):
    import concourse.bacc as _bacc
    from concourse.bass_utils import run_bass_kernel_spmd as _run

    nc = _bacc.Bacc("TRN2", target_bir_lowering=False, num_devices=1)
    arrays, ins = {}, {}
    for name, a in [(n, inputs[n]) for n in _INS] + list(constants().items()):
        a = np.ascontiguousarray(a)
        arrays[f"in_{name}"] = a
        ins[name] = nc.dram_tensor(f"in_{name}", a.shape, mybir.dt.from_np(a.dtype), kind="ExternalInput").ap()
    out = nc.dram_tensor("out_0", (B, S, D), F32, kind="ExternalOutput").ap()
    program(nc, ins, out)
    r = _run(nc, [arrays], core_ids=[0])
    return r.results[0]["out_0"]
```

```python
from contextlib import ExitStack

import numpy as np
import concourse.bass as bass
from concourse import mybir

ALU = mybir.AluOpType
ACT = mybir.ActivationFunctionType
AX = mybir.AxisListType
F32 = mybir.dt.float32
F32R = mybir.dt.float32r
BF16 = mybir.dt.bfloat16
I32 = mybir.dt.int32
U32 = mybir.dt.uint32

B, S, D = 4, 512, 512
H, NOPE, ROPE, VD, LORA = 16, 128, 64, 128, 128
E, SH, F = 16, 2, 256
P = 128
DC = D // P
FC = F // P
TB = S // P
NT = B * TB
QD = NOPE + ROPE
KVD = NOPE + VD
SCALE = 1.0 / float(np.sqrt(NOPE + ROPE))
EPS = 1e-5
HALF = ROPE // 2
TOP = 2
PB = 2 * P
NBLK = (B * S * TOP) // PB + E
VECS = 6


class Chain:

    def __init__(self, eng, sem, base=0):
        self.eng, self.sem, self.base, self.n = eng, sem, base, 0

    def after(self, ins):
        ins.then_inc(self.sem, 1)
        self.wait()

    def wait(self):
        self.n += 1
        self.eng.wait_ge(self.sem, self.base + self.n)


class Kernel:

    def __init__(self, nc, ctx, ins, out):
        self.nc, self.ctx, self.out = nc, ctx, out
        self.ins = ins
        self.sems = []
        d = lambda name, shape, dt: nc.dram_tensor(name, shape, dt, kind="Internal").ap()
        self.mod_d = d("mod_d", [B, VECS * D], F32)
        self.wqk_d = d("wqk_d", [H, P, 2, DC, P], F32)
        self.hT_d = d("hT_d", [B, P, DC, 2, S], F32)
        self.cT_d = d("cT_d", [B, P, 2, S], F32)
        self.kpe_d = d("kpe_d", [B, P, 2, S], F32)
        self.c_d = d("c_d", [B, P, TB, 2, P], F32)
        self.qpe_d = d("qpe_d", [B, H, P, S], F32)
        self.attn_d = d("attn_d", [NT, P, D], F32)
        self.h2_d = d("h2_d", [B * S, D], F32)
        self.y_d = d("y_d", [NBLK * PB, D], F32)
        self.idx_d = d("idx_d", [NBLK * PB, 1], I32)
        self.ident = self.sb("ident", [P, P], F32)
        self.identb = self.sb("identb", [P, P], BF16)
        self.maskb = self.sb("maskb", [P, P], BF16)

    def sb(self, name, shape, dt, ctx=None):
        return (ctx or self.ctx).enter_context(self.nc.sbuf_tensor(name, shape, dt))

    def ps(self, name, shape, dt, ctx):
        return ctx.enter_context(self.nc.psum_tensor(name, shape, dt))

    def sem(self, name):
        self.sems.append(self.nc.alloc_semaphore(name=name))
        return self.sems[-1]

    def free_sems(self):
        self.nc.all_engine_barrier()
        self.nc.clear_and_free_semaphores(self.sems)
        self.nc.all_engine_barrier()
        self.sems = []


def split3(nc, out, pairs):
    last = None
    for n, (sh, sl, mh, ml) in enumerate(pairs):
        nc.tensor.matmul(out, sh, mh, start=n == 0, stop=False)
        nc.tensor.matmul(out, sh, ml, start=False, stop=False)
        last = nc.tensor.matmul(out, sl, mh, start=False, stop=n == len(pairs) - 1)
    return last


def stage_weights(K, Mhl, modcol):
    nc = K.nc
    with ExitStack() as ctx:
        sb = lambda n, s, d: K.sb(n, s, d, ctx)
        constf = sb("w_constf", [P, 2, P], F32)
        cs = sb("w_c", [B, D], F32)
        csg = sb("w_csg", [B, D], F32)
        csT = sb("w_csT", [P, DC, B], F32)
        wm = sb("w_wm", [P, 2, DC, D], F32)
        mrow = sb("w_mrow", [B, VECS, D], F32)
        msgn = sb("w_msgn", [B, 2, D], F32)
        wq = sb("w_wq", [P, 2, DC, P], F32)
        wkv = sb("w_wkv", [P, 2, KVD], F32)
        wo = sb("w_wo", [P, 2, D], F32)
        wqT = sb("w_wqT", [P, 2, D], F32)
        kvT = sb("w_kvT", [P, 2, KVD], F32)
        hl = sb("w_hl", [P, 2, 2, D], F32R)
        pq = K.ps("w_pq", [P, 2, D], F32, ctx)
        pk = K.ps("w_pk", [P, 2, D], F32, ctx)
        pw = K.ps("w_pw", [P, 2, D], F32, ctx)
        pm = K.ps("w_pm", [P, 2, D], F32, ctx)
        const_in, c_in, const_ok = K.sem("w_const_in"), K.sem("w_c_in"), K.sem("w_const_ok")
        silu, mod_t, mod_tc = K.sem("w_silu"), K.sem("w_mod_t"), K.sem("w_mod_tc")
        wm_in = [K.sem("w_wm_in0"), K.sem("w_wm_in1")]
        mod_mm, mod_ev, dch = K.sem("w_mod_mm"), K.sem("w_mod_ev"), K.sem("w_dch")
        mod_ok, col_t, col_ok, mod_out = K.sem("w_mod_ok"), K.sem("w_col_t"), K.sem("w_col_ok"), K.sem("w_mod_out")
        in_s = [K.sem("w_in0"), K.sem("w_in1")]
        out_s = [K.sem("w_out0"), K.sem("w_out1")]
        tr, ev_q, ev_k, mm = K.sem("w_tr"), K.sem("w_ev_q"), K.sem("w_ev_k"), K.sem("w_mm")
        hi_w, lo_w = K.sem("w_hi"), K.sem("w_lo")

        with nc.Block() as block:

            @block.sync
            def _(sp):
                sp.dma_start(constf[:, :, :], K.ins["c_const"][0:2].rearrange("a p c -> p a c")).then_inc(const_in, 16)
                sp.dma_start(cs[:, :], K.ins["L0_c"]).then_inc(c_in, 16)
                wmv = K.ins["L0_wmod"].rearrange("(c p) (v n) -> v p c n", p=P, n=D)
                for v in range(VECS):
                    if v >= 2:
                        sp.wait_ge(mod_mm, v - 1)
                    sp.dma_start(wm[:, v % 2], wmv[v]).then_inc(wm_in[v % 2], 16)
                def load(h, u):
                    sp.dma_start(wq[:, u], K.ins["L0_attn_wq"].rearrange("(c p) n -> p c n", p=P)[
                        :, :, bass.ds(h * QD, NOPE)]).then_inc(in_s[u], 16)
                    sp.dma_start(wkv[:, u], K.ins["L0_attn_wkv_b"][:, bass.ds(h * KVD, KVD)]).then_inc(in_s[u], 16)
                    sp.dma_start(wo[:, u], K.ins["L0_attn_wo"][bass.ds(h * VD, VD), :]).then_inc(in_s[u], 16)

                def heads(j, more):
                    for u in range(2):
                        h = j * 2 + u
                        if more:
                            sp.wait_ge(mm, h + 1)
                            load(h + 2, u)
                        sp.wait_ge(hi_w, h * 2 + 1)
                        sp.wait_ge(lo_w, h * 2 + 1)
                        sp.dma_start(K.wqk_d[bass.ds(h, 1)].rearrange("a p s c n -> p (a s) (c n)"),
                                     hl[:, u].bitcast(F32)).then_inc(out_s[u], 16)

                load(0, 0)
                load(1, 1)
                with sp.Fori(0, H // 2 - 1) as j:
                    heads(j, True)
                heads(H // 2 - 1, False)
                for u in range(2):
                    sp.wait_ge(out_s[u], 16 * (H // 2 + 1))
                sp.wait_ge(mod_ok, 1)
                sp.dma_start(K.mod_d.rearrange("b (v n) -> b v n", n=D), mrow[:, :, :]).then_inc(mod_out, 16)
                sp.wait_ge(mod_out, 16)

            @block.scalar
            def _(act):
                act.wait_ge(c_in, 16)
                nc.scalar.activation(csg[:, :], cs[:, :], ACT.Sigmoid).then_inc(silu, 1)
                act.sem_inc(out_s[0], 16)
                act.sem_inc(out_s[1], 16)
                with act.Fori(0, H // 2) as j:
                    for u in range(2):
                        h = j * 2 + u
                        act.wait_ge(tr, h + 1)
                        nc.scalar.activation(wqT[:, u], pq[:, u], ACT.Copy).then_inc(ev_q, 1)
                        act.wait_ge(mm, h + 1)
                        act.wait_ge(out_s[u], j * 16 + 16)
                        nc.scalar.activation(hl[:, u, 0], pw[:, u], ACT.Copy).then_inc(hi_w, 1)
                        nc.scalar.activation(Mhl[:, bass.ds(h, 1), 0, :].rearrange("p a n -> p (a n)"),
                                             pm[:, u], ACT.Copy).then_inc(hi_w, 1)

            @block.vector
            def _(dve):
                dve.wait_ge(const_in, 16)
                nc.vector.tensor_copy(K.ident[:, :], constf[:, 0]).then_inc(const_ok, 1)
                nc.vector.tensor_copy(K.identb[:, :], constf[:, 0]).then_inc(const_ok, 1)
                nc.vector.tensor_copy(K.maskb[:, :], constf[:, 1]).then_inc(const_ok, 1)
                dve.wait_ge(silu, 1)
                nc.vector.tensor_tensor(csg[:, :], csg[:, :], cs[:, :], ALU.mult).then_inc(silu, 1)
                dve.wait_ge(mod_t, 1)
                nc.vector.tensor_copy(csT[:, :, :], pk[:, 0, 0:DC * B].rearrange("p (c b) -> p c b", b=B)).then_inc(mod_tc, 1)
                for v in range(VECS):
                    dve.wait_ge(mod_mm, v + 1)
                    nc.vector.tensor_copy(mrow[:, v], pm[0:B, v % 2]).then_inc(mod_ev, 1)
                dve.wait_ge(mod_ev, VECS)
                ch = Chain(dve, dch)
                for v in (1, 4):
                    nc.vector.tensor_scalar(mrow[:, v], mrow[:, v], 1.0, None, ALU.add).then_inc(mod_ev, 1)
                for n, v in enumerate((2, 5)):
                    ch.after(nc.vector.tensor_scalar(msgn[:, n], mrow[:, v], 0.0, 2.0, ALU.is_ge, ALU.mult))
                    ch.after(nc.vector.tensor_scalar(msgn[:, n], msgn[:, n], -1.0, None, ALU.add))
                    ch.after(nc.vector.tensor_tensor(mrow[:, v], mrow[:, v], msgn[:, n], ALU.mult))
                    ch.after(nc.vector.tensor_scalar(mrow[:, v], mrow[:, v], 0.25, None, ALU.max))
                    ch.after(nc.vector.tensor_tensor(mrow[:, v], mrow[:, v], msgn[:, n], ALU.mult))
                dve.wait_ge(mod_ev, VECS + 2)
                nc.vector.tensor_scalar(msgn[:, 0], msgn[:, 0], 1.0, None, ALU.mult).then_inc(mod_ok, 1)
                dve.wait_ge(col_t, 1)
                nc.vector.tensor_copy(modcol[:, :, :, :], pk[:, 1, 0:2 * DC * B].rearrange(
                    "p (v c b) -> p b v c", v=2, c=DC)).then_inc(col_ok, 1)
                with dve.Fori(0, H // 2) as j:
                    for u in range(2):
                        h = j * 2 + u
                        dve.wait_ge(tr, h + 1)
                        nc.vector.tensor_copy(kvT[:, u], pk[:, u, 0:KVD]).then_inc(ev_k, 1)
                        dve.wait_ge(hi_w, h * 2 + 1)
                        nc.vector.tensor_tensor(hl[:, u, 1], pw[:, u], hl[:, u, 0].bitcast(F32),
                                                ALU.subtract).then_inc(lo_w, 1)
                        dve.wait_ge(hi_w, h * 2 + 2)
                        nc.vector.tensor_tensor(Mhl[:, bass.ds(h, 1), 1, :].rearrange("p a n -> p (a n)"), pm[:, u],
                                                Mhl[:, bass.ds(h, 1), 0, :].rearrange("p a n -> p (a n)").bitcast(F32),
                                                ALU.subtract).then_inc(lo_w, 1)

            @block.tensor
            def _(pe):
                pe.wait_ge(const_ok, 3)
                pe.wait_ge(silu, 2)
                for c in range(DC):
                    t = nc.tensor.transpose(pk[:, 0, c * B:(c + 1) * B], csg[:, c * P:(c + 1) * P], K.ident[0:B, 0:B])
                t.then_inc(mod_t, 1)
                pe.wait_ge(mod_tc, 1)
                for v in range(VECS):
                    pe.wait_ge(wm_in[v % 2], 16 * (v // 2 + 1))
                    if v >= 2:
                        pe.wait_ge(mod_ev, v - 1)
                    for c in range(DC):
                        m = nc.tensor.matmul(pm[0:B, v % 2], csT[:, c], wm[:, v % 2, c], start=c == 0, stop=c == DC - 1)
                    m.then_inc(mod_mm, 1)
                pe.wait_ge(mod_ok, 1)
                for v in range(2):
                    for c in range(DC):
                        o = (v * DC + c) * B
                        t = nc.tensor.transpose(pk[:, 1, o:o + B], mrow[:, v, c * P:(c + 1) * P], K.ident[0:B, 0:B])
                t.then_inc(col_t, 1)
                pe.wait_ge(col_ok, 1)
                with pe.Fori(0, H // 2) as j:
                    for u in range(2):
                        h = j * 2 + u
                        pe.wait_ge(in_s[u], j * 48 + 48)
                        for c in range(DC):
                            nc.tensor.transpose(pq[:, u, c * P:(c + 1) * P], wq[:, u, c], K.ident[:, :])
                        for n in range(2):
                            t = nc.tensor.transpose(pk[:, u, n * P:(n + 1) * P], wkv[:, u, n * P:(n + 1) * P], K.ident[:, :])
                        t.then_inc(tr, 1)
                    for u in range(2):
                        h = j * 2 + u
                        pe.wait_ge(ev_q, h + 1)
                        pe.wait_ge(ev_k, h + 1)
                        for c in range(DC):
                            nc.tensor.matmul(pw[:, u, c * P:(c + 1) * P], wqT[:, u, c * P:(c + 1) * P],
                                             kvT[:, u, 0:P], start=True, stop=True)
                        nc.tensor.matmul(pm[:, u], kvT[:, u, P:2 * P], wo[:, u], start=True, stop=True).then_inc(mm, 1)
                    pe.wait_ge(lo_w, j * 4 + 4)


def stage_project(K, modcol):
    nc = K.nc
    NQ = H * ROPE
    NC = LORA + ROPE
    with ExitStack() as ctx:
        sb = lambda n, s, d: K.sb(n, s, d, ctx)
        wst = sb("p_wst", [P, DC, NQ], F32)
        wpe = sb("p_wpe", [P, DC, 2, NQ], F32R)
        wcst = sb("p_wcst", [P, DC, NC], F32)
        wc = sb("p_wc", [P, DC, 2, NC], F32R)
        rope = sb("p_rope", [P, TB, ROPE], F32)
        half = sb("p_half", [P, 1], F32)
        x = sb("p_x", [P, 2, D], F32)
        st = sb("p_st", [P, 2, 6], F32)
        mv = sb("p_mv", [P, 2, 4], F32)
        hf = sb("p_hf", [P, 2, DC, P], F32)
        hT = sb("p_hT", [P, 2, DC, 2, P], F32R)
        cf = sb("p_cf", [P, 2, P], F32)
        chl = sb("p_chl", [P, 2, 2, P], F32R)
        qk = sb("p_qk", [P, 2, H + 1, ROPE], F32)
        rt = sb("p_rt", [P, 2, 4, H + 1, HALF], F32)
        qr = sb("p_qr", [P, 2, H + 1, ROPE], F32)
        qs = sb("p_qs", [P, 2, H, P], F32R)
        ck = sb("p_ck", [P, 2, 2, 2, P], F32R)
        px = K.ps("p_px", [P, 2, DC * P], F32, ctx)
        pc = K.ps("p_pc", [P, 512], F32, ctx)
        pq = K.ps("p_pq", [P, NQ], F32, ctx)
        pt = K.ps("p_pt", [P, 2, 4 * P], F32, ctx)
        pk = K.ps("p_pk", [P, 512], F32, ctx)
        w_in, w_hi, w_lo = K.sem("p_w_in"), K.sem("p_w_hi"), K.sem("p_w_lo")
        x_in = [K.sem("p_x_in0"), K.sem("p_x_in1")]
        pch, dch = K.sem("p_pch"), K.sem("p_dch")
        step_v, step_e = K.sem("p_step_v"), K.sem("p_step_e")
        var_ok, rstd_ok, x_n, x_t = K.sem("p_var_ok"), K.sem("p_rstd_ok"), K.sem("p_x_n"), K.sem("p_x_t")
        h_full, h_hi, h_lo = K.sem("p_h_full"), K.sem("p_h_hi"), K.sem("p_h_lo")
        proj, pev = K.sem("p_proj"), K.sem("p_pev")
        c_hi, c_lo = K.sem("p_c_hi"), K.sem("p_c_lo")
        rot_p, rot = K.sem("p_rot_p"), K.sem("p_rot")
        qt, q_hi, q_lo = K.sem("p_qt"), K.sem("p_q_hi"), K.sem("p_q_lo")
        kt, k_hi, k_lo = K.sem("p_kt"), K.sem("p_k_hi"), K.sem("p_k_lo")
        out_s = [K.sem("p_out0"), K.sem("p_out1")]
        NOUT = 5

        with nc.Block() as block:

            @block.sync
            def _(sp):
                xv = K.ins["L0_attn_x"].rearrange("b (t p) n -> (b t) p n", p=P)
                wqv = K.ins["L0_attn_wq"].rearrange("(c p) (h q) -> p c h q", p=P, q=QD)
                for c in range(DC):
                    sp.dma_start(wst[:, c].rearrange("p (h q) -> p h q", q=ROPE), wqv[:, c, :, NOPE:QD]).then_inc(w_in, 16)
                sp.dma_start(wcst[:, :, :], K.ins["L0_attn_wkv_a"].rearrange("(c p) n -> p c n", p=P)).then_inc(w_in, 16)
                sp.dma_start(rope[:, :, :], K.ins["c_rope"].rearrange("(t p) n -> p t n", p=P)).then_inc(w_in, 16)
                for u in range(2):
                    sp.dma_start(x[:, u], xv[u]).then_inc(x_in[u], 16)
                def tiles(j, more):
                    b = j // 2
                    for u in range(2):
                        t = j * 2 + u
                        ti = (j % 2) * 2 + u
                        tok = ti * P
                        if more:
                            sp.wait_ge(x_t, t + 1)
                            sp.dma_start(x[:, u], xv[bass.ds(t + 2, 1)].rearrange("a p n -> p (a n)")).then_inc(x_in[u], 16)
                        sp.wait_ge(h_hi, t + 1)
                        sp.wait_ge(h_lo, t + 1)
                        sp.dma_start(K.hT_d[bass.ds(b, 1), :, :, :, bass.ds(tok, P)].rearrange("a p c s n -> (a p) c s n"),
                                     hT[:, u].bitcast(F32)).then_inc(out_s[u], 16)
                        sp.wait_ge(c_hi, t + 1)
                        sp.wait_ge(c_lo, t + 1)
                        sp.dma_start(K.c_d[bass.ds(b, 1), :, bass.ds(ti, 1)].rearrange("a p t s n -> (a p) (t s) n"),
                                     chl[:, u].bitcast(F32)).then_inc(out_s[u], 16)
                        sp.wait_ge(k_hi, t + 1)
                        sp.wait_ge(k_lo, t + 1)
                        sp.dma_start(K.cT_d[bass.ds(b, 1), :, :, bass.ds(tok, P)].rearrange("a p s n -> (a p) s n"),
                                     ck[:, u, :, 0].bitcast(F32)).then_inc(out_s[u], 16)
                        sp.dma_start(K.kpe_d[bass.ds(b, 1), :, :, bass.ds(tok, P)].rearrange("a p s n -> (a p) s n"),
                                     ck[:, u, :, 1].bitcast(F32)).then_inc(out_s[u], 16)
                        sp.wait_ge(q_hi, t * 4 + 4)
                        sp.wait_ge(q_lo, t * 4 + 4)
                        sp.dma_start(K.qpe_d[bass.ds(b, 1), :, :, bass.ds(tok, P)].rearrange("a h p n -> p (a h) n"),
                                     qs[:, u].bitcast(F32)).then_inc(out_s[u], 16)

                with sp.Fori(0, NT // 2 - 1) as j:
                    tiles(j, True)
                tiles(NT // 2 - 1, False)
                for u in range(2):
                    sp.wait_ge(out_s[u], 16 * NOUT * (NT // 2 + 1))

            @block.gpsimd
            def _(pool):
                nc.gpsimd.memset(half[:, :], -0.5).then_inc(pch, 1)
                pool.wait_ge(pch, 1)
                with pool.Fori(0, NT // 2) as j:
                    for u in range(2):
                        t = j * 2 + u
                        ti = (j % 2) * 2 + u
                        pool.wait_ge(var_ok, t + 1)
                        nc.gpsimd.tensor_tensor(mv[:, u, 3:4], mv[:, u, 2:3], half[:, :], ALU.pow).then_inc(rstd_ok, 1)
                        pool.wait_ge(pev, t * 2 + 2)
                        sin = rope[:, bass.ds(ti, 1), HALF:ROPE].broadcast_to([P, H + 1, HALF])
                        nc.gpsimd.tensor_tensor(rt[:, u, 0], qk[:, u, :, 1::2], sin, ALU.mult)
                        nc.gpsimd.tensor_tensor(rt[:, u, 1], qk[:, u, :, 0::2], sin, ALU.mult).then_inc(rot_p, 1)

            @block.scalar
            def _(act):
                act.wait_ge(w_in, 96)
                nc.scalar.activation(wc[:, :, 0], wcst[:, :, :], ACT.Copy).then_inc(w_hi, 1)
                for c in range(DC):
                    nc.scalar.activation(wpe[:, c, 0], wst[:, c], ACT.Copy).then_inc(w_hi, 1)
                for u in range(2):
                    act.sem_inc(out_s[u], 16 * NOUT)
                with act.Fori(0, NT // 2) as j:
                    for u in range(2):
                        t = j * 2 + u
                        act.wait_ge(h_full, t + 1)
                        act.wait_ge(out_s[u], j * (16 * NOUT) + 16 * NOUT)
                        nc.scalar.activation(hT[:, u, :, 0], hf[:, u], ACT.Copy).then_inc(h_hi, 1)
                        act.wait_ge(proj, t * 2 + 1)
                        nc.scalar.activation(cf[:, u], pc[:, 0:LORA], ACT.Copy).then_inc(pev, 1)
                        nc.scalar.activation(qk[:, u, H], pc[:, LORA:NC], ACT.Copy)
                        nc.scalar.activation(chl[:, u, 0], pc[:, 0:LORA], ACT.Copy).then_inc(c_hi, 1)
                        act.wait_ge(proj, t * 2 + 2)
                        nc.scalar.activation(qk[:, u, 0:H].rearrange("p h q -> p (h q)"), pq[:, :], ACT.Copy).then_inc(pev, 1)
                        act.wait_ge(kt, t + 1)
                        nc.scalar.activation(ck[:, u, 0, 0], pk[:, 0:P], ACT.Copy)
                        nc.scalar.activation(ck[0:ROPE, u, 0, 1], pk[0:ROPE, P:2 * P], ACT.Copy)
                        nc.scalar.activation(ck[ROPE:P, u, 0, 1], pk[0:ROPE, P:2 * P], ACT.Copy).then_inc(k_hi, 1)
                        for g in range(4):
                            act.wait_ge(qt, t * 4 + g + 1)
                            nc.scalar.activation(qs[0:ROPE, u, 4 * g:4 * g + 4].rearrange("p h n -> p (h n)"), pt[0:ROPE, g % 2],
                                                 ACT.Copy, scale=SCALE).then_inc(q_hi, 1)

            @block.vector
            def _(dve):
                dve.wait_ge(w_hi, 1)
                nc.vector.tensor_tensor(wc[:, :, 1], wcst[:, :, :], wc[:, :, 0].bitcast(F32), ALU.subtract).then_inc(w_lo, 1)
                for c in range(DC):
                    dve.wait_ge(w_hi, c + 2)
                    nc.vector.tensor_tensor(wpe[:, c, 1], wst[:, c], wpe[:, c, 0].bitcast(F32), ALU.subtract).then_inc(w_lo, 1)

                def norm(j, u):
                    t = j * 2 + u
                    dve.wait_ge(x_in[u], j * 16 + 16)
                    ch = Chain(dve, dch, t * 4)
                    nc.vector.bn_stats(st[:, u], x[:, u]).then_inc(ch.sem, 1)
                    ch.wait()
                    dve.sem_inc(step_v, 1)
                    ch.after(nc.vector.bn_aggr(mv[:, u, 0:2], st[:, u]))
                    nc.vector.tensor_scalar(mv[:, u, 2:3], mv[:, u, 1:2], EPS, None, ALU.add).then_inc(var_ok, 1)
                    dve.wait_ge(rstd_ok, t + 1)
                    nc.vector.tensor_scalar(x[:, u], x[:, u], mv[:, u, 0:1], mv[:, u, 3:4], ALU.subtract, ALU.mult).then_inc(x_n, 1)
                    return ch

                with dve.Fori(0, NT // 2) as j:
                    b = j // 2
                    for u in range(2):
                        t = j * 2 + u
                        ti = (j % 2) * 2 + u
                        ch = norm(j, u)
                        dve.wait_ge(x_t, t + 1)
                        ca = modcol[:, bass.ds(b, 1), 1, :].rearrange("p a c -> p (a c)").unsqueeze(2).broadcast_to([P, DC, P])
                        sa = modcol[:, bass.ds(b, 1), 0, :].rearrange("p a c -> p (a c)").unsqueeze(2).broadcast_to([P, DC, P])
                        pxv = px[:, u].rearrange("p (c n) -> p c n", c=DC)
                        ch.after(nc.vector.tensor_tensor(hf[:, u], pxv, ca, ALU.mult))
                        nc.vector.tensor_tensor(hf[:, u], hf[:, u], sa, ALU.add).then_inc(h_full, 1)
                        dve.wait_ge(h_hi, t + 1)
                        nc.vector.tensor_tensor(hT[:, u, :, 1], hf[:, u], hT[:, u, :, 0].bitcast(F32), ALU.subtract).then_inc(h_lo, 1)
                        dve.wait_ge(c_hi, t + 1)
                        nc.vector.tensor_tensor(chl[:, u, 1], cf[:, u], chl[:, u, 0].bitcast(F32), ALU.subtract).then_inc(c_lo, 1)
                        dve.wait_ge(pev, t * 2 + 2)
                        cos = rope[:, bass.ds(ti, 1), 0:HALF].broadcast_to([P, H + 1, HALF])
                        nc.vector.tensor_tensor(rt[:, u, 2], qk[:, u, :, 0::2], cos, ALU.mult)
                        ch.after(nc.vector.tensor_tensor(rt[:, u, 3], qk[:, u, :, 1::2], cos, ALU.mult))
                        dve.wait_ge(rot_p, t + 1)
                        nc.vector.tensor_tensor(qr[:, u, :, 0:HALF], rt[:, u, 2], rt[:, u, 0], ALU.subtract)
                        nc.vector.tensor_tensor(qr[:, u, :, HALF:ROPE], rt[:, u, 3], rt[:, u, 1], ALU.add).then_inc(rot, 1)
                        dve.wait_ge(k_hi, t + 1)
                        nc.vector.tensor_tensor(ck[:, u, 1, 0], pk[:, 0:P], ck[:, u, 0, 0].bitcast(F32), ALU.subtract)
                        for r in (slice(0, ROPE), slice(ROPE, P)):
                            m = nc.vector.tensor_tensor(ck[r, u, 1, 1], pk[0:ROPE, P:2 * P],
                                                        ck[0:ROPE, u, 0, 1].bitcast(F32), ALU.subtract)
                        m.then_inc(k_lo, 1)
                        for g in range(4):
                            dve.wait_ge(q_hi, t * 4 + g + 1)
                            part = lambda r: qs[r, u, 4 * g:4 * g + 4].rearrange("p h n -> p (h n)")
                            nc.vector.scalar_tensor_tensor(out=part(slice(ROPE, P)), in0=pt[0:ROPE, g % 2], scalar=SCALE,
                                                           in1=part(slice(0, ROPE)).bitcast(F32),
                                                           op0=ALU.mult, op1=ALU.subtract).then_inc(q_lo, 1)
                        assert ch.n == 4

            @block.tensor
            def _(pe):
                pe.wait_ge(w_lo, DC + 1)
                with pe.Fori(0, NT // 2) as j:
                    for u in range(2):
                        t = j * 2 + u
                        pe.wait_ge(x_n, t + 1)
                        for c in range(DC):
                            m = nc.tensor.transpose(px[:, u, c * P:(c + 1) * P], x[:, u, c * P:(c + 1) * P], K.ident[:, :])
                        m.then_inc(x_t, 1)
                        pe.wait_ge(h_lo, t + 1)
                        hs = [(hT[:, u, c, 0], hT[:, u, c, 1]) for c in range(DC)]
                        split3(nc, pc[:, 0:NC], [(*hs[c], wc[:, c, 0], wc[:, c, 1]) for c in range(DC)]).then_inc(proj, 1)
                        for n in range(NQ // 512):
                            w = slice(n * 512, (n + 1) * 512)
                            m = split3(nc, pq[:, w], [(*hs[c], wpe[:, c, 0, w], wpe[:, c, 1, w]) for c in range(DC)])
                        m.then_inc(proj, 1)
                        pe.wait_ge(rot, t + 1)
                        nc.tensor.transpose(pk[:, 0:P], cf[:, u], K.ident[:, :])
                        nc.tensor.transpose(pk[0:ROPE, P:2 * P], qr[:, u, H], K.ident[:, :]).then_inc(kt, 1)
                        for g in range(4):
                            if g >= 2:
                                pe.wait_ge(q_lo, t * 4 + g - 1)
                                pe.sem_inc(step_e, 1)
                            for i in range(4):
                                m = nc.tensor.transpose(pt[0:ROPE, g % 2, i * P:(i + 1) * P], qr[:, u, 4 * g + i], K.ident[:, :])
                            m.then_inc(qt, 1)
                        pe.wait_ge(k_lo, t + 1)
                        pe.wait_ge(q_lo, t * 4 + 4)


def stage_attention(K, Mhl):
    nc = K.nc
    PAIRS = H // 2
    OFF = {0: 0, 3: 5 * P, 1: 6 * P, 2: 9 * P}
    ZERO = 4 * P
    NPT = 11 * P
    with ExitStack() as ctx:
        sb = lambda n, s, d: K.sb(n, s, d, ctx)
        hT = sb("a_hT", [P, 2, DC, 2, S], F32R)
        cT = sb("a_cT", [P, 2, 2, S], F32R)
        kpe = sb("a_kpe", [P, 2, 2, S], F32R)
        cv = sb("a_cv", [P, TB, 2, P], F32R)
        wqk = sb("a_wqk", [P, 2, 2, DC, P], F32R)
        qpe = sb("a_qpe", [P, 2, S], F32R)
        qT = sb("a_qT", [P, 2, S], F32R)
        pr = sb("a_pr", [P, TB, S], F32)
        pT = sb("a_pT", [P, 2, NPT], F32R)
        oT = sb("a_oT", [P, 2, 2, S], F32R)
        acc = sb("a_acc", [P, TB, D], F32)
        nmax = sb("a_nmax", [P, TB], F32)
        rsum = sb("a_rsum", [P, TB], F32)
        rinv = sb("a_rinv", [P, TB], F32)
        psS = K.ps("a_psS", [P, 3, 512], F32, ctx)
        psX = K.ps("a_psX", [P, 512], F32, ctx)
        psY = K.ps("a_psY", [P, 512], F32, ctx)
        psZ = K.ps("a_psZ", [P, 512], F32, ctx)
        psT = K.ps("a_psT", [P, 2, 512], F32, ctx)
        b_in = [K.sem("a_b_in0"), K.sem("a_b_in1")]
        c_in, landed = K.sem("a_c_in"), K.sem("a_landed")
        w_in = [K.sem("a_w_in0"), K.sem("a_w_in1")]
        q_in = [K.sem("a_q_in0"), K.sem("a_q_in1")]
        qp, q_hi, q_lo = K.sem("a_qp"), K.sem("a_q_hi"), K.sem("a_q_lo")
        sc, mx, ex, rc, nr = K.sem("a_sc"), K.sem("a_mx"), K.sem("a_ex"), K.sem("a_rc"), K.sem("a_nr")
        pt, p_hi, p_lo = K.sem("a_pt"), K.sem("a_p_hi"), K.sem("a_p_lo")
        pv, o_hi, o_lo = K.sem("a_pv"), K.sem("a_o_hi"), K.sem("a_o_lo")
        ot, ac, acc_out, zero = K.sem("a_ot"), K.sem("a_ac"), K.sem("a_acc_out"), K.sem("a_zero")
        score = [psS[:, 0, 0:2 * P], psS[:, 0, 2 * P:4 * P], psS[:, 1, 0:3 * P], psS[:, 2, :]]
        groups = [(psT[:, 0], slice(0, 4 * P), [(0, 0)]),
                  (psT[:, 1], slice(OFF[3], OFF[3] + 4 * P), [(3, 0), (1, P)]),
                  (psX[:, 0:2 * P], slice(OFF[2], OFF[2] + 2 * P), [(2, 0)])]

        with nc.Block() as block:

            @block.sync
            def _(sp):
                def load_w(g, u):
                    sp.dma_start(wqk[:, u].rearrange("p s c n -> p (s c n)").bitcast(F32),
                                 K.wqk_d[bass.ds(g % H, 1)].rearrange("a p s c n -> p (a s c n)")).then_inc(w_in[u], 16)

                def load_q(g, u):
                    sp.dma_start(qpe[:, u].bitcast(F32), K.qpe_d.rearrange("b h p n -> (b h) p n")[bass.ds(g, 1)]
                                 .rearrange("a p n -> p (a n)")).then_inc(q_in[u], 16)

                for u in range(2):
                    load_w(u, u)
                    load_q(u, u)
                with sp.Fori(0, B * PAIRS - 1) as n:
                    for u in range(2):
                        g = n * 2 + u
                        sp.wait_ge(qp, g + 1)
                        load_w(g + 2, u)
                        sp.wait_ge(sc, g * 4 + 4)
                        load_q(g + 2, u)

            @block.gpsimd
            def _(pool):
                def load(b):
                    s = b % 2
                    pool.dma_start(hT[:, s].rearrange("p c s n -> p (c s n)").bitcast(F32),
                                   K.hT_d[b].rearrange("p c s n -> p (c s n)")).then_inc(b_in[s], 16)
                    pool.dma_start(cT[:, s].rearrange("p s n -> p (s n)").bitcast(F32),
                                   K.cT_d[b].rearrange("p s n -> p (s n)")).then_inc(b_in[s], 16)
                    pool.dma_start(kpe[:, s].rearrange("p s n -> p (s n)").bitcast(F32),
                                   K.kpe_d[b].rearrange("p s n -> p (s n)")).then_inc(b_in[s], 16)

                def load_c(b):
                    pool.dma_start(cv[:, :, :, :].rearrange("p t s n -> p (t s n)").bitcast(F32),
                                   K.c_d[b].rearrange("p t s n -> p (t s n)")).then_inc(c_in, 16)

                load(0)
                load_c(0)
                load(1)
                for b in range(B):
                    if b:
                        pool.wait_ge(pv, H * b)
                        load_c(b)
                        if b + 1 < B:
                            pool.wait_ge(qp, H * b)
                            pool.wait_ge(sc, 4 * H * b)
                            load(b + 1)
                    pool.wait_ge(c_in, 16 * (b + 1))
                    pool.wait_ge(b_in[b % 2], 48 * (b // 2 + 1))
                    pool.sem_inc(landed, 1)

            @block.scalar
            def _(act):
                act.sem_inc(acc_out, 16)

                def exps(g):
                    for i in range(TB):
                        act.wait_ge(mx, g * 4 + max(i + 1, 2))
                        w = (i + 1) * P
                        nc.scalar.activation(pr[:, i, 0:w], score[i][:, 0:w], ACT.Exp, bias=nmax[:, i:i + 1],
                                             accum_out=rsum[:, i:i + 1]).then_inc(ex, 1)

                def q_high(g):
                    act.wait_ge(qp, g + 1)
                    nc.scalar.activation(qT[:, 0], psX[:, :], ACT.Copy, scale=SCALE).then_inc(q_hi, 1)

                def o_high(g, n, u):
                    act.wait_ge(pv, g + 1)
                    act.wait_ge(ot, n * 4 + 1)
                    nc.scalar.activation(oT[:, u, 0], psY[:, :], ACT.Copy).then_inc(o_hi, 1)

                def p_high(g):
                    for k, (src, dst, _) in enumerate(groups):
                        act.wait_ge(pt, g * 3 + k + 1)
                        nc.scalar.activation(pT[:, 0, dst], src, ACT.Copy).then_inc(p_hi, 1)

                def pair(b, i, first, last):
                    n = b * PAIRS + i
                    for u in range(2):
                        g = n * 2 + u
                        exps(g)
                        if not (last and u):
                            q_high(g + 1)
                        if not (first and not u):
                            o_high(g - 1, n - 1 if not u else n, 1 - u)
                        p_high(g)

                with act.Fori(0, B) as b:
                    q_high(b * H)
                    pair(b, 0, True, False)
                    with act.Fori(1, PAIRS - 1) as i:
                        pair(b, i, False, False)
                    pair(b, PAIRS - 1, False, True)
                    o_high(b * H + H - 1, b * PAIRS + PAIRS - 1, 1)
                    act.wait_ge(ac, b * (PAIRS * TB) + PAIRS * TB + 1)
                    act.dma_start(K.attn_d[bass.ds(b * TB, TB)].rearrange("t p n -> p t n"),
                                  acc[:, :, :]).then_inc(acc_out, 16)
                act.wait_ge(acc_out, 16 * B + 16)

            @block.vector
            def _(dve):
                for credit in (o_lo, p_lo, ac):
                    dve.sem_inc(credit, 1)
                for s in range(2):
                    nc.vector.memset(pT[:, s, ZERO:ZERO + P].bitcast(U32), 0).then_inc(zero, 1)

                def softmax(g):
                    for i in range(TB):
                        dve.wait_ge(sc, g * 4 + max(i + 1, 2))
                        nc.vector.tensor_reduce(nmax[:, i:i + 1], score[i][:, 0:(i + 1) * P], AX.X, ALU.max,
                                                negate=True).then_inc(mx, 1)
                    dve.wait_ge(ex, g * 4 + 4)
                    nc.vector.reciprocal(rinv[:, :], rsum[:, :]).then_inc(rc, 1)
                    dve.wait_ge(rc, g + 1)
                    for i in range(TB):
                        w = (i + 1) * P
                        nc.vector.tensor_scalar(pr[:, i, 0:w], pr[:, i, 0:w], rinv[:, i:i + 1], None, ALU.mult).then_inc(nr, 1)

                def q_low(g):
                    dve.wait_ge(q_hi, g + 1)
                    nc.vector.scalar_tensor_tensor(out=qT[:, 1], in0=psX[:, :], scalar=SCALE, in1=qT[:, 0].bitcast(F32),
                                                   op0=ALU.mult, op1=ALU.subtract).then_inc(q_lo, 1)

                def o_low(g, u):
                    dve.wait_ge(o_hi, g + 1)
                    nc.vector.tensor_tensor(oT[:, u, 1], psY[:, :], oT[:, u, 0].bitcast(F32), ALU.subtract).then_inc(o_lo, 1)

                def p_low(g):
                    for k, (src, dst, _) in enumerate(groups):
                        dve.wait_ge(p_hi, g * 3 + k + 1)
                        nc.vector.tensor_tensor(pT[:, 1, dst], src, pT[:, 0, dst].bitcast(F32), ALU.subtract).then_inc(p_lo, 1)

                def add_out(b, n, t, first):
                    dve.wait_ge(ot, n * 4 + t + 2)
                    part = acc[:, t]
                    if first:
                        nc.vector.tensor_copy(part, psZ[:, :]).then_inc(ac, 1)
                    else:
                        dve.wait_ge(ac, n * 4 + t - 2)
                        nc.vector.tensor_tensor(part, psZ[:, :], part, ALU.add).then_inc(ac, 1)

                def pair(b, i, first, last, second=False):
                    n = b * PAIRS + i
                    for u in range(2):
                        g = n * 2 + u
                        softmax(g)
                        if u and not first:
                            add_out(b, n - 1, 1, second)
                        if not (last and u):
                            q_low(g + 1)
                        if u and not first:
                            add_out(b, n - 1, 2, second)
                            add_out(b, n - 1, 3, second)
                        if not (first and not u):
                            o_low(g - 1, 1 - u)
                        p_low(g)
                        if not u and not first:
                            add_out(b, n - 1, 0, second)

                with dve.Fori(0, B) as b:
                    q_low(b * H)
                    pair(b, 0, True, False)
                    dve.wait_ge(acc_out, b * 16 + 16)
                    pair(b, 1, False, False, True)
                    with dve.Fori(2, PAIRS - 1) as i:
                        pair(b, i, False, False)
                    pair(b, PAIRS - 1, False, True)
                    o_low(b * H + H - 1, 1)
                    for t in range(TB):
                        add_out(b, b * PAIRS + PAIRS - 1, t, False)

            @block.tensor
            def _(pe):
                def qproj(b, g, u, transposed):
                    pe.wait_ge(w_in[u], (g // 2) * 16 + 16)
                    pe.wait_ge(p_lo, transposed * 3 + 1)
                    h_ = lambda c, s: hT[:, bass.ds(b % 2, 1), c, s].rearrange("p a n -> p (a n)")
                    split3(nc, psX[:, :], [(wqk[:, u, 0, c], wqk[:, u, 1, c], h_(c, 0), h_(c, 1))
                                           for c in range(DC)]).then_inc(qp, 1)

                def scores(b, g, u):
                    pe.wait_ge(q_lo, g + 1)
                    pe.wait_ge(q_in[u], (g // 2) * 16 + 16)
                    for i in range(TB):
                        w = max(i + 1, 2) * P
                        q = slice(i * P, (i + 1) * P)
                        out = score[i][:, 0:w]
                        k_ = lambda src, s: src[:, bass.ds(b % 2, 1), s, 0:w].rearrange("p a n -> p (a n)")
                        nc.tensor.matmul(out, qT[:, 0, q], k_(cT, 0), start=True, stop=False)
                        nc.tensor.matmul(out, qT[:, 0, q], k_(cT, 1), start=False, stop=False)
                        nc.tensor.matmul(out, qT[:, 1, q], k_(cT, 0), start=False, stop=False)
                        nc.tensor.matmul(out, qpe[:, u, q], k_(kpe, 0), start=False, stop=False)
                        nc.tensor.matmul(out, qpe[:, u, q], k_(kpe, 1), start=False, stop=False)
                        nc.tensor.matmul(out[:, q], K.identb[:, :], K.maskb[:, :], start=False, stop=True).then_inc(sc, 1)

                def values(g):
                    pe.wait_ge(p_lo, g * 3 + 4)
                    pe.wait_ge(o_lo, g + 1)
                    n = 0
                    for j in range(TB):
                        q0 = min(j, 2) * P
                        o = OFF[j] - (j * P - q0)
                        w = S - q0
                        for cs, ps in ((0, 0), (0, 1), (1, 0)):
                            m = nc.tensor.matmul(psY[:, q0:S], cv[:, j, cs], pT[:, ps, o:o + w], start=n == 0, stop=n == 11)
                            n += 1
                    m.then_inc(pv, 1)

                def transposes(g):
                    pe.wait_ge(nr, g * 4 + 4)
                    for k, (dst, _, parts) in enumerate(groups):
                        for j, o in parts:
                            for i in range(j, TB):
                                m = nc.tensor.transpose(dst[:, o + (i - j) * P:o + (i - j + 1) * P],
                                                        pr[:, i, j * P:(j + 1) * P], K.ident[:, :])
                        m.then_inc(pt, 1)

                def output(n, i, t):
                    pe.wait_ge(o_lo, n * 2 + 3)
                    pe.wait_ge(ac, n * 4 + t + 1)
                    q = slice(t * P, (t + 1) * P)
                    M_ = lambda u, s: Mhl[:, bass.ds(i * 2 + u, 1), s].rearrange("p a n -> p (a n)")
                    split3(nc, psZ[:, :], [(oT[:, u, 0, q], oT[:, u, 1, q], M_(u, 0), M_(u, 1))
                                           for u in range(2)]).then_inc(ot, 1)

                def pair(b, i, first, last):
                    n = b * PAIRS + i
                    for u in range(2):
                        g = n * 2 + u
                        scores(b, g, u)
                        if u and not first:
                            output(n - 1, i - 1, 1)
                        if not (last and u):
                            qproj(b, g + 1, 1 - u, g)
                        if u and not first:
                            output(n - 1, i - 1, 2)
                        if not (first and not u):
                            values(g - 1)
                        if u and not first:
                            output(n - 1, i - 1, 3)
                        if not (last and u):
                            pe.wait_ge(q_lo, g + 2)
                        transposes(g)
                        if not u and not first:
                            output(n - 1, i - 1, 0)

                pe.wait_ge(zero, 2)
                pe.sem_inc(ot, 1)
                with pe.Fori(0, B) as b:
                    pe.wait_ge(landed, b + 1)
                    qproj(b, b * H, 0, b * H)
                    pair(b, 0, True, False)
                    with pe.Fori(1, PAIRS - 1) as i:
                        pair(b, i, False, False)
                    pair(b, PAIRS - 1, False, True)
                    values(b * H + H - 1)
                    for t in range(TB):
                        output(b * PAIRS + PAIRS - 1, PAIRS - 1, t)


def stage_shared(K, M):
    nc = K.nc
    with ExitStack() as ctx:
        sb = lambda n, s, d: K.sb(n, s, d, ctx)
        st1 = sb("s_st1", [P, DC, 2, F], F32)
        st2 = sb("s_st2", [P, FC, D], F32)
        w1 = sb("s_w1", [P, SH, DC, 2, 2 * F], F32R)
        w2 = sb("s_w2", [P, SH, FC, 2, D], F32R)
        b1 = sb("s_b1", [P, SH, 2 * F], F32)
        b2 = sb("s_b2", [P, SH, D], F32)
        wa = sb("s_wa", [P, DC, E], F32)
        half = sb("s_half", [P, 1], F32)
        x = sb("s_x", [P, 2, D], F32)
        at = sb("s_at", [P, 2, D], F32)
        x1 = sb("s_x1", [P, 2, D], F32)
        h2 = sb("s_h2", [P, 2, D], F32)
        st = sb("s_st", [P, 2, 6], F32)
        mv = sb("s_mv", [P, 2, 4], F32)
        hf = sb("s_hf", [P, 2, D], F32)
        hT = sb("s_hT", [P, 2, 2, D], F32R)
        z = sb("s_z", [P, 2, 2 * F], F32)
        y = sb("s_y", [P, 2, F], F32)
        yT = sb("s_yT", [P, 2, 2, F], F32R)
        so = sb("s_so", [P, 2, D], F32)
        px = K.ps("s_px", [P, D], F32, ctx)
        pg = K.ps("s_pg", [P, 2, 2 * F], F32, ctx)
        py = K.ps("s_py", [P, 2, 512], F32, ctx)
        po = K.ps("s_po", [P, 2, D], F32, ctx)
        pl = K.ps("s_pl", [P, 512], F32, ctx)
        w_in, w_hi, w_lo, c_in = K.sem("s_w_in"), K.sem("s_w_hi"), K.sem("s_w_lo"), K.sem("s_c_in")
        x_in = [K.sem("s_x_in0"), K.sem("s_x_in1")]
        h_out = [K.sem("s_h_out0"), K.sem("s_h_out1")]
        step_v, step_p = K.sem("s_step_v"), K.sem("s_step_p")
        dch, pch, b2_ok = K.sem("s_dch"), K.sem("s_pch"), K.sem("s_b2_ok")
        var_ok, rstd, xn, x_used = K.sem("s_var_ok"), K.sem("s_rstd"), K.sem("s_xn"), K.sem("s_x_used")
        h2_ok, tr, h_hi, h_lo = K.sem("s_h2_ok"), K.sem("s_tr"), K.sem("s_h_hi"), K.sem("s_h_lo")
        lg, lg_ok = K.sem("s_lg"), K.sem("s_lg_ok")
        gu, z_ok, ge, y_ok = K.sem("s_gu"), K.sem("s_z_ok"), K.sem("s_ge"), K.sem("s_y_ok")
        yt, y_hi, y_lo, oo, so_ok, base_ok = (K.sem("s_yt"), K.sem("s_y_hi"), K.sem("s_y_lo"), K.sem("s_oo"),
                                              K.sem("s_so_ok"), K.sem("s_base_ok"))

        with nc.Block() as block:

            @block.sync
            def _(sp):
                for b in range(B):
                    sp.dma_start(M.rows[:, b].rearrange("p v n -> p (v n)"),
                                 K.mod_d[b:b + 1, 2 * D:6 * D].broadcast_to([P, 4 * D])).then_inc(c_in, 16)
                sp.dma_start(wa[:, :, :], K.ins["L0_ffn_wa"].rearrange("(c p) e -> p c e", p=P)).then_inc(c_in, 16)
                for e in range(SH):
                    for n, bias in enumerate((K.ins["L0_ffn_sgb"], K.ins["L0_ffn_sb1"])):
                        sp.dma_start(b1[:, e, n * F:(n + 1) * F], bias[e:e + 1, :].broadcast_to([P, F])).then_inc(c_in, 16)
                    sp.dma_start(b2[:, e], K.ins["L0_ffn_sb2"][e:e + 1, :].broadcast_to([P, D])).then_inc(c_in, 16)
                xv = K.ins["L0_attn_x"].rearrange("b (t p) n -> (b t) p n", p=P)

                def load(t, u):
                    sp.dma_start(x[:, u], xv[bass.ds(t, 1)].rearrange("a p n -> p (a n)")).then_inc(x_in[u], 16)
                    sp.dma_start(at[:, u], K.attn_d[bass.ds(t, 1)].rearrange("a p n -> p (a n)")).then_inc(x_in[u], 16)

                load(0, 0)
                load(1, 1)
                for e in range(SH):
                    if e:
                        sp.wait_ge(w_lo, 2 * e)
                    sp.dma_start(st1[:, :, 0], K.ins["L0_ffn_sg"][e].rearrange("(c p) f -> p c f", p=P)).then_inc(w_in, 16)
                    sp.dma_start(st1[:, :, 1], K.ins["L0_ffn_sw1"][e].rearrange("(c p) f -> p c f", p=P)).then_inc(w_in, 16)
                    sp.dma_start(st2[:, :, :], K.ins["L0_ffn_sw2"][e].rearrange("(c p) n -> p c n", p=P)).then_inc(w_in, 16)

                def tiles(j, more):
                    for u in range(2):
                        t = j * 2 + u
                        if more:
                            sp.wait_ge(x_used, t + 1)
                            load(t + 2, u)
                        sp.wait_ge(h2_ok, t + 1)
                        sp.dma_start(K.h2_d[bass.ds(t * P, P), :], h2[:, u]).then_inc(h_out[u], 16)

                with sp.Fori(0, NT // 2 - 1) as j:
                    tiles(j, True)
                tiles(NT // 2 - 1, False)
                for u in range(2):
                    sp.wait_ge(h_out[u], 16 * (NT // 2))

            @block.gpsimd
            def _(pool):
                nc.gpsimd.memset(half[:, :], -0.5).then_inc(pch, 1)
                pool.wait_ge(pch, 1)
                pool.wait_ge(c_in, 16 * (B + 1 + 3 * SH))
                nc.gpsimd.tensor_tensor(b2[:, 0], b2[:, 0], b2[:, 1], ALU.add).then_inc(b2_ok, 1)

                def scale(b, t, u):
                    pool.wait_ge(var_ok, t + 1)
                    nc.gpsimd.tensor_tensor(mv[:, u, 3:4], mv[:, u, 2:3], half[:, :], ALU.pow).then_inc(rstd, 1)
                    pool.wait_ge(xn, t + 1)
                    pool.sem_inc(step_p, 1)
                    row = lambda v: M.rows[:, bass.ds(b, 1), v].rearrange("p a n -> p (a n)")
                    nc.gpsimd.tensor_tensor(h2[:, u], h2[:, u], row(2), ALU.mult).then_inc(pch, 1)
                    pool.wait_ge(pch, t + 2)
                    pool.sem_inc(step_p, 1)
                    nc.gpsimd.tensor_tensor(h2[:, u], h2[:, u], row(1), ALU.add).then_inc(h2_ok, 1)

                def base(b, t, u):
                    row = M.rows[:, bass.ds(b, 1), 3].rearrange("p a n -> p (a n)")
                    bt = M.base[:, bass.ds(t, 1)].rearrange("p a n -> p (a n)")
                    pool.wait_ge(so_ok, t + 1)
                    pool.sem_inc(step_p, 1)
                    nc.gpsimd.tensor_tensor(so[:, u], so[:, u], h2[:, u], ALU.add).then_inc(base_ok, 1)
                    pool.wait_ge(base_ok, t * 3 + 1)
                    pool.sem_inc(step_p, 1)
                    nc.gpsimd.tensor_tensor(so[:, u], so[:, u], row, ALU.mult).then_inc(base_ok, 1)
                    pool.wait_ge(base_ok, t * 3 + 2)
                    pool.sem_inc(step_p, 1)
                    nc.gpsimd.tensor_tensor(bt, so[:, u], x1[:, u], ALU.add).then_inc(base_ok, 1)

                def tiles(j, more):
                    for u in range(2):
                        t = j * 2 + u
                        if more or not u:
                            scale((t + 1) // TB, t + 1, 1 - u)
                        base(j // 2, t, u)

                scale(0, 0, 0)
                with pool.Fori(0, NT // 2 - 1) as j:
                    tiles(j, True)
                tiles(NT // 2 - 1, False)

            @block.scalar
            def _(act):
                for e in range(SH):
                    act.wait_ge(w_in, 48 * (e + 1))
                    nc.scalar.activation(w1[:, e, :, 0].rearrange("p c (a f) -> p c a f", a=2), st1[:, :, :, :], ACT.Copy).then_inc(w_hi, 1)
                    nc.scalar.activation(w2[:, e, :, 0], st2[:, :, :], ACT.Copy).then_inc(w_hi, 1)

                def h_high(t, u):
                    act.wait_ge(tr, t + 1)
                    nc.scalar.activation(hf[:, u], px[:, :], ACT.Copy)
                    nc.scalar.activation(hT[:, u, 0], px[:, :], ACT.Copy).then_inc(h_hi, 1)

                def logits(t):
                    act.wait_ge(lg, t + 1)
                    nc.scalar.activation(M.aff[:, bass.ds(t, 1)].rearrange("p a e -> p (a e)"), pl[:, 0:E], ACT.Copy).then_inc(lg_ok, 1)

                def gelu(t, e):
                    act.wait_ge(z_ok, t * 2 + e + 1)
                    nc.scalar.activation(y[:, e], z[:, e, 0:F], ACT.Gelu).then_inc(ge, 1)

                def y_high(t, e):
                    act.wait_ge(yt, t * 2 + e + 1)
                    nc.scalar.activation(yT[:, e, 0], py[:, e, 0:F], ACT.Copy).then_inc(y_hi, 1)

                def tiles(j, more):
                    for u in range(2):
                        t = j * 2 + u
                        gelu(t, 0)
                        gelu(t, 1)
                        y_high(t, 0)
                        if more or not u:
                            h_high(t + 1, 1 - u)
                        y_high(t, 1)
                        if more or not u:
                            logits(t + 1)

                h_high(0, 0)
                logits(0)
                with act.Fori(0, NT // 2 - 1) as j:
                    tiles(j, True)
                tiles(NT // 2 - 1, False)

            @block.vector
            def _(dve):
                for e in range(SH):
                    dve.wait_ge(w_hi, 2 * e + 1)
                    nc.vector.tensor_tensor(w1[:, e, :, 1].rearrange("p c (a f) -> p c a f", a=2), st1[:, :, :, :],
                                            w1[:, e, :, 0].rearrange("p c (a f) -> p c a f", a=2).bitcast(F32),
                                            ALU.subtract).then_inc(w_lo, 1)
                    dve.wait_ge(w_hi, 2 * e + 2)
                    nc.vector.tensor_tensor(w2[:, e, :, 1], st2[:, :, :], w2[:, e, :, 0].bitcast(F32), ALU.subtract).then_inc(w_lo, 1)

                def norm(b, t, u, slot_loads, former):
                    ch = Chain(dve, dch, t * 4)
                    dve.wait_ge(x_in[u], slot_loads * 32)
                    row = M.rows[:, bass.ds(b, 1), 0].rearrange("p a n -> p (a n)")
                    ch.after(nc.vector.tensor_tensor(at[:, u], at[:, u], row, ALU.mult))
                    if former is not None:
                        dve.wait_ge(base_ok, former * 3 + 3)
                    nc.vector.tensor_tensor(x1[:, u], x[:, u], at[:, u], ALU.add).then_inc(x_used, 1)
                    dve.wait_ge(x_used, t + 1)
                    nc.vector.bn_stats(st[:, u], x1[:, u]).then_inc(ch.sem, 1)
                    ch.wait()
                    dve.sem_inc(step_v, 1)
                    ch.after(nc.vector.bn_aggr(mv[:, u, 0:2], st[:, u]))
                    nc.vector.tensor_scalar(mv[:, u, 2:3], mv[:, u, 1:2], EPS, None, ALU.add).then_inc(var_ok, 1)
                    dve.wait_ge(rstd, t + 1)
                    dve.wait_ge(h_out[u], (slot_loads - 1) * 16)
                    nc.vector.tensor_scalar(h2[:, u], x1[:, u], mv[:, u, 0:1], mv[:, u, 3:4], ALU.subtract, ALU.mult).then_inc(xn, 1)
                    dve.wait_ge(xn, t + 1)
                    ch.after(nc.vector.tensor_copy(mv[:, u, 2:3], mv[:, u, 1:2]))
                    assert ch.n == 4

                def h_low(t, u):
                    dve.wait_ge(h_hi, t + 1)
                    nc.vector.tensor_tensor(hT[:, u, 1], px[:, :], hT[:, u, 0].bitcast(F32), ALU.subtract).then_inc(h_lo, 1)

                def bias(t, e):
                    dve.wait_ge(gu, t * 2 + e + 1)
                    nc.vector.tensor_tensor(z[:, e], pg[:, e], b1[:, e], ALU.add).then_inc(z_ok, 1)

                def gate(t, e):
                    dve.wait_ge(ge, t * 2 + e + 1)
                    nc.vector.tensor_tensor(y[:, e], y[:, e], z[:, e, F:2 * F], ALU.mult).then_inc(y_ok, 1)

                def y_low(t, e):
                    dve.wait_ge(y_hi, t * 2 + e + 1)
                    nc.vector.tensor_tensor(yT[:, e, 1], py[:, e, 0:F], yT[:, e, 0].bitcast(F32), ALU.subtract).then_inc(y_lo, 1)

                def tiles(j, more, fresh=False):
                    for u in range(2):
                        t = j * 2 + u
                        if more or not u:
                            norm((t + 1) // TB, t + 1, 1 - u, j + 1 + u, None if fresh and not u else t - 1)
                        bias(t, 0)
                        gate(t, 0)
                        bias(t, 1)
                        gate(t, 1)
                        y_low(t, 0)
                        if more or not u:
                            h_low(t + 1, 1 - u)
                        y_low(t, 1)
                        dve.wait_ge(oo, t + 1)
                        nc.vector.tensor_tensor(so[:, u], po[:, u], b2[:, 0], ALU.add).then_inc(so_ok, 1)

                dve.wait_ge(c_in, 16 * (B + 1 + 3 * SH))
                dve.wait_ge(b2_ok, 1)
                norm(0, 0, 0, 1, None)
                h_low(0, 0)
                tiles(0, True, True)
                with dve.Fori(1, NT // 2 - 1) as j:
                    tiles(j, True)
                tiles(NT // 2 - 1, False)

            @block.tensor
            def _(pe):
                def transposes(t, u):
                    pe.wait_ge(h2_ok, t + 1)
                    for c in range(DC):
                        m = nc.tensor.transpose(px[:, c * P:(c + 1) * P], h2[:, u, c * P:(c + 1) * P], K.ident[:, :])
                    m.then_inc(tr, 1)

                def router(t, u):
                    pe.wait_ge(h_hi, t + 1)
                    pe.wait_ge(lg_ok, t)
                    for c in range(DC):
                        m = nc.tensor.matmul(pl[:, 0:E], hf[:, u, c * P:(c + 1) * P], wa[:, c], start=c == 0, stop=c == DC - 1)
                    m.then_inc(lg, 1)

                def first(t, u, e):
                    pe.wait_ge(h_lo, t + 1)
                    c_ = lambda c: slice(c * P, (c + 1) * P)
                    split3(nc, pg[:, e], [(hT[:, u, 0, c_(c)], hT[:, u, 1, c_(c)], w1[:, e, c, 0], w1[:, e, c, 1])
                                          for c in range(DC)]).then_inc(gu, 1)

                def y_trans(t, e):
                    pe.wait_ge(y_ok, t * 2 + e + 1)
                    for c in range(FC):
                        m = nc.tensor.transpose(py[:, e, c * P:(c + 1) * P], y[:, e, c * P:(c + 1) * P], K.ident[:, :])
                    m.then_inc(yt, 1)

                def second(t, u, e):
                    pe.wait_ge(y_lo, t * 2 + e + 1)
                    n = 0
                    for c in range(FC):
                        for s, w in ((0, 0), (0, 1), (1, 0)):
                            m = nc.tensor.matmul(po[:, u], yT[:, e, s, c * P:(c + 1) * P], w2[:, e, c, w],
                                                 start=e == 0 and n == 0, stop=e == SH - 1 and n == 3 * FC - 1)
                            n += 1
                    if e == SH - 1:
                        m.then_inc(oo, 1)

                def tiles(j, more):
                    for u in range(2):
                        t = j * 2 + u
                        first(t, u, 0)
                        first(t, u, 1)
                        y_trans(t, 0)
                        if more or not u:
                            transposes(t + 1, 1 - u)
                        second(t, u, 0)
                        y_trans(t, 1)
                        if more or not u:
                            router(t + 1, 1 - u)
                        second(t, u, 1)

                pe.wait_ge(c_in, 16 * (B + 1 + 3 * SH))
                pe.wait_ge(w_lo, 2 * SH)
                transposes(0, 0)
                router(0, 0)
                with pe.Fori(0, NT // 2 - 1) as j:
                    tiles(j, True)
                tiles(NT // 2 - 1, False)


def stage_route(K, M):
    nc = K.nc
    NS = E + E * E + NBLK
    with ExitStack() as ctx:
        sb = lambda n, s, d: K.sb(n, s, d, ctx)
        small = sb("r_small", [P, NS], F32)
        tok = sb("r_tok", [P, NT], I32)
        trif = sb("r_trif", [P, P], F32)
        tri = sb("r_tri", [P, P], BF16)
        ones = sb("r_ones", [P, P], BF16)
        zeros = sb("r_zeros", [P, NBLK * PB // P], I32)
        wide = lambda n: sb(n, [P, NT, E], F32)
        af, oh1, oh2, t1, rank = wide("r_af"), wide("r_oh1"), wide("r_oh2"), wide("r_t1"), wide("r_rank")
        mb = sb("r_mb", [P, NT, E], BF16)
        m1, m2, mt = sb("r_m1", [P, NT], F32), sb("r_m2", [P, NT], F32), sb("r_mt", [P, NT], F32)
        cnt, cnti = sb("r_cnt", [P, E], F32), sb("r_cnti", [P, 2, E], I32)
        nb, first, base = sb("r_nb", [P, E], F32), sb("r_first", [P, E], F32), sb("r_base", [P, E], F32)
        tt = sb("r_tt", [P, E, E], F32)
        cmp = sb("r_cmp", [P, NBLK, E], F32)
        bef = sb("r_bef", [P, NBLK], F32)
        pr = K.ps("r_pr", [P, NT * E], F32, ctx)
        pn = K.ps("r_pn", [P, 512], F32, ctx)
        c_in, z_out, sc_out = K.sem("r_c_in"), K.sem("r_z_out"), K.sem("r_sc_out")
        dch, sig, mb_ok, ranks, zero = K.sem("r_dch"), K.sem("r_sig"), K.sem("r_mb_ok"), K.sem("r_ranks"), K.sem("r_zero")
        pos_ok = K.sem("r_pos_ok")
        rev = small[:, 0:E]
        before = small[:, E:E + E * E].rearrange("p (e f) -> p e f", f=E)
        blk = small[:, E + E * E:NS]

        with nc.Block() as block:

            @block.sync
            def _(sp):
                sp.dma_start(small[:, :], K.ins["c_small"].broadcast_to([P, NS])).then_inc(c_in, 16)
                sp.dma_start(tok[:, :], K.ins["c_tok"]).then_inc(c_in, 16)
                sp.dma_start(trif[:, :], K.ins["c_const"][2]).then_inc(c_in, 16)
                sp.wait_ge(zero, 1)
                sp.dma_start(K.idx_d.rearrange("(p k) o -> p (k o)", p=P), zeros[:, :]).then_inc(z_out, 16)

            @block.scalar
            def _(act):
                nc.scalar.activation(af[:, :, :], M.aff[:, :, :], ACT.Sigmoid).then_inc(sig, 1)

            @block.gpsimd
            def _(pool):
                nc.gpsimd.memset(zeros[:, :], 0).then_inc(zero, 1)
                nc.gpsimd.memset(ones[:, :], 1.0).then_inc(zero, 1)
                pool.wait_ge(c_in, 48)
                pool.wait_ge(z_out, 16)
                pool.wait_ge(pos_ok, 1)
                for t in range(NT):
                    for k in range(TOP):
                        pool.indirect_dma_start(
                            out=K.idx_d, out_offset=bass.IndirectOffsetOnAxis(ap=M.pos[:, k, t:t + 1], axis=0),
                            in_=tok[:, t:t + 1], in_offset=None).then_inc(sc_out, 16)
                pool.wait_ge(sc_out, 16 * NT * TOP)

            @block.vector
            def _(dve):
                ch = Chain(dve, dch)
                dve.wait_ge(c_in, 48)
                dve.wait_ge(sig, 1)
                over = lambda a: a.unsqueeze(2).broadcast_to([P, NT, E])
                under = lambda a: a.unsqueeze(1).broadcast_to([P, NT, E])
                tt_, v = nc.vector.tensor_tensor, nc.vector
                ch.after(v.tensor_copy(tri[:, :], trif[:, :]))
                for m, oh in ((m1, oh1), (m2, oh2)):
                    ch.after(v.tensor_reduce(m[:, :], af[:, :, :], AX.X, ALU.max))
                    ch.after(tt_(t1[:, :, :], af[:, :, :], over(m[:, :]), ALU.is_equal))
                    ch.after(tt_(t1[:, :, :], t1[:, :, :], under(rev), ALU.mult))
                    ch.after(v.tensor_reduce(mt[:, :], t1[:, :, :], AX.X, ALU.max))
                    ch.after(tt_(oh[:, :, :], t1[:, :, :], over(mt[:, :]), ALU.is_equal))
                    if oh is oh1:
                        ch.after(v.scalar_tensor_tensor(out=af[:, :, :].rearrange("p t e -> p (t e)"),
                                                        in0=oh[:, :, :].rearrange("p t e -> p (t e)"), scalar=-2.0,
                                                        in1=af[:, :, :].rearrange("p t e -> p (t e)"),
                                                        op0=ALU.mult, op1=ALU.add))
                tt_(mb[:, :, :], oh1[:, :, :], oh2[:, :, :], ALU.add).then_inc(mb_ok, 1)
                ch.after(tt_(mt[:, :], m1[:, :], m2[:, :], ALU.add))
                ch.after(v.reciprocal(mt[:, :], mt[:, :]))
                ch.after(tt_(M.wt[:, 0], m1[:, :], mt[:, :], ALU.mult))
                ch.after(tt_(M.wt[:, 1], m2[:, :], mt[:, :], ALU.mult))
                ch.after(tt_(M.cmb[:, :, :], oh1[:, :, :], over(M.wt[:, 0]), ALU.mult))
                ch.after(tt_(t1[:, :, :], oh2[:, :, :], over(M.wt[:, 1]), ALU.mult))
                ch.after(tt_(M.cmb[:, :, :], M.cmb[:, :, :], t1[:, :, :], ALU.add))
                dve.wait_ge(ranks, 1)
                ch.after(v.tensor_scalar(cnti[:, 0], pn[:, 0:E], float(PB - 1), None, ALU.add))
                ch.after(v.tensor_scalar(cnti[:, 1], cnti[:, 0], PB.bit_length() - 1, None, ALU.logical_shift_right))
                ch.after(v.tensor_copy(nb[:, :], cnti[:, 1]))
                ch.after(tt_(tt[:, :, :], before, nb[:, :].unsqueeze(1).broadcast_to([P, E, E]), ALU.mult))
                ch.after(v.tensor_reduce(first[:, :], tt[:, :, :], AX.X, ALU.add))
                ch.after(v.tensor_scalar(base[:, :], first[:, :], float(PB), None, ALU.mult))
                ch.after(tt_(rank[:, :, :], pr[:, :].rearrange("p (t e) -> p t e", e=E), under(base[:, :]), ALU.add))
                for k, oh in enumerate((oh1, oh2)):
                    ch.after(tt_(t1[:, :, :], rank[:, :, :], oh[:, :, :], ALU.mult))
                    ch.after(v.tensor_reduce(mt[:, :], t1[:, :, :], AX.X, ALU.add))
                    ch.after(v.tensor_copy(M.pos[:, k], mt[:, :]))
                ch.after(tt_(first[:, :], first[:, :], nb[:, :], ALU.add))
                v.tensor_scalar(m1[:, :], m1[:, :], 1.0, None, ALU.mult).then_inc(pos_ok, 1)
                ch.after(tt_(cmp[:, :, :], first[:, :].unsqueeze(1).broadcast_to([P, NBLK, E]),
                             blk.unsqueeze(2).broadcast_to([P, NBLK, E]), ALU.is_le))
                ch.after(v.tensor_reduce(bef[:, :], cmp[:, :, :], AX.X, ALU.add))
                ch.after(v.tensor_scalar(M.be[:, :], bef[:, :], float(E - 1), None, ALU.min))

            @block.tensor
            def _(pe):
                pe.wait_ge(mb_ok, 1)
                pe.wait_ge(zero, 2)
                nc.tensor.matmul(pr[:, :], tri[:, :], mb[:, :, :].rearrange("p t e -> p (t e)"), start=True, stop=False)
                for t in range(NT - 1):
                    nc.tensor.matmul(pr[:, (t + 1) * E:].rearrange("p (t e) -> p t e", e=E), ones[:, :],
                                     mb[:, t:t + 1].broadcast_to([P, NT - 1 - t, E]), start=False, stop=t == NT - 2)
                for t in range(NT):
                    m = nc.tensor.matmul(pn[:, 0:E], ones[:, :], mb[:, t], start=t == 0, stop=t == NT - 1)
                m.then_inc(ranks, 1)


def stage_routed(K, M):
    nc = K.nc
    LB = NBLK // 2
    PT = PB // P
    PW = 2
    NF = 2 * FC
    with ExitStack() as ctx:
        sb = lambda n, s, d: K.sb(n, s, d, ctx)
        st1 = sb("e_st1", [P, 2, DC, 2, F], F32)
        st2 = sb("e_st2", [P, 2, FC, D], F32)
        w1 = sb("e_w1", [P, 2, DC, 2, 2 * F], F32R)
        w2 = sb("e_w2", [P, 2, FC, 2, D], F32R)
        places = sb("e_places", [NBLK * PT, P], I32)
        placef = sb("e_placef", [NBLK * PT, P], F32)
        idxs = sb("e_idxs", [P, NBLK * PT], I32)
        bst = sb("e_bst", [E, 2, F], F32)
        bT = sb("e_bT", [P, E, NF], F32)
        bias = sb("e_bias", [P, 2, NF], F32)
        idx = sb("e_idx", [P, 2, PT], I32)
        xg = sb("e_xg", [P, 2, PT, D], F32)
        xT = sb("e_xT", [P, 2, 2, DC, PB], F32R)
        y = sb("e_y", [P, 2, FC, PB], F32)
        yT = sb("e_yT", [P, 2, 2, FC, PB], F32R)
        yo = sb("e_yo", [P, 2, PT, D], F32)
        px = K.ps("e_px", [P, DC, PB], F32, ctx)
        pg = K.ps("e_pg", [P, 2, NF, PB], F32, ctx)
        po = K.ps("e_po", [P, PT, D], F32, ctx)
        two = lambda n: [K.sem(n + "0"), K.sem(n + "1")]
        p_in, b_st = K.sem("e_p_in"), K.sem("e_b_st")
        pf_ok, p_tr, tab_ok = K.sem("e_pf_ok"), K.sem("e_p_tr"), K.sem("e_tab_ok")
        w1_in, w2_in, b_in, x_in, y_out = two("e_w1_in"), two("e_w2_in"), two("e_b_in"), two("e_x_in"), two("e_y_out")
        step_p, step_s = K.sem("e_step_p"), K.sem("e_step_s")
        w1_hi, w1_lo, w1_lop = K.sem("e_w1_hi"), K.sem("e_w1_lo"), K.sem("e_w1_lop")
        w2_hi, w2_lo, idx_ok = K.sem("e_w2_hi"), K.sem("e_w2_lo"), K.sem("e_idx_ok")
        tr, x_hi, x_lo = K.sem("e_tr"), K.sem("e_x_hi"), K.sem("e_x_lo")
        gate, up, ge, y_ok = K.sem("e_gate"), K.sem("e_up"), K.sem("e_ge"), K.sem("e_y_ok")
        y_hi, y_lo, oo = K.sem("e_y_hi"), K.sem("e_y_lo"), K.sem("e_oo")
        yo_a, yo_v = K.sem("e_yo_a"), K.sem("e_yo_v")

        def run(eng, head, body, tail):
            head()
            body(0, True, LB)
            with eng.Fori(1, LB - 2) as j:
                body(j, False, LB)
            body(LB - 2, False, 1)
            body(LB - 1, False, 0)
            tail()

        with nc.Block() as block:

            @block.sync
            def _(sp):
                rg = K.ins["L0_ffn_rg"].rearrange("e (c p) f -> e p c f", p=P)
                rw1 = K.ins["L0_ffn_rw1"].rearrange("e (c p) f -> e p c f", p=P)
                rw2 = K.ins["L0_ffn_rw2"].rearrange("e (c p) n -> e p c n", p=P)

                def expert(k):
                    sp.sem_inc(step_s, 1)
                    return bass.ds(sp.value_load(M.be[0:1, bass.ds(k, 1)], min_val=0, max_val=E - 1), 1)

                def load1(k, u):
                    one = expert(k)
                    sp.dma_start(st1[:, u, :, 0], rg[one].rearrange("a p c f -> (a p) c f")).then_inc(w1_in[u], 16)
                    sp.dma_start(st1[:, u, :, 1], rw1[one].rearrange("a p c f -> (a p) c f")).then_inc(w1_in[u], 16)

                def load2(k, u):
                    one = expert(k)
                    sp.dma_start(st2[:, u], rw2[one].rearrange("a p c n -> (a p) c n")).then_inc(w2_in[u], 16)

                def load_bias(k, u):
                    one = expert(k)
                    sp.dma_start(bias[:, u], bT[:, one].rearrange("p a n -> p (a n)")).then_inc(b_in[u], 16)

                def store(k, u):
                    sp.wait_ge(yo_a, k + 1)
                    sp.wait_ge(yo_v, k + 1)
                    sp.dma_start(K.y_d[bass.ds(k * PB, PB), :].rearrange("(i p) n -> p i n", p=P), yo[:, u]).then_inc(y_out[u], 16)

                def head():
                    sp.dma_start(places[:, :], K.idx_d.rearrange("(k p) o -> k (p o)", p=P)).then_inc(p_in, 16)
                    sp.dma_start(bst[:, 0], K.ins["L0_ffn_rgb"]).then_inc(b_st, 16)
                    sp.dma_start(bst[:, 1], K.ins["L0_ffn_rb1"]).then_inc(b_st, 16)
                    load1(0, 0)
                    load1(1, 1)
                    load2(0, 0)
                    load2(1, 1)
                    sp.wait_ge(tab_ok, 2)
                    load_bias(0, 0)
                    load_bias(1, 1)
                    sp.wait_ge(w1_lo, 1)
                    sp.wait_ge(w1_lop, 1)
                    load1(2, 0)

                def body(j, first, left):
                    for u in range(2):
                        k = j * 2 + u
                        if left * 2 - u >= 2:
                            sp.wait_ge(w1_lo, k + 2)
                            sp.wait_ge(w1_lop, k + 2)
                            load1(k + 3, 1 - u)
                        if left:
                            sp.wait_ge(w2_lo, k + 1)
                            load2(k + 2, u)
                        if not first:
                            store(k - 2, u)
                        if left:
                            sp.wait_ge(y_ok, k * 2 + 2)
                            load_bias(k + 2, u)

                def tail():
                    for u in range(2):
                        store(NBLK - 2 + u, u)
                    for u in range(2):
                        sp.wait_ge(y_out[u], 16 * LB + 16)

                run(sp, head, body, tail)

            @block.gpsimd
            def _(pool):
                def gather(k, u):
                    pool.wait_ge(idx_ok, k + 1)
                    pool.sem_inc(step_p, 1)
                    for i in range(PT):
                        pool.indirect_dma_start(out=xg[:, u, i], out_offset=None, in_=K.h2_d,
                                                in_offset=bass.IndirectOffsetOnAxis(ap=idx[:, u, i:i + 1], axis=0)
                                                ).then_inc(x_in[u], 16)

                def w1_low(k, u):
                    pool.wait_ge(w1_hi, k + 1)
                    nc.gpsimd.tensor_tensor(w1[:, u, 0:PW, 1].rearrange("p c (a f) -> p c a f", a=2), st1[:, u, 0:PW],
                                            w1[:, u, 0:PW, 0].rearrange("p c (a f) -> p c a f", a=2).bitcast(F32),
                                            ALU.subtract).then_inc(w1_lop, 1)

                def head():
                    gather(0, 0)
                    gather(1, 1)
                    w1_low(0, 0)
                    gather(2, 0)

                def body(j, first, left):
                    for u in range(2):
                        k = j * 2 + u
                        if left or not u:
                            w1_low(k + 1, 1 - u)
                        if left * 2 - u >= 2:
                            gather(k + 3, 1 - u)

                run(pool, head, body, lambda: None)

            @block.scalar
            def _(act):
                def w1_high(k, j, u, free=True):
                    act.wait_ge(w1_in[u], j * 32 + 32)
                    if free:
                        act.wait_ge(up, k - 1)
                    nc.scalar.activation(w1[:, u, :, 0].rearrange("p c (a f) -> p c a f", a=2), st1[:, u], ACT.Copy).then_inc(w1_hi, 1)

                def w2_high(k, j, u, first):
                    act.wait_ge(w2_in[u], j * 16 + 16)
                    if not first:
                        act.wait_ge(oo, k - 1)
                    nc.scalar.activation(w2[:, u, :, 0], st2[:, u], ACT.Copy).then_inc(w2_hi, 1)

                def x_high(k, u):
                    act.wait_ge(tr, k + 1)
                    for c in range(0, DC, 2):
                        nc.scalar.activation(xT[:, u, 0, c:c + 2], px[:, c:c + 2], ACT.Copy).then_inc(x_hi, 1)

                def gelu(k, j, u, first):
                    act.wait_ge(b_in[u], j * 16 + 16)
                    act.wait_ge(gate, k + 1)
                    if not first:
                        act.wait_ge(y_lo, k - 1)
                    for f in range(FC):
                        nc.scalar.activation(y[:, u, f], pg[:, u, f], ACT.Gelu, bias=bias[:, u, f:f + 1]).then_inc(ge, 1)

                def y_high(k, u):
                    act.wait_ge(y_ok, k * 2 + 2)
                    nc.scalar.activation(yT[:, u, 0], y[:, u], ACT.Copy).then_inc(y_hi, 1)

                def rows(k, j, u):
                    act.wait_ge(oo, k + 1)
                    act.wait_ge(y_out[u], j * 16 + 16)
                    nc.scalar.activation(yo[:, u, 0], po[:, 0], ACT.Copy).then_inc(yo_a, 1)

                def head():
                    w1_high(0, 0, 0, False)
                    x_high(0, 0)

                def body(j, first, left):
                    for u in range(2):
                        k = j * 2 + u
                        if u or not first:
                            y_high(k - 1, 1 - u)
                        if left or not u:
                            w1_high(k + 1, j + u, 1 - u, u or not first)
                        w2_high(k, j, u, first)
                        if not first:
                            rows(k - 2, j - 1, u)
                        gelu(k, j, u, first)
                        if left or not u:
                            x_high(k + 1, 1 - u)

                def tail():
                    rows(NBLK - 2, LB - 1, 0)
                    y_high(NBLK - 1, 1)
                    rows(NBLK - 1, LB - 1, 1)

                run(act, head, body, tail)

            @block.vector
            def _(dve):
                def w1_low(k, u):
                    dve.wait_ge(w1_hi, k + 1)
                    nc.vector.tensor_tensor(w1[:, u, PW:DC, 1].rearrange("p c (a f) -> p c a f", a=2), st1[:, u, PW:DC],
                                            w1[:, u, PW:DC, 0].rearrange("p c (a f) -> p c a f", a=2).bitcast(F32),
                                            ALU.subtract).then_inc(w1_lo, 1)

                def w2_low(k, u):
                    dve.wait_ge(w2_hi, k + 1)
                    nc.vector.tensor_tensor(w2[:, u, :, 1], st2[:, u], w2[:, u, :, 0].bitcast(F32), ALU.subtract).then_inc(w2_lo, 1)

                def name(k, u):
                    nc.vector.tensor_copy(idx[:, u], idxs[:, bass.ds(k * PT, PT)]).then_inc(idx_ok, 1)

                def x_low(k, u):
                    for n, c in enumerate(range(0, DC, 2)):
                        dve.wait_ge(x_hi, k * 2 + n + 1)
                        nc.vector.tensor_tensor(xT[:, u, 1, c:c + 2], px[:, c:c + 2], xT[:, u, 0, c:c + 2].bitcast(F32),
                                                ALU.subtract).then_inc(x_lo, 1)

                def times(k, u):
                    dve.wait_ge(up, k + 1)
                    for f in range(FC):
                        dve.wait_ge(ge, k * 2 + f + 1)
                        nc.vector.scalar_tensor_tensor(out=y[:, u, f], in0=pg[:, u, FC + f], scalar=bias[:, u, FC + f:FC + f + 1],
                                                       in1=y[:, u, f], op0=ALU.add, op1=ALU.mult).then_inc(y_ok, 1)

                def y_low(k, u):
                    dve.wait_ge(y_hi, k + 1)
                    nc.vector.tensor_tensor(yT[:, u, 1], y[:, u], yT[:, u, 0].bitcast(F32), ALU.subtract).then_inc(y_lo, 1)

                def rows(k, j, u):
                    dve.wait_ge(oo, k + 1)
                    dve.wait_ge(y_out[u], j * 16 + 16)
                    nc.vector.tensor_copy(yo[:, u, 1], po[:, 1]).then_inc(yo_v, 1)

                def head():
                    for u in range(2):
                        dve.sem_inc(y_out[u], 16)
                    dve.wait_ge(p_in, 16)
                    nc.vector.tensor_copy(placef[:, :], places[:, :]).then_inc(pf_ok, 1)
                    dve.wait_ge(p_tr, 1)
                    nc.vector.tensor_copy(idxs[:, :], po[:, 0, 0:NBLK * PT]).then_inc(tab_ok, 1)
                    dve.wait_ge(p_tr, 2)
                    nc.vector.tensor_copy(bT[:, :, :], po[:, 1, 0:NF * E].rearrange("p (a e) -> p e a", e=E)).then_inc(tab_ok, 1)
                    dve.wait_ge(tab_ok, 1)
                    name(0, 0)
                    name(1, 1)
                    w1_low(0, 0)
                    x_low(0, 0)
                    name(2, 0)

                def body(j, first, left):
                    for u in range(2):
                        k = j * 2 + u
                        if u or not first:
                            y_low(k - 1, 1 - u)
                        if left or not u:
                            w1_low(k + 1, 1 - u)
                        w2_low(k, u)
                        if not first:
                            rows(k - 2, j - 1, u)
                        times(k, u)
                        if left or not u:
                            x_low(k + 1, 1 - u)
                        if left * 2 - u >= 2:
                            name(k + 3, 1 - u)

                def tail():
                    rows(NBLK - 2, LB - 1, 0)
                    y_low(NBLK - 1, 1)
                    rows(NBLK - 1, LB - 1, 1)

                run(dve, head, body, tail)

            @block.tensor
            def _(pe):
                def x_trans(k, j, u):
                    pe.wait_ge(x_in[u], j * 16 * PT + 16 * PT)
                    for c in range(DC):
                        for i in range(PT):
                            m = nc.tensor.transpose(px[:, c, i * P:(i + 1) * P], xg[:, u, i, c * P:(c + 1) * P], K.ident[:, :])
                    m.then_inc(tr, 1)

                def first_(k, u):
                    pe.wait_ge(x_lo, k * 2 + 2)
                    pe.wait_ge(w1_lo, k + 1)
                    pe.wait_ge(w1_lop, k + 1)
                    for n in range(NF):
                        f_ = slice(n * P, (n + 1) * P)
                        m = split3(nc, pg[:, u, n], [(w1[:, u, c, 0, f_], w1[:, u, c, 1, f_], xT[:, u, 0, c], xT[:, u, 1, c])
                                                     for c in range(DC)])
                        if n == FC - 1:
                            m.then_inc(gate, 1)
                    m.then_inc(up, 1)

                def second(k, u, first):
                    pe.wait_ge(y_lo, k + 1)
                    pe.wait_ge(w2_lo, k + 1)
                    if not first:
                        pe.wait_ge(yo_a, k)
                        pe.wait_ge(yo_v, k)
                    for i in range(PT):
                        t_ = slice(i * P, (i + 1) * P)
                        m = split3(nc, po[:, i], [(yT[:, u, 0, f, t_], yT[:, u, 1, f, t_], w2[:, u, f, 0], w2[:, u, f, 1])
                                                  for f in range(FC)])
                    m.then_inc(oo, 1)

                def head():
                    pe.wait_ge(pf_ok, 1)
                    nc.tensor.transpose(po[:, 0, 0:NBLK * PT], placef[:, :], K.ident[0:NBLK * PT, 0:NBLK * PT]).then_inc(p_tr, 1)
                    pe.wait_ge(b_st, 32)
                    for n in range(NF):
                        m = nc.tensor.transpose(po[:, 1, n * E:(n + 1) * E], bst[:, n // FC, (n % FC) * P:(n % FC + 1) * P],
                                                K.ident[0:E, 0:E])
                    m.then_inc(p_tr, 1)
                    x_trans(0, 0, 0)

                def body(j, first, left):
                    for u in range(2):
                        k = j * 2 + u
                        first_(k, u)
                        if left or not u:
                            x_trans(k + 1, j + u, 1 - u)
                        if u or not first:
                            second(k - 1, 1 - u, first)

                run(pe, head, body, lambda: second(NBLK - 1, 1, False))


def stage_combine(K, M):
    nc = K.nc
    with ExitStack() as ctx:
        sb = lambda n, s, d: K.sb(n, s, d, ctx)
        at = sb("f_at", [P, 2, TOP], I32)
        b2 = sb("f_b2", [E, D], F32)
        cm = sb("f_cm", [P, 2, E], F32)
        cT = sb("f_cT", [E, 2, P], F32)
        r = sb("f_r", [P, 2, TOP, D], F32)
        o = sb("f_o", [P, 2, D], F32)
        pc = K.ps("f_pc", [E, 2, 512], F32, ctx)
        pb = K.ps("f_pb", [P, 2, D], F32, ctx)
        step_p = K.sem("f_step_p")
        at_ok, dch, o_ok, b2_in = K.sem("f_at_ok"), K.sem("f_dch"), K.sem("f_o_ok"), K.sem("f_b2_in")
        ct, ct_ok, bb = K.sem("f_ct"), K.sem("f_ct_ok"), K.sem("f_bb")
        r_in = [K.sem("f_r_in0"), K.sem("f_r_in1")]
        o_out = [K.sem("f_o_out0"), K.sem("f_o_out1")]

        with nc.Block() as block:

            @block.sync
            def _(sp):
                ov = K.out.rearrange("b (t p) n -> (b t) p n", p=P)
                sp.dma_start(b2[:, :], K.ins["L0_ffn_rb2"]).then_inc(b2_in, 16)
                with sp.Fori(0, NT // 2) as j:
                    for u in range(2):
                        t = j * 2 + u
                        sp.wait_ge(o_ok, t + 1)
                        sp.dma_start(ov[bass.ds(t, 1)].rearrange("a p n -> p (a n)"), o[:, u]).then_inc(o_out[u], 16)
                for u in range(2):
                    sp.wait_ge(o_out[u], 16 * (NT // 2) + 16)

            @block.gpsimd
            def _(pool):
                with pool.Fori(0, NT // 2) as j:
                    for u in range(2):
                        t = j * 2 + u
                        pool.wait_ge(at_ok, t * 2 + 1)
                        pool.sem_inc(step_p, 1)
                        for k in range(TOP):
                            pool.indirect_dma_start(out=r[:, u, k], out_offset=None, in_=K.y_d,
                                                    in_offset=bass.IndirectOffsetOnAxis(ap=at[:, u, k:k + 1], axis=0)
                                                    ).then_inc(r_in[u], 16)

            @block.scalar
            def _(act):
                with act.Fori(0, NT // 2) as j:
                    for u in range(2):
                        act.wait_ge(ct, j * 2 + u + 1)
                        nc.scalar.activation(cT[:, u], pc[:, u, 0:P], ACT.Copy).then_inc(ct_ok, 1)

            @block.tensor
            def _(pe):
                pe.wait_ge(b2_in, 16)
                with pe.Fori(0, NT // 2) as j:
                    for u in range(2):
                        t = j * 2 + u
                        pe.wait_ge(at_ok, t * 2 + 2)
                        nc.tensor.transpose(pc[:, u, 0:P], cm[:, u], K.ident[:, :]).then_inc(ct, 1)
                        pe.wait_ge(ct_ok, t + 1)
                        nc.tensor.matmul(pb[:, u], cT[:, u], b2[:, :], start=True, stop=True).then_inc(bb, 1)

            @block.vector
            def _(dve):
                def places(t, u):
                    nc.vector.tensor_copy(at[:, u], M.pos[:, :, bass.ds(t, 1)].rearrange("p k a -> p (k a)")).then_inc(at_ok, 1)
                    nc.vector.tensor_copy(cm[:, u], M.cmb[:, bass.ds(t, 1)].rearrange("p a e -> p (a e)")).then_inc(at_ok, 1)

                def tiles(j, more):
                    for u in range(2):
                        t = j * 2 + u
                        ch = Chain(dve, dch, t * 3)
                        dve.wait_ge(r_in[u], j * 32 + 32)
                        dve.wait_ge(bb, t + 1)
                        w = lambda k: M.wt[:, k, bass.ds(t, 1)]
                        for k in range(TOP):
                            ch.after(nc.vector.scalar_tensor_tensor(out=r[:, u, 0], in0=r[:, u, k], scalar=w(k),
                                                                    in1=r[:, u, 0] if k else pb[:, u],
                                                                    op0=ALU.mult, op1=ALU.add))
                        row = M.rows[:, bass.ds(j // 2, 1), 3].rearrange("p a n -> p (a n)")
                        ch.after(nc.vector.tensor_tensor(r[:, u, 0], r[:, u, 0], row, ALU.mult))
                        dve.wait_ge(o_out[u], j * 16 + 16)
                        nc.vector.tensor_tensor(o[:, u], r[:, u, 0], M.base[:, bass.ds(t, 1)].rearrange("p a n -> p (a n)"),
                                                ALU.add).then_inc(o_ok, 1)
                        if more:
                            dve.wait_ge(o_ok, t + 1)
                            places(t + 2, u)

                for u in range(2):
                    dve.sem_inc(o_out[u], 16)
                places(0, 0)
                places(1, 1)
                with dve.Fori(0, NT // 2 - 1) as j:
                    tiles(j, True)
                tiles(NT // 2 - 1, False)


class Kept:

    def __init__(self, K, ctx):
        self.rows = K.sb("rows", [P, B, 4, D], F32, ctx)
        self.base = K.sb("base", [P, NT, D], F32, ctx)
        self.aff = K.sb("aff", [P, NT, E], F32, ctx)
        self.wt = K.sb("wt", [P, TOP, NT], F32, ctx)
        self.cmb = K.sb("cmb", [P, NT, E], F32, ctx)
        self.pos = K.sb("pos", [P, TOP, NT], I32, ctx)
        self.be = K.sb("be", [P, NBLK], I32, ctx)


def program(nc, ins, out):
    with ExitStack() as ctx:
        K = Kernel(nc, ctx, ins, out)
        with ExitStack() as att:
            Mhl = K.sb("Mhl", [P, H, 2, D], F32R, att)
            modcol = K.sb("modcol", [P, B, 2, DC], F32, att)
            stage_weights(K, Mhl, modcol)
            stage_project(K, modcol)
            stage_attention(K, Mhl)
        K.free_sems()
        with ExitStack() as moe:
            M = Kept(K, moe)
            stage_shared(K, M)
            stage_route(K, M)
            stage_routed(K, M)
            stage_combine(K, M)


_INS = ["L0_attn_x", "L0_attn_wq", "L0_attn_wkv_a", "L0_attn_wkv_b", "L0_attn_wo", "L0_ffn_wa", "L0_ffn_rg",
        "L0_ffn_rgb", "L0_ffn_rw1", "L0_ffn_rb1", "L0_ffn_rw2", "L0_ffn_rb2", "L0_ffn_sg", "L0_ffn_sgb",
        "L0_ffn_sw1", "L0_ffn_sb1", "L0_ffn_sw2", "L0_ffn_sb2", "L0_c", "L0_wmod"]


def constants():
    inv = (np.float32(1.0) / np.float32(10000.0) ** (np.arange(HALF, dtype=np.float32) * np.float32(2.0)
                                                     / np.float32(ROPE))).astype(np.float32)
    ang = (np.arange(S, dtype=np.float32)[:, None] * inv[None, :]).astype(np.float32)
    rope = np.concatenate([np.cos(ang), np.sin(ang)], axis=1).astype(np.float32)
    k, m = np.arange(P)[:, None], np.arange(P)[None, :]
    const = np.stack([k == m, np.where(m > k, -1e30, 0.0), k < m]).astype(np.float32)
    e, f = np.arange(E)[:, None], np.arange(E)[None, :]
    small = np.concatenate([E - np.arange(E), (f < e).ravel(), np.arange(NBLK)]).astype(np.float32)[None, :]
    tok = (np.arange(P)[:, None] + P * np.arange(NT)[None, :]).astype(np.int32)
    return {"c_rope": rope, "c_const": const, "c_small": small, "c_tok": tok}


def kernel(**inputs):
    import concourse.bacc as _bacc
    from concourse.bass_utils import run_bass_kernel_spmd as _run

    nc = _bacc.Bacc("TRN2", target_bir_lowering=False, num_devices=1)
    arrays, ins = {}, {}
    for name, a in [(n, inputs[n]) for n in _INS] + list(constants().items()):
        a = np.ascontiguousarray(a)
        arrays[f"in_{name}"] = a
        ins[name] = nc.dram_tensor(f"in_{name}", a.shape, mybir.dt.from_np(a.dtype), kind="ExternalInput").ap()
    out = nc.dram_tensor("out_0", (B, S, D), F32, kind="ExternalOutput").ap()
    program(nc, ins, out)
    r = _run(nc, [arrays], core_ids=[0])
    return r.results[0]["out_0"]
```

```python
from contextlib import ExitStack

import numpy as np
import concourse.bass as bass
from concourse import mybir

ALU = mybir.AluOpType
ACT = mybir.ActivationFunctionType
AX = mybir.AxisListType
F32 = mybir.dt.float32
F32R = mybir.dt.float32r
BF16 = mybir.dt.bfloat16
I32 = mybir.dt.int32
U32 = mybir.dt.uint32

B, S, D = 4, 512, 512
H, NOPE, ROPE, VD, LORA = 16, 128, 64, 128, 128
E, SH, F = 16, 2, 256
P = 128
DC = D // P
FC = F // P
TB = S // P
NT = B * TB
QD = NOPE + ROPE
KVD = NOPE + VD
SCALE = 1.0 / float(np.sqrt(NOPE + ROPE))
EPS = 1e-5
HALF = ROPE // 2
TOP = 2
PB = 2 * P
NBLK = (B * S * TOP) // PB + E
VECS = 6


class Chain:

    def __init__(self, eng, sem, base=0):
        self.eng, self.sem, self.base, self.n = eng, sem, base, 0

    def after(self, ins):
        ins.then_inc(self.sem, 1)
        self.wait()

    def wait(self):
        self.n += 1
        self.eng.wait_ge(self.sem, self.base + self.n)


class Kernel:

    def __init__(self, nc, ctx, ins, out):
        self.nc, self.ctx, self.out = nc, ctx, out
        self.ins = ins
        self.sems = []
        d = lambda name, shape, dt: nc.dram_tensor(name, shape, dt, kind="Internal").ap()
        self.mod_d = d("mod_d", [B, VECS * D], F32)
        self.wqk_d = d("wqk_d", [H, P, 2, DC, P], F32)
        self.hT_d = d("hT_d", [B, P, DC, 2, S], F32)
        self.cT_d = d("cT_d", [B, P, 2, S], F32)
        self.kpe_d = d("kpe_d", [B, P, 2, S], F32)
        self.c_d = d("c_d", [B, P, TB, 2, P], F32)
        self.qpe_d = d("qpe_d", [B, H, P, S], F32)
        self.base_d = d("base_d", [B, TB, P, D], F32)
        self.h2_d = d("h2_d", [B * S, D], F32)
        self.y_d = d("y_d", [NBLK * PB, D], F32)
        self.ident = self.sb("ident", [P, P], F32)
        self.identb = self.sb("identb", [P, P], BF16)
        self.maskb = self.sb("maskb", [P, P], BF16)

    def sb(self, name, shape, dt, ctx=None):
        return (ctx or self.ctx).enter_context(self.nc.sbuf_tensor(name, shape, dt))

    def ps(self, name, shape, dt, ctx):
        return ctx.enter_context(self.nc.psum_tensor(name, shape, dt))

    def sem(self, name):
        self.sems.append(self.nc.alloc_semaphore(name=name))
        return self.sems[-1]

    def free_sems(self):
        self.nc.all_engine_barrier()
        self.nc.clear_and_free_semaphores(self.sems)
        self.nc.all_engine_barrier()
        self.sems = []


def split3(nc, out, pairs):
    last = None
    for n, (sh, sl, mh, ml) in enumerate(pairs):
        nc.tensor.matmul(out, sh, mh, start=n == 0, stop=False)
        nc.tensor.matmul(out, sh, ml, start=False, stop=False)
        last = nc.tensor.matmul(out, sl, mh, start=False, stop=n == len(pairs) - 1)
    return last


def stage_weights(K, N, Mhl, modcol):
    nc = K.nc
    NI = 4
    HD = D // 2
    MJ = VECS * 2 // NI
    assert VECS * 2 % NI == 0 and MJ < H // NI
    with ExitStack() as ctx:
        sb = lambda n, s, d: K.sb(n, s, d, ctx)
        constf = sb("w_constf", [P, 2, P], F32)
        csT = sb("w_csT", [P, DC, B], F32)
        wm = sb("w_wm", [P, VECS, DC, D], F32)
        mrow = sb("w_mrow", [B, VECS, D], F32)
        wkv = sb("w_wkv", [P, NI, KVD], F32)
        wqT = sb("w_wqT", [P, 2, D], F32)
        kvT = sb("w_kvT", [P, 2, KVD], F32)
        hl = sb("w_hl", [P, NI, 2, D], F32R)
        assert NI == TB
        wq = N.x[:, :, :].rearrange("p u (c n) -> p u c n", c=DC)
        wo = N.t
        msgn, cs, csg = N.h[0:B, 0:2], N.h[0:B, 2], N.h[0:B, 3]
        pq = K.ps("w_pq", [P, 2, D], F32, ctx)
        pk = K.ps("w_pk", [P, 2, D], F32, ctx)
        pw = K.ps("w_pw", [P, 2, D], F32, ctx)
        pm = K.ps("w_pm", [P, 2, D], F32, ctx)
        const_in, c_in, const_ok = K.sem("w_const_in"), K.sem("w_c_in"), K.sem("w_const_ok")
        silu, mod_t, mod_tc = K.sem("w_silu"), K.sem("w_mod_t"), K.sem("w_mod_tc")
        wm_in = [K.sem("w_wm_in0"), K.sem("w_wm_in1")]
        mod_mm, mod_ev, dch, one_ok = K.sem("w_mod_mm"), K.sem("w_mod_ev"), K.sem("w_dch"), K.sem("w_one_ok")
        mod_ok, col_t, mod_out = K.sem("w_mod_ok"), K.sem("w_col_t"), K.sem("w_mod_out")
        in_s = [K.sem(f"w_in{u}") for u in range(NI)]
        out_s = [K.sem(f"w_out{u}") for u in range(NI)]
        tr, ev_q, ev_k, mm = K.sem("w_tr"), K.sem("w_ev_q"), K.sem("w_ev_k"), K.sem("w_mm")
        hi_w, lo_w = K.sem("w_hi"), K.sem("w_lo")
        step_s = K.sem("w_step_s")
        K.x_in, K.t_in = K.sem("p_x_in"), K.sem("p_t_in")

        def run(eng, body):
            with eng.Fori(0, MJ) as j:
                body(j, True, True)
            for j in range(MJ, H // NI):
                body(j, False, j < H // NI - 1)

        with nc.Block() as block:

            @block.sync
            def _(sp):
                sp.dma_start(constf[:, :, :], K.ins["c_const"][0:2].rearrange("a p c -> p a c")).then_inc(const_in, 16)
                sp.dma_start(cs, K.ins["L0_c"]).then_inc(c_in, 16)

                def load(h, u):
                    sp.dma_start(wq[:, u], K.ins["L0_attn_wq"].rearrange("(c p) n -> p c n", p=P)[
                        :, :, bass.ds(h * QD, NOPE)]).then_inc(in_s[u], 16)
                    sp.dma_start(wkv[:, u], K.ins["L0_attn_wkv_b"][:, bass.ds(h * KVD, KVD)]).then_inc(in_s[u], 16)
                    sp.dma_start(wo[:, u], K.ins["L0_attn_wo"][bass.ds(h * VD, VD), :]).then_inc(in_s[u], 16)

                def body(j, mod, more):
                    for u in range(NI):
                        h = j * NI + u
                        if more:
                            sp.wait_ge(mm, h + 1)
                            sp.sem_inc(step_s, 1)
                            load(h + NI, u)
                        sp.wait_ge(lo_w, h * 2 + 5)
                        sp.sem_inc(step_s, 1)
                        sp.dma_start(K.wqk_d[bass.ds(h, 1)].rearrange("a p s c n -> p (a s) (c n)"),
                                     hl[:, u].bitcast(F32)).then_inc(out_s[u], 16)

                for u in range(NI):
                    load(u, u)
                sp.dma_start(N.rows[:, :, :], K.ins["c_rope"].rearrange("a p n -> p a n")).then_inc(K.t_in, 16)
                run(sp, body)
                sp.dma_start(N.x[:, :, :], K.ins["L0_attn_x"][0].rearrange("(t p) n -> p t n", p=P)).then_inc(K.x_in, 16)
                sp.wait_ge(mod_ok, 1)
                sp.dma_start(K.mod_d.rearrange("b (v n) -> b v n", n=D), mrow[:, :, :]).then_inc(mod_out, 16)
                for u in range(NI):
                    sp.wait_ge(out_s[u], 16 * (H // NI + 1))
                sp.wait_ge(mod_out, 16)

            @block.gpsimd
            def _(pool):
                wmv = K.ins["L0_wmod"].rearrange("(c p) (v n) -> v p c n", p=P, n=D)
                for v in range(VECS):
                    if v:
                        pool.wait_ge(mm, 2 * v - 1)
                    pool.dma_start(wm[:, v], wmv[v]).then_inc(wm_in[v % 2], 16)

            @block.scalar
            def _(act):
                act.wait_ge(c_in, 16)
                nc.scalar.activation(csg, cs, ACT.Sigmoid).then_inc(silu, 1)
                for u in range(NI):
                    act.sem_inc(out_s[u], 16)

                def take(h, u):
                    act.wait_ge(tr, h + 1)
                    nc.scalar.activation(wqT[:, u % 2], pq[:, u % 2], ACT.Copy).then_inc(ev_q, 1)

                def body(j, mod, more):
                    for u in range(NI):
                        h = j * NI + u
                        if more or u < NI - 1:
                            take(h + 1, u + 1)
                        act.wait_ge(mm, h + 1)
                        act.wait_ge(out_s[u], j * 16 + 16)
                        nc.scalar.activation(hl[:, u, 0], pw[:, u % 2], ACT.Copy).then_inc(hi_w, 1)
                        nc.scalar.activation(Mhl[:, bass.ds(h, 1), 0, :].rearrange("p a n -> p (a n)"),
                                             pm[:, u % 2], ACT.Copy).then_inc(hi_w, 1)

                take(0, 0)
                run(act, body)

            @block.vector
            def _(dve):
                dve.sem_inc(lo_w, 4)
                dve.sem_inc(mod_ev, 1)
                dve.wait_ge(const_in, 16)
                nc.vector.tensor_copy(K.ident[:, :], constf[:, 0]).then_inc(const_ok, 1)
                nc.vector.tensor_copy(K.identb[:, :], constf[:, 0]).then_inc(const_ok, 1)
                nc.vector.tensor_copy(K.maskb[:, :], constf[:, 1]).then_inc(const_ok, 1)
                dve.wait_ge(silu, 1)
                nc.vector.tensor_tensor(csg, csg, cs, ALU.mult).then_inc(silu, 1)
                dve.wait_ge(mod_t, 1)
                nc.vector.tensor_copy(csT[:, :, :], pm[:, 1, 0:DC * B].rearrange("p (c b) -> p c b", b=B)).then_inc(mod_tc, 1)

                def take(h, u):
                    dve.wait_ge(tr, h + 1)
                    nc.vector.tensor_copy(kvT[:, u % 2], pk[:, u % 2, 0:KVD]).then_inc(ev_k, 1)

                def low(h, u):
                    dve.wait_ge(hi_w, h * 2 + 1)
                    nc.vector.tensor_tensor(hl[:, u, 1], pw[:, u % 2], hl[:, u, 0].bitcast(F32),
                                            ALU.subtract).then_inc(lo_w, 1)
                    dve.wait_ge(hi_w, h * 2 + 2)
                    nc.vector.tensor_tensor(Mhl[:, bass.ds(h, 1), 1, :].rearrange("p a n -> p (a n)"), pm[:, u % 2],
                                            Mhl[:, bass.ds(h, 1), 0, :].rearrange("p a n -> p (a n)").bitcast(F32),
                                            ALU.subtract).then_inc(lo_w, 1)

                def body(j, mod, more):
                    for u in range(NI):
                        h = j * NI + u
                        if more or u < NI - 1:
                            take(h + 1, u + 1)
                        low(h, u)
                        if mod:
                            dve.wait_ge(mod_mm, h + 1)
                            nc.vector.tensor_copy(mrow[:, bass.ds(j * (NI // 2) + u // 2, 1), (u % 2) * HD:(u % 2 + 1) * HD]
                                                  .rearrange("b a n -> b (a n)"), pk[0:B, u % 2, KVD:KVD + HD]).then_inc(mod_ev, 1)

                take(0, 0)
                with dve.Fori(0, MJ) as j:
                    body(j, True, True)
                dve.wait_ge(mod_ev, 2 * VECS + 1)
                ch = Chain(dve, dch)
                for v in (1, 4):
                    nc.vector.tensor_scalar(mrow[:, v], mrow[:, v], 1.0, None, ALU.add).then_inc(one_ok, 1)
                for n, v in enumerate((2, 5)):
                    ch.after(nc.vector.tensor_scalar(msgn[:, n], mrow[:, v], 0.0, 2.0, ALU.is_ge, ALU.mult))
                    ch.after(nc.vector.tensor_scalar(msgn[:, n], msgn[:, n], -1.0, None, ALU.add))
                    ch.after(nc.vector.tensor_tensor(mrow[:, v], mrow[:, v], msgn[:, n], ALU.mult))
                    ch.after(nc.vector.tensor_scalar(mrow[:, v], mrow[:, v], 0.25, None, ALU.max))
                    ch.after(nc.vector.tensor_tensor(mrow[:, v], mrow[:, v], msgn[:, n], ALU.mult))
                dve.wait_ge(one_ok, 2)
                dve.sem_inc(mod_ok, 1)
                for j in range(MJ, H // NI):
                    body(j, False, j < H // NI - 1)
                dve.wait_ge(col_t, 1)
                nc.vector.tensor_copy(modcol[:, :, :, :], pk[:, 1, 0:2 * DC * B].rearrange(
                    "p (v c b) -> p b v c", v=2, c=DC))

            @block.tensor
            def _(pe):
                def transposes(h, j, u):
                    pe.wait_ge(in_s[u], j * 48 + 48)
                    for c in range(DC):
                        nc.tensor.transpose(pq[:, u % 2, c * P:(c + 1) * P], wq[:, u, c], K.ident[:, :])
                    for n in range(2):
                        t = nc.tensor.transpose(pk[:, u % 2, n * P:(n + 1) * P], wkv[:, u, n * P:(n + 1) * P], K.ident[:, :])
                    t.then_inc(tr, 1)

                pe.wait_ge(const_ok, 3)
                transposes(0, 0, 0)
                pe.wait_ge(silu, 2)
                for c in range(DC):
                    t = nc.tensor.transpose(pm[:, 1, c * B:(c + 1) * B], csg[:, c * P:(c + 1) * P], K.ident[0:B, 0:B])
                t.then_inc(mod_t, 1)
                pe.wait_ge(mod_tc, 1)

                def body(j, mod, more):
                    for u in range(NI):
                        h = j * NI + u
                        if more or u < NI - 1:
                            if mod or (j == MJ and not u):
                                pe.wait_ge(mod_ev, h + 1)
                            transposes(h + 1, j + (u + 1) // NI, (u + 1) % NI)
                        pe.wait_ge(ev_q, h + 1)
                        pe.wait_ge(ev_k, h + 1)
                        pe.wait_ge(lo_w, h * 2 + 2)
                        for c in range(DC):
                            nc.tensor.matmul(pw[:, u % 2, c * P:(c + 1) * P], wqT[:, u % 2, c * P:(c + 1) * P],
                                             kvT[:, u % 2, 0:P], start=True, stop=True)
                        nc.tensor.matmul(pm[:, u % 2], kvT[:, u % 2, P:2 * P], wo[:, u], start=True, stop=True).then_inc(mm, 1)
                        if mod:
                            v = j * (NI // 2) + u // 2
                            pe.wait_ge(wm_in[u // 2], j * 16 + 16)
                            for c in range(DC):
                                w = wm[:, bass.ds(v, 1), c, (u % 2) * HD:(u % 2 + 1) * HD].rearrange("p a n -> p (a n)")
                                m = nc.tensor.matmul(pk[0:B, u % 2, KVD:KVD + HD], csT[:, c], w, start=c == 0, stop=c == DC - 1)
                            m.then_inc(mod_mm, 1)

                run(pe, body)
                pe.wait_ge(mod_ok, 1)
                for v in range(2):
                    for c in range(DC):
                        o = (v * DC + c) * B
                        t = nc.tensor.transpose(pk[:, 1, o:o + B], mrow[:, v, c * P:(c + 1) * P], K.ident[0:B, 0:B])
                t.then_inc(col_t, 1)


def stage_project(K, N, modcol):
    nc = K.nc
    NQ = H * ROPE
    NC = LORA + ROPE
    GH = P // HALF
    NG = H // GH
    assert NG == TB == DC == 4 and ROPE + ROPE == P
    with ExitStack() as ctx:
        sb = lambda n, s, d: K.sb(n, s, d, ctx)
        wpe = sb("p_wpe", [P, DC, 2, NG, 2, P], F32R)
        wc = sb("p_wc", [P, DC, 2, 2 * P], F32R)
        st = sb("p_st", [P, TB, 6], F32)
        mv = sb("p_mv", [P, TB, 2], F32)
        ve = sb("p_ve", [P, TB], F32)
        rs = sb("p_rs", [P, TB], F32)
        half = sb("p_half", [P, TB], F32)
        mc = sb("p_mc", [P, 2, 2, DC], F32)
        hT = sb("p_hT", [P, 2, DC, 2, S], F32R)
        ck = sb("p_ck", [P, 2, 2, S], F32R)
        cr = sb("p_cr", [P, TB, 2, P], F32R)
        qs = sb("p_qs", [P, 2, 4, S], F32R)
        x = N.x
        hf = N.acc[:, 0:2]
        cf = N.acc[:, 2]
        kr = N.acc[:, 3]
        qc = N.t[:, :, :].rearrange("p (a b) n -> p a b n", a=2)
        qr = N.h[:, :, :].rearrange("p (a b) n -> p a b n", a=2)
        tab = N.rows
        wcst = N.h[:, :, :].rearrange("p a n -> p (a n)")[:, 0:DC * NC].rearrange("p (c n) -> p c n", c=DC)
        wst = qs[:, :, :, :].bitcast(F32).rearrange("p a b n -> p (a b n)").rearrange("p (c n) -> p c n", c=DC)
        px = K.ps("p_px", [P, 2, S], F32, ctx)
        pc = K.ps("p_pc", [P, 2, S], F32, ctx)
        pq = K.ps("p_pq", [P, 2, 2, S], F32, ctx)
        w_in, wc_in, t_in, w_hi, w_lo = (K.sem("p_w_in"), K.sem("p_wc_in"), K.t_in, K.sem("p_w_hi"), K.sem("p_w_lo"))
        x_in, pch, dch = K.x_in, K.sem("p_pch"), K.sem("p_dch")
        step_v = K.sem("p_step_v")
        var_ok, rstd_ok, x_n, x_t = K.sem("p_var_ok"), K.sem("p_rstd_ok"), K.sem("p_x_n"), K.sem("p_x_t")
        h_hi, h_full, h_lo = K.sem("p_h_hi"), K.sem("p_h_full"), K.sem("p_h_lo")
        cp, c_hi, c_lo = K.sem("p_cp"), K.sem("p_c_hi"), K.sem("p_c_lo")
        k_rd, k_rot, k_hi, k_lo = K.sem("p_k_rd"), K.sem("p_k_rot"), K.sem("p_k_hi"), K.sem("p_k_lo")
        qp, q_rd, rot, q_hi, q_lo = K.sem("p_qp"), K.sem("p_q_rd"), K.sem("p_rot"), K.sem("p_q_hi"), K.sem("p_q_lo")
        ct, r_hi, r_lo = K.sem("p_ct"), K.sem("p_r_hi"), K.sem("p_r_lo")
        out_h, out_q = [K.sem("p_out_h0"), K.sem("p_out_h1")], [K.sem("p_out_q0"), K.sem("p_out_q1")]
        out_k, out_c = K.sem("p_out_k"), K.sem("p_out_c")

        def run(eng, body):
            with eng.Fori(0, B // 2 - 1) as j:
                body(j, False)
            body(B // 2 - 1, True)

        with nc.Block() as block:

            @block.sync
            def _(sp):
                def load_x(b):
                    sp.dma_start(x[:, :, :], K.ins["L0_attn_x"][bass.ds(b, 1)].rearrange("a (t p) n -> p (a t) n", p=P)).then_inc(x_in, 16)

                sp.dma_start(wcst[:, :, :], K.ins["L0_attn_wkv_a"].rearrange("(c p) n -> p c n", p=P)).then_inc(wc_in, 16)
                wqv = K.ins["L0_attn_wq"].rearrange("(c p) (h q) -> p c h q", p=P, q=QD)
                for c in range(DC):
                    sp.dma_start(wst[:, c].rearrange("p (h q) -> p h q", q=ROPE), wqv[:, c, :, NOPE:QD]).then_inc(w_in, 16)
                sp.wait_ge(x_t, DC)
                load_x(1)

                def body(j, last):
                    for u in range(2):
                        b = j * 2 + u
                        sp.wait_ge(h_hi, b * DC + DC)
                        sp.wait_ge(h_lo, b * DC + DC)
                        sp.dma_start(K.hT_d[bass.ds(b, 1)].rearrange("a p c s n -> (a p) (c s n)"),
                                     hT[:, u].rearrange("p c s n -> p (c s n)").bitcast(F32)).then_inc(out_h[u], 16)
                        sp.wait_ge(c_lo, b + 1)
                        sp.dma_start(K.cT_d[bass.ds(b, 1)].rearrange("a p s n -> (a p) (s n)"),
                                     ck[:, 0].rearrange("p s n -> p (s n)").bitcast(F32)).then_inc(out_k, 16)
                        sp.wait_ge(k_lo, b + 1)
                        sp.dma_start(K.kpe_d[bass.ds(b, 1)].rearrange("a p s n -> (a p) (s n)"),
                                     ck[:, 1].rearrange("p s n -> p (s n)").bitcast(F32)).then_inc(out_k, 16)
                        for g in range(NG):
                            sp.wait_ge(q_lo, b * NG + g + 1)
                            for h in range(GH):
                                sp.dma_start(K.qpe_d[bass.ds(b, 1), g * GH + h].rearrange("a (k r) n -> (a r) k n", r=HALF),
                                             qs[h * HALF:(h + 1) * HALF, g % 2].bitcast(F32)).then_inc(out_q[g % 2], 16)
                            if g == 1:
                                sp.wait_ge(r_lo, b + 2)
                                sp.dma_start(K.c_d[bass.ds(b, 1)].rearrange("a p t s n -> (a p) (t s n)"),
                                             cr[:, :, :, :].rearrange("p t s n -> p (t s n)").bitcast(F32)).then_inc(out_c, 16)
                                if not last:
                                    sp.wait_ge(x_t, b * DC + 2 * DC)
                                    load_x(b + 2)

                run(sp, body)
                for u in range(2):
                    sp.wait_ge(out_h[u], 16 * (B // 2 + 1))
                    sp.wait_ge(out_q[u], 16 * GH * (B * NG // 2 + 1))
                sp.wait_ge(out_k, 32 * (B + 1))
                sp.wait_ge(out_c, 16 * (B + 1))

            @block.gpsimd
            def _(pool):
                def rstd(b):
                    pool.wait_ge(var_ok, b + 1)
                    nc.gpsimd.tensor_tensor(rs[:, :], ve[:, :], half[:, :], ALU.pow).then_inc(rstd_ok, 1)

                def add(b, g):
                    pool.wait_ge(q_rd, b * NG + g + 3)
                    nc.gpsimd.tensor_tensor(qr[:, g % 2, 0], qc[:, 0, 0], qc[:, 1, 1], ALU.subtract)
                    nc.gpsimd.tensor_tensor(qr[:, g % 2, 1], qc[:, 0, 1], qc[:, 1, 0], ALU.add).then_inc(rot, 1)

                def q_low(b, g):
                    pool.wait_ge(q_hi, b * NG + g + 1)
                    nc.gpsimd.tensor_tensor(qs[:, g % 2, 1::2], qr[:, g % 2], qs[:, g % 2, 0::2].bitcast(F32),
                                            ALU.subtract).then_inc(q_lo, 1)

                nc.gpsimd.memset(half[:, :], -0.5).then_inc(pch, 1)
                pool.wait_ge(pch, 1)
                rstd(0)

                def body(j, last):
                    for u in range(2):
                        b = j * 2 + u
                        more = not (last and u)
                        if more:
                            rstd(b + 1)
                        for g in range(NG):
                            add(b, g)
                            q_low(b, g)

                run(pool, body)

            @block.scalar
            def _(act):
                def h_high(b, j, v, c):
                    act.wait_ge(x_t, b * DC + c + 1)
                    act.wait_ge(out_h[v], j * 16 + 16)
                    nc.scalar.activation(hT[:, v, c, 0], px[:, c % 2], ACT.Identity, bias=mc[:, v, 0, c:c + 1],
                                         scale=mc[:, v, 1, c:c + 1]).then_inc(h_hi, 1)

                def q_high(b, g):
                    act.wait_ge(rot, b * NG + g + 2)
                    act.wait_ge(out_q[g % 2], (b * 2 + g // 2) * (16 * GH) + 16 * GH)
                    nc.scalar.activation(qs[:, g % 2, 0::2], qr[:, g % 2], ACT.Copy).then_inc(q_hi, 1)

                for u in range(2):
                    act.sem_inc(out_h[u], 16)
                    act.sem_inc(out_q[u], 16 * GH)
                act.sem_inc(out_k, 32)
                act.sem_inc(out_c, 16)
                for c in range(DC):
                    h_high(0, 0, 0, c)
                act.wait_ge(wc_in, 16)
                nc.scalar.activation(wc[:, :, 0, 0:P], wcst[:, :, 0:LORA], ACT.Copy).then_inc(w_hi, 1)
                for e in range(2):
                    part = wcst[:, :, LORA + e:NC:2]
                    for i in range(2):
                        o = P + (e * 2 + i) * HALF
                        nc.scalar.activation(wc[:, :, 0, o:o + HALF], part, ACT.Copy).then_inc(w_hi, 1)
                act.wait_ge(w_in, 16 * DC)
                for c in range(DC):
                    for e in range(2):
                        nc.scalar.activation(wpe[:, c, 0, :, e].rearrange("p g (h r) -> p g h r", r=HALF),
                                             wst[:, c, e::2].rearrange("p (g h r) -> p g h r", h=GH, r=HALF),
                                             ACT.Copy).then_inc(w_hi, 1)

                def body(j, last):
                    for u in range(2):
                        b = j * 2 + u
                        more = not (last and u)
                        act.wait_ge(cp, b * 2 + 1)
                        nc.scalar.activation(cf, pc[:, 0], ACT.Copy)
                        act.wait_ge(out_k, b * 32 + 32)
                        nc.scalar.activation(ck[:, 0, 0], pc[:, 0], ACT.Copy).then_inc(c_hi, 1)
                        act.wait_ge(k_rot, b + 1)
                        nc.scalar.activation(ck[:, 1, 0], kr, ACT.Copy).then_inc(k_hi, 1)
                        for g in range(NG):
                            if more:
                                for c in {0: [0], 1: [1], 2: [2, 3], 3: []}[g]:
                                    h_high(b + 1, j + u, 1 - u, c)
                            if g == 1:
                                act.wait_ge(ct, b + 1)
                                act.wait_ge(out_c, b * 16 + 16)
                                nc.scalar.activation(cr[:, :, 0], pc[:, 0].rearrange("p (t n) -> p t n", t=TB), ACT.Copy).then_inc(r_hi, 1)
                            q_high(b, g)

                run(act, body)

            @block.vector
            def _(dve):
                def norm(b, v):
                    ch = Chain(dve, dch, b * (2 * TB))
                    nc.vector.tensor_copy(mc[:, v], modcol[:, bass.ds(b, 1)].rearrange("p a v c -> p (a v) c"))
                    dve.wait_ge(x_in, b * 16 + 16)
                    for t in range(TB):
                        ch.n += 1
                        nc.vector.bn_stats(st[:, t], x[:, t]).then_inc(ch.sem, 1)
                    dve.wait_ge(ch.sem, ch.base + ch.n)
                    dve.sem_inc(step_v, 1)
                    for t in range(TB):
                        ch.n += 1
                        nc.vector.bn_aggr(mv[:, t], st[:, t]).then_inc(ch.sem, 1)
                    dve.wait_ge(ch.sem, ch.base + ch.n)
                    nc.vector.tensor_scalar(ve[:, :], mv[:, :, 1], EPS, None, ALU.add).then_inc(var_ok, 1)
                    dve.wait_ge(rstd_ok, b + 1)
                    for t in range(TB):
                        m = nc.vector.tensor_scalar(x[:, t], x[:, t], mv[:, t, 0:1], rs[:, t:t + 1], ALU.subtract, ALU.mult)
                    m.then_inc(x_n, 1)

                def h_whole_low(b, v, c):
                    dve.wait_ge(h_hi, b * DC + c + 1)
                    nc.vector.tensor_scalar(hf[:, c % 2], px[:, c % 2], mc[:, v, 1, c:c + 1], mc[:, v, 0, c:c + 1],
                                            ALU.mult, ALU.add).then_inc(h_full, 1)
                    dve.wait_ge(h_full, b * DC + c + 1)
                    nc.vector.tensor_tensor(hT[:, v, c, 1], hf[:, c % 2], hT[:, v, c, 0].bitcast(F32), ALU.subtract).then_inc(h_lo, 1)

                dve.sem_inc(q_rd, 2)
                for credit in (r_lo, k_rd, rot):
                    dve.sem_inc(credit, 1)
                norm(0, 0)
                for c in range(DC):
                    h_whole_low(0, 0, c)
                dve.wait_ge(w_hi, 5)
                nc.vector.tensor_tensor(wc[:, :, 1, 0:P], wcst[:, :, 0:LORA], wc[:, :, 0, 0:P].bitcast(F32), ALU.subtract).then_inc(w_lo, 1)
                for e in range(2):
                    part = wcst[:, :, LORA + e:NC:2]
                    for i in range(2):
                        o = P + (e * 2 + i) * HALF
                        nc.vector.tensor_tensor(wc[:, :, 1, o:o + HALF], part, wc[:, :, 0, o:o + HALF].bitcast(F32),
                                                ALU.subtract).then_inc(w_lo, 1)
                for c in range(DC):
                    for e in range(2):
                        dve.wait_ge(w_hi, 5 + c * 2 + e + 1)
                        v_ = lambda s: wpe[:, c, s, :, e].rearrange("p g (h r) -> p g h r", r=HALF)
                        nc.vector.tensor_tensor(v_(1), wst[:, c, e::2].rearrange("p (g h r) -> p g h r", h=GH, r=HALF),
                                                v_(0).bitcast(F32), ALU.subtract).then_inc(w_lo, 1)
                dve.wait_ge(t_in, 16)

                def body(j, last):
                    for u in range(2):
                        b = j * 2 + u
                        more = not (last and u)
                        if more:
                            norm(b + 1, 1 - u)
                        dve.wait_ge(c_hi, b + 1)
                        nc.vector.tensor_tensor(ck[:, 0, 1], pc[:, 0], ck[:, 0, 0].bitcast(F32), ALU.subtract).then_inc(c_lo, 1)
                        dve.wait_ge(cp, b * 2 + 2)
                        dve.wait_ge(rot, b * NG + 1)
                        nc.vector.tensor_tensor(qc[:, 0, 0], pc[:, 1], tab[:, 2], ALU.mult)
                        nc.vector.tensor_tensor(qc[ROPE:P, 1, 0], pc[0:ROPE, 1], tab[0:ROPE, 3], ALU.mult)
                        nc.vector.tensor_tensor(qc[0:ROPE, 1, 0], pc[ROPE:P, 1], tab[ROPE:P, 3], ALU.mult).then_inc(k_rd, 1)
                        dve.wait_ge(k_rd, b + 2)
                        nc.vector.tensor_tensor(kr, qc[:, 0, 0], qc[:, 1, 0], ALU.add).then_inc(k_rot, 1)
                        for g in range(NG):
                            dve.wait_ge(qp, b * NG + g + 1)
                            dve.wait_ge(rot, b * NG + g + 1)
                            if g == 0:
                                dve.wait_ge(k_rot, b + 1)
                            for k in range(2):
                                m = nc.vector.tensor_tensor(qc[:, k], pq[:, g % 2], tab[:, k:k + 1].broadcast_to([P, 2, S]), ALU.mult)
                            m.then_inc(q_rd, 1)
                            if g == 0:
                                dve.wait_ge(k_hi, b + 1)
                                nc.vector.tensor_tensor(ck[:, 1, 1], kr, ck[:, 1, 0].bitcast(F32), ALU.subtract).then_inc(k_lo, 1)
                            if more:
                                for c in {0: [0], 1: [1], 2: [2, 3], 3: []}[g]:
                                    h_whole_low(b + 1, 1 - u, c)
                            if g == 1:
                                dve.wait_ge(r_hi, b + 1)
                                nc.vector.tensor_tensor(cr[:, :, 1], pc[:, 0].rearrange("p (t n) -> p t n", t=TB),
                                                        cr[:, :, 0].bitcast(F32), ALU.subtract).then_inc(r_lo, 1)

                run(dve, body)

            @block.tensor
            def _(pe):
                def x_trans(b, c, first=False):
                    if not (first and c < 2):
                        pe.wait_ge(h_full, b * DC + c - 1)
                    for t in range(TB):
                        m = nc.tensor.transpose(px[:, c % 2, t * P:(t + 1) * P], x[:, t, c * P:(c + 1) * P], K.ident[:, :])
                    m.then_inc(x_t, 1)

                pe.wait_ge(x_n, 1)
                for c in range(DC):
                    x_trans(0, c, True)

                def product(out, u, w):
                    return split3(nc, out, [(w(c, 0), w(c, 1), hT[:, u, c, 0], hT[:, u, c, 1]) for c in range(DC)])

                def body(j, last):
                    for u in range(2):
                        b = j * 2 + u
                        more = not (last and u)
                        pe.wait_ge(h_lo, b * DC + DC)
                        pe.wait_ge(r_lo, b + 1)
                        pe.wait_ge(k_rd, b + 1)
                        pe.wait_ge(w_lo, 5)
                        for n in range(2):
                            product(pc[:, n], u, lambda c, s: wc[:, c, s, n * P:(n + 1) * P]).then_inc(cp, 1)
                        pe.wait_ge(w_lo, 5 + 2 * DC)
                        for g in range(NG):
                            pe.wait_ge(q_rd, b * NG + g + 1)
                            for e in range(2):
                                m = product(pq[:, g % 2, e], u, lambda c, s: wpe[:, c, s, g, e])
                            m.then_inc(qp, 1)
                            if more:
                                pe.wait_ge(x_n, b + 2)
                                for c in {0: [0], 1: [1], 2: [2, 3], 3: []}[g]:
                                    x_trans(b + 1, c)
                            if g == 1:
                                pe.wait_ge(c_lo, b + 1)
                                for t in range(TB):
                                    m = nc.tensor.transpose(pc[:, 0, t * P:(t + 1) * P], cf[:, t * P:(t + 1) * P], K.ident[:, :])
                                m.then_inc(ct, 1)

                run(pe, body)


class SecondNorm:

    def __init__(self, K, ctx):
        self.K = K
        sb = lambda n, s, d: K.sb(n, s, d, ctx)
        self.acc = sb("n_acc", [P, TB, D], F32)
        self.x = sb("n_x", [P, TB, D], F32)
        self.t = sb("n_t", [P, TB, D], F32)
        self.h = sb("n_h", [P, TB, D], F32)
        self.rows = sb("n_rows", [P, 4, D], F32)
        self.b2 = sb("n_b2", [P, D], F32)
        self.st = sb("n_st", [P, TB, 6], F32)
        self.mv = sb("n_mv", [P, TB, 2], F32)
        self.ve = sb("n_ve", [P, TB], F32)
        self.rs = sb("n_rs", [P, TB], F32)
        self.half = sb("n_half", [P, TB], F32)

    def sems(self, pre):
        s = lambda n: self.K.sem(pre + n)
        self.loaded, self.pch, self.dch, self.step = s("n_loaded"), s("n_pch"), s("n_dch"), s("n_step")
        self.acc_used, self.x1_ok, self.var_ok = s("n_acc_used"), s("n_x1_ok"), s("n_var_ok")
        self.h2_out, self.base_out = s("n_h2_out"), s("n_base_out")

    def prepare(self, pool):
        nc, ins = self.K.nc, self.K.ins["L0_ffn_sb2"]
        self.chain = Chain(pool, self.pch)
        nc.gpsimd.memset(self.acc[:, :, :], 0.0).then_inc(self.acc_used, 1)
        self.chain.after(nc.gpsimd.memset(self.half[:, :], -0.5))
        for e in range(SH):
            pool.dma_start(self.t[:, e], ins[e:e + 1, :].broadcast_to([P, D])).then_inc(self.loaded, 16)
        pool.wait_ge(self.loaded, 16 * SH)
        self.chain.after(nc.gpsimd.tensor_tensor(self.b2[:, :], self.t[:, 0], self.t[:, 1], ALU.add))

    def load(self, pool, b):
        K = self.K
        pool.dma_start(self.x[:, :, :], K.ins["L0_attn_x"][b].rearrange("(t p) n -> p t n", p=P)).then_inc(self.loaded, 16)
        pool.dma_start(self.rows[:, :, :].rearrange("p v n -> p (v n)"),
                       K.mod_d[b:b + 1, 2 * D:6 * D].broadcast_to([P, 4 * D])).then_inc(self.loaded, 16)

    def steps(self, pool, b, n, base):
        K, nc, tt = self.K, self.K.nc, self.K.nc.gpsimd.tensor_tensor
        ch = self.chain
        row = lambda v: self.rows[:, v:v + 1].broadcast_to([P, TB, D])
        x, t, h = self.x[:, :, :], self.t[:, :, :], self.h[:, :, :]
        ch.after(tt(t, self.acc[:, :, :], row(0), ALU.mult))
        nc.gpsimd.memset(self.acc[:, :, :], 0.0).then_inc(self.acc_used, 1)
        tt(x, t, x, ALU.add).then_inc(self.x1_ok, 1)
        pool.wait_ge(self.var_ok, n + 1)
        ch.after(tt(self.rs[:, :], self.ve[:, :], self.half[:, :], ALU.pow))
        for i in range(TB):
            nc.gpsimd.tensor_scalar(self.h[:, i], self.x[:, i], self.mv[:, i, 0:1], self.rs[:, i:i + 1],
                                    ALU.subtract, ALU.mult).then_inc(ch.sem, 1)
            ch.n += 1
        pool.wait_ge(ch.sem, ch.base + ch.n)
        ch.after(tt(h, h, row(2), ALU.mult))
        ch.after(tt(h, h, row(1), ALU.add))
        pool.dma_start(K.h2_d[b * S:(b + 1) * S].rearrange("(t p) n -> p t n", p=P), h).then_inc(self.h2_out, 16)
        ch.after(tt(t, h, self.b2[:, :].unsqueeze(1).broadcast_to([P, TB, D]), ALU.add))
        ch.after(tt(t, t, row(3), ALU.mult))
        ch.after(tt(base, x, t, ALU.add))

    def stats(self, dve, n):
        nc = self.K.nc
        dve.wait_ge(self.x1_ok, n + 1)
        for i in range(TB):
            nc.vector.bn_stats(self.st[:, i], self.x[:, i]).then_inc(self.dch, 1)
        dve.wait_ge(self.dch, n * (2 * TB) + TB)
        dve.sem_inc(self.step, 1)
        for i in range(TB):
            nc.vector.bn_aggr(self.mv[:, i], self.st[:, i]).then_inc(self.dch, 1)
        dve.wait_ge(self.dch, n * (2 * TB) + 2 * TB)
        nc.vector.tensor_scalar(self.ve[:, :], self.mv[:, :, 1], EPS, None, ALU.add).then_inc(self.var_ok, 1)


def stage_attention(K, N, Mhl):
    nc = K.nc
    PAIRS = H // 2
    OFF = {0: 0, 3: 5 * P, 1: 6 * P, 2: 9 * P}
    ZERO = 4 * P
    NPT = 11 * P
    with ExitStack() as ctx:
        sb = lambda n, s, d: K.sb(n, s, d, ctx)
        hT = sb("a_hT", [P, 2, DC, 2, S], F32R)
        cT = sb("a_cT", [P, 2, 2, S], F32R)
        kpe = sb("a_kpe", [P, 2, 2, S], F32R)
        cv = sb("a_cv", [P, TB, 2, P], F32R)
        wqk = sb("a_wqk", [P, 2, 2, DC, P], F32R)
        qpe = sb("a_qpe", [P, 2, S], F32R)
        qT = sb("a_qT", [P, 2, S], F32R)
        prs = sb("a_pr", [P, TB * (TB + 1) // 2 * P], F32)
        pr = [prs[:, i * (i + 1) // 2 * P:(i + 1) * (i + 2) // 2 * P] for i in range(TB)]
        pT = sb("a_pT", [P, 2, NPT], F32R)
        oT = sb("a_oT", [P, 4, 2, S], F32R)
        acc = N.acc
        nmax = sb("a_nmax", [P, TB], F32)
        rsum = sb("a_rsum", [P, TB], F32)
        rinv = sb("a_rinv", [P, TB], F32)
        psS = K.ps("a_psS", [P, 3, 512], F32, ctx)
        psX = K.ps("a_psX", [P, 512], F32, ctx)
        psY = K.ps("a_psY", [P, 512], F32, ctx)
        psZ = K.ps("a_psZ", [P, 512], F32, ctx)
        psT = K.ps("a_psT", [P, 2, 512], F32, ctx)
        h_in = [K.sem("a_h_in0"), K.sem("a_h_in1")]
        b_in = [K.sem("a_b_in0"), K.sem("a_b_in1")]
        landed_h = K.sem("a_landed_h")
        c_in, landed, landed_c = K.sem("a_c_in"), K.sem("a_landed"), K.sem("a_landed_c")
        w_in = [K.sem("a_w_in0"), K.sem("a_w_in1")]
        q_in = [K.sem("a_q_in0"), K.sem("a_q_in1")]
        qp, q_hi, q_lo = K.sem("a_qp"), K.sem("a_q_hi"), K.sem("a_q_lo")
        sc, mx, ex, rc, nr = K.sem("a_sc"), K.sem("a_mx"), K.sem("a_ex"), K.sem("a_rc"), K.sem("a_nr")
        pt, p_hi, p_lo = K.sem("a_pt"), K.sem("a_p_hi"), K.sem("a_p_lo")
        pv, o_hi, o_lo = K.sem("a_pv"), K.sem("a_o_hi"), K.sem("a_o_lo")
        ot, ac, zero = K.sem("a_ot"), K.sem("a_ac"), K.sem("a_zero")
        N.sems("a_")
        score = [psS[:, 0, 0:2 * P], psS[:, 0, 2 * P:4 * P], psS[:, 1, 0:3 * P], psS[:, 2, :]]
        groups = [(psT[:, 0], slice(0, 4 * P), [(0, 0)]),
                  (psT[:, 1], slice(OFF[3], OFF[3] + 4 * P), [(3, 0), (1, P)]),
                  (psX[:, 0:2 * P], slice(OFF[2], OFF[2] + 2 * P), [(2, 0)])]

        def run(eng, pair, pause=None):
            two = lambda m: [pair(m * 2 + v, v, 4, False) for v in range(2)]
            pair(0, 0, 0, False)
            pair(1, 1, 1, False)
            pair(2, 0, 2, False)
            pair(3, 1, 3, False)
            QB = PAIRS // 2
            if pause is None:
                with eng.Fori(2, B * QB - 1) as m:
                    two(m)
            else:
                def batch(b, count):
                    two(b * QB)
                    pause(b)
                    with eng.Fori(1, count) as m:
                        two(b * QB + m)
                with eng.Fori(2, QB) as m:
                    two(m)
                with eng.Fori(1, B - 1) as b:
                    batch(b, QB)
                batch(B - 1, QB - 1)
            pair(B * PAIRS - 2, 0, 4, False)
            pair(B * PAIRS - 1, 1, 4, True)

        with nc.Block() as block:

            @block.sync
            def _(sp):
                def load_w(g, u):
                    sp.dma_start(wqk[:, u].rearrange("p s c n -> p (s c n)").bitcast(F32),
                                 K.wqk_d[bass.ds(g % H, 1)].rearrange("a p s c n -> p (a s c n)")).then_inc(w_in[u], 16)

                def load_q(g, u):
                    sp.dma_start(qpe[:, u].bitcast(F32), K.qpe_d.rearrange("b h p n -> (b h) p n")[bass.ds(g, 1)]
                                 .rearrange("a p n -> p (a n)")).then_inc(q_in[u], 16)

                for u in range(2):
                    load_w(u, u)
                    load_q(u, u)
                with sp.Fori(0, B * PAIRS - 1) as n:
                    for u in range(2):
                        g = n * 2 + u
                        sp.wait_ge(qp, g + 1)
                        load_w(g + 2, u)
                        sp.wait_ge(sc, g * 4 + 4)
                        load_q(g + 2, u)

            @block.gpsimd
            def _(pool):
                def load(b):
                    s = b % 2
                    pool.dma_start(hT[:, s].rearrange("p c s n -> p (c s n)").bitcast(F32),
                                   K.hT_d[b].rearrange("p c s n -> p (c s n)")).then_inc(h_in[s], 16)
                    pool.dma_start(cT[:, s].rearrange("p s n -> p (s n)").bitcast(F32),
                                   K.cT_d[b].rearrange("p s n -> p (s n)")).then_inc(b_in[s], 16)
                    pool.dma_start(kpe[:, s].rearrange("p s n -> p (s n)").bitcast(F32),
                                   K.kpe_d[b].rearrange("p s n -> p (s n)")).then_inc(b_in[s], 16)

                def load_c(b):
                    pool.dma_start(cv[:, :, :, :].rearrange("p t s n -> p (t s n)").bitcast(F32),
                                   K.c_d[b].rearrange("p t s n -> p (t s n)")).then_inc(c_in, 16)

                load(0)
                load_c(0)
                pool.wait_ge(h_in[0], 16)
                pool.sem_inc(landed_h, 1)
                pool.wait_ge(b_in[0], 32)
                pool.sem_inc(landed, 1)
                pool.wait_ge(c_in, 16)
                pool.sem_inc(landed_c, 1)
                N.prepare(pool)
                N.load(pool, 0)
                load(1)
                pool.wait_ge(h_in[1], 16)
                pool.sem_inc(landed_h, 1)
                pool.wait_ge(b_in[1], 32)
                pool.sem_inc(landed, 1)
                for b in range(1, B):
                    pool.wait_ge(pv, H * b)
                    load_c(b)
                    if b + 1 < B:
                        pool.wait_ge(qp, H * b)
                        pool.wait_ge(sc, 4 * H * b)
                        load(b + 1)
                    pool.wait_ge(c_in, 16 * (b + 1))
                    pool.sem_inc(landed_c, 1)
                    if b + 1 < B:
                        pool.wait_ge(h_in[(b + 1) % 2], 16 * ((b + 1) // 2 + 1))
                        pool.sem_inc(landed_h, 1)
                        pool.wait_ge(b_in[(b + 1) % 2], 32 * ((b + 1) // 2 + 1))
                        pool.sem_inc(landed, 1)
                    pool.wait_ge(ac, b * (PAIRS * TB) + TB)
                    pool.wait_ge(N.loaded, 16 * SH + 32 * b)
                    N.steps(pool, b - 1, b - 1, N.x[:, :, :])
                    pool.dma_start(K.base_d[b - 1].rearrange("t p n -> p t n"), N.x[:, :, :]).then_inc(N.base_out, 16)
                    pool.wait_ge(N.base_out, 16 * b)
                    pool.wait_ge(N.h2_out, 16 * b)
                    N.load(pool, b)
                pool.wait_ge(N.loaded, 16 * SH + 32 * B)

            @block.scalar
            def _(act):
                def exps(g):
                    for i in range(TB):
                        act.wait_ge(mx, g * 4 + max(i + 1, 2))
                        w = (i + 1) * P
                        nc.scalar.activation(pr[i], score[i][:, 0:w], ACT.Exp, bias=nmax[:, i:i + 1],
                                             accum_out=rsum[:, i:i + 1]).then_inc(ex, 1)

                def q_high(g):
                    act.wait_ge(qp, g + 1)
                    nc.scalar.activation(qT[:, 0], psX[:, :], ACT.Copy, scale=SCALE).then_inc(q_hi, 1)

                def o_high(g, n, s, fresh):
                    act.wait_ge(pv, g + 1)
                    if not fresh:
                        act.wait_ge(ot, n * 4 - 3)
                    nc.scalar.activation(oT[:, s, 0], psY[:, :], ACT.Copy).then_inc(o_hi, 1)

                def p_high(g):
                    for k, (src, dst, _) in enumerate(groups):
                        act.wait_ge(pt, g * 3 + k + 1)
                        nc.scalar.activation(pT[:, 0, dst], src, ACT.Copy).then_inc(p_hi, 1)

                def pair(n, v, early, last):
                    for u in range(2):
                        g = n * 2 + u
                        exps(g)
                        if not (last and u):
                            q_high(g + 1)
                        if u:
                            o_high(g - 1, n, v * 2, early < 2)
                        elif early:
                            o_high(g - 1, n - 1, 3 - v * 2, early < 3)
                        p_high(g)

                q_high(0)
                run(act, pair)
                o_high(B * H - 1, B * PAIRS - 1, 3, False)

            @block.vector
            def _(dve):
                for credit in (o_lo, p_lo):
                    dve.sem_inc(credit, 1)
                dve.sem_inc(ac, TB)
                for s in range(2):
                    nc.vector.memset(pT[:, s, ZERO:ZERO + P].bitcast(U32), 0).then_inc(zero, 1)

                def softmax(g, between):
                    for i in range(TB):
                        dve.wait_ge(sc, g * 4 + max(i + 1, 2))
                        nc.vector.tensor_reduce(nmax[:, i:i + 1], score[i][:, 0:(i + 1) * P], AX.X, ALU.max,
                                                negate=True).then_inc(mx, 1)
                    between()
                    dve.wait_ge(ex, g * 4 + 4)
                    nc.vector.reciprocal(rinv[:, :], rsum[:, :]).then_inc(rc, 1)
                    dve.wait_ge(rc, g + 1)
                    for i in range(TB):
                        nc.vector.tensor_scalar(pr[i], pr[i], rinv[:, i:i + 1], None, ALU.mult).then_inc(nr, 1)

                def q_low(g):
                    dve.wait_ge(q_hi, g + 1)
                    nc.vector.scalar_tensor_tensor(out=qT[:, 1], in0=psX[:, :], scalar=SCALE, in1=qT[:, 0].bitcast(F32),
                                                   op0=ALU.mult, op1=ALU.subtract).then_inc(q_lo, 1)

                def o_low(g, s):
                    dve.wait_ge(o_hi, g + 1)
                    nc.vector.tensor_tensor(oT[:, s, 1], psY[:, :], oT[:, s, 0].bitcast(F32), ALU.subtract).then_inc(o_lo, 1)

                def p_low(g):
                    for k, (src, dst, _) in enumerate(groups):
                        dve.wait_ge(p_hi, g * 3 + k + 1)
                        nc.vector.tensor_tensor(pT[:, 1, dst], src, pT[:, 0, dst].bitcast(F32), ALU.subtract).then_inc(p_lo, 1)

                def add_out(n, t):
                    dve.wait_ge(ot, n * 4 + t + 2)
                    if t == 0:
                        dve.wait_ge(N.acc_used, n // PAIRS + 1)
                    dve.wait_ge(ac, n * 4 + t + 1)
                    nc.vector.tensor_tensor(acc[:, t], psZ[:, :], acc[:, t], ALU.add).then_inc(ac, 1)

                def pair(n, v, early, last):
                    for u in range(2):
                        g = n * 2 + u
                        if u:
                            out = (lambda t: add_out(n - 1, t)) if early else (lambda t: None)
                        else:
                            out = (lambda t: add_out(n - 2, 2 + t)) if early > 1 else (lambda t: None)
                        softmax(g, lambda: out(0))
                        if not (last and u):
                            q_low(g + 1)
                        out(1)
                        if u or early:
                            o_low(g - 1, v * 2 if u else 3 - v * 2)
                        p_low(g)

                q_low(0)
                run(dve, pair, lambda b: N.stats(dve, b - 1))
                o_low(B * H - 1, 3)
                add_out(B * PAIRS - 2, 2)
                add_out(B * PAIRS - 2, 3)
                for t in range(TB):
                    add_out(B * PAIRS - 1, t)

            @block.tensor
            def _(pe):
                def qproj(g, u, transposed):
                    pe.wait_ge(landed_h, g // H + 1)
                    pe.wait_ge(w_in[u], (g // 2) * 16 + 16)
                    pe.wait_ge(p_lo, transposed * 3 + 1)
                    h_ = lambda c, s: hT[:, bass.ds((g // H) % 2, 1), c, s].rearrange("p a n -> p (a n)")
                    split3(nc, psX[:, :], [(wqk[:, u, 0, c], wqk[:, u, 1, c], h_(c, 0), h_(c, 1))
                                           for c in range(DC)]).then_inc(qp, 1)

                def scores(g, u):
                    pe.wait_ge(landed, g // H + 1)
                    pe.wait_ge(q_lo, g + 1)
                    pe.wait_ge(q_in[u], (g // 2) * 16 + 16)
                    for i in range(TB):
                        w = max(i + 1, 2) * P
                        q = slice(i * P, (i + 1) * P)
                        out = score[i][:, 0:w]
                        k_ = lambda src, s: src[:, bass.ds((g // H) % 2, 1), s, 0:w].rearrange("p a n -> p (a n)")
                        nc.tensor.matmul(out, qT[:, 0, q], k_(cT, 0), start=True, stop=False)
                        nc.tensor.matmul(out, qT[:, 0, q], k_(cT, 1), start=False, stop=False)
                        nc.tensor.matmul(out, qT[:, 1, q], k_(cT, 0), start=False, stop=False)
                        nc.tensor.matmul(out, qpe[:, u, q], k_(kpe, 0), start=False, stop=False)
                        nc.tensor.matmul(out, qpe[:, u, q], k_(kpe, 1), start=False, stop=False)
                        nc.tensor.matmul(out[:, q], K.identb[:, :], K.maskb[:, :], start=False, stop=True).then_inc(sc, 1)

                def values(g):
                    pe.wait_ge(landed_c, g // H + 1)
                    pe.wait_ge(p_lo, g * 3 + 4)
                    pe.wait_ge(o_lo, g + 1)
                    n = 0
                    for j in range(TB):
                        q0 = min(j, 2) * P
                        o = OFF[j] - (j * P - q0)
                        w = S - q0
                        for cs, ps in ((0, 0), (0, 1), (1, 0)):
                            m = nc.tensor.matmul(psY[:, q0:S], cv[:, j, cs], pT[:, ps, o:o + w], start=n == 0, stop=n == 11)
                            n += 1
                    m.then_inc(pv, 1)

                def transposes(g):
                    pe.wait_ge(nr, g * 4 + 4)
                    for k, (dst, _, parts) in enumerate(groups):
                        for j, o in parts:
                            for i in range(j, TB):
                                m = nc.tensor.transpose(dst[:, o + (i - j) * P:o + (i - j + 1) * P],
                                                        pr[i][:, j * P:(j + 1) * P], K.ident[:, :])
                        m.then_inc(pt, 1)

                def output(n, v, t):
                    pe.wait_ge(o_lo, n * 2 + 3)
                    pe.wait_ge(ac, n * 4 + t + TB)
                    q = slice(t * P, (t + 1) * P)
                    M_ = lambda u, s: Mhl[:, bass.ds((n % PAIRS) * 2 + u, 1), s].rearrange("p a n -> p (a n)")
                    split3(nc, psZ[:, :], [(oT[:, v * 2 + u, 0, q], oT[:, v * 2 + u, 1, q], M_(u, 0), M_(u, 1))
                                           for u in range(2)]).then_inc(ot, 1)

                def pair(n, v, early, last):
                    for u in range(2):
                        g = n * 2 + u
                        if u:
                            out = (lambda t: output(n - 1, 1 - v, t)) if early else (lambda t: None)
                        else:
                            out = (lambda t: output(n - 2, v, 2 + t)) if early > 1 else (lambda t: None)
                        scores(g, u)
                        out(0)
                        if not (last and u):
                            qproj(g + 1, 1 - u, g)
                        out(1)
                        if u or early:
                            values(g - 1)
                        if not (last and u):
                            pe.wait_ge(q_lo, g + 2)
                        transposes(g)

                pe.wait_ge(zero, 2)
                pe.sem_inc(ot, 1)
                qproj(0, 0, 0)
                run(pe, pair)
                values(B * H - 1)
                output(B * PAIRS - 2, 0, 2)
                output(B * PAIRS - 2, 0, 3)
                for t in range(TB):
                    output(B * PAIRS - 1, 1, t)


def stage_shared(K, N, M):
    nc = K.nc
    NU = SH * FC
    NP = NBLK * PB // P
    NS = E + E * E + NBLK + P
    with ExitStack() as ctx:
        sb = lambda n, s, d: K.sb(n, s, d, ctx)
        w1 = sb("s_w1", [P, SH, DC, 2, 2 * F], F32R)
        w2 = sb("s_w2", [P, SH, FC, 2, D], F32R)
        bst = sb("s_bst", [2 * SH, F], F32)
        bT = sb("s_bT", [P, FC, 2 * SH], F32)
        waf = sb("s_waf", [P, DC, E], F32)
        wa = sb("s_wa", [P, 2, DC, E], F32R)
        hx = sb("s_hx", [P, TB, D], F32)
        hT = sb("s_hT", [P, 2, DC, 2, S], F32R)
        ys = sb("s_ys", [P, 4, D], F32)
        y, so = ys[:, 0:2], ys[:, 2:4]
        yT = sb("s_yT", [P, NU, 2, S], F32R)
        st2 = sb("s_st2", [P, FC, D], F32)
        lt = sb("s_lt", [E, S], F32)
        st1 = ys[:, :, :].rearrange("p a n -> p (a n)").rearrange("p (c a f) -> p c a f", c=DC, a=2)
        small = N.acc[:, 0, 0:NS]
        row = sb("r_row", [P, 1], F32)
        trif = N.acc[:, 1, 0:P]
        tri = sb("r_tri", [P, P], BF16)
        ones = sb("r_ones", [P, P], BF16)
        shape = lambda a: a.rearrange("p (a k t) -> p a k t", a=2, k=TOP)
        part = shape(N.acc[:, 2, 0:2 * TOP * NT].bitcast(I32))
        partf = shape(N.acc[:, 2, 2 * TOP * NT:4 * TOP * NT])
        rowsum = N.acc[:, 3, 0:NP]
        mb = sb("r_mb", [P, NT, E], BF16)
        m1, m2, mt = sb("r_m1", [P, NT], F32), sb("r_m2", [P, NT], F32), sb("r_mt", [P, NT], F32)
        cnti = sb("r_cnti", [P, 2, E], I32)
        nb, first, base = sb("r_nb", [P, E], F32), sb("r_first", [P, E], F32), sb("r_base", [P, E], F32)
        bef = sb("r_bef", [P, NBLK], F32)
        free = N.t[:, :, :].rearrange("p t n -> p (t n)")
        wide = lambda n: free[:, n * NT * E:(n + 1) * NT * E].rearrange("p (t e) -> p t e", e=E)
        af, oh1, oh2, t1, rank = (wide(n) for n in range(5))
        tt = free[:, 5 * NT * E:5 * NT * E + E * E].rearrange("p (e f) -> p e f", f=E)
        cmp = N.h[:, 0:NBLK * E // D].rearrange("p t n -> p (t n)").rearrange("p (k e) -> p k e", e=E)
        rev = small[:, 0:E]
        before = small[:, E:E + E * E].rearrange("p (e f) -> p e f", f=E)
        blk = small[:, E + E * E:E + E * E + NBLK]
        count = small[:, NS - P:NS]
        hot_row = N.x[:, :, :].bitcast(BF16).rearrange("p t n -> p (t n)").rearrange("p (k t n) -> p k t n", k=TOP, t=NT)
        hot_tile = N.rows[:, :, :].bitcast(BF16).rearrange("p t n -> p (t n)").rearrange("p (k t a n) -> p k t a n", k=TOP, t=NT, a=2)
        hot = N.h[:, 2:4].rearrange("p t n -> p (t n)")[:, 0:NT * NP].rearrange("p (t n) -> p t n", t=NT)
        px = K.ps("s_px", [P, S], F32, ctx)
        pl = K.ps("s_pl", [P, S], F32, ctx)
        pg = K.ps("s_pg", [P, 2, 2, S], F32, ctx)
        po = K.ps("s_po", [P, 2, D], F32, ctx)
        pr, pn = pl[:, 0:NT * E], pl[:, NT * E:NT * E + E]
        w_in, w_hi, w_lo, wa_in = K.sem("s_w_in"), K.sem("s_w_hi"), K.sem("s_w_lo"), K.sem("s_wa_in")
        c_in, hx_in, b_in, g_in = K.sem("s_c_in"), K.sem("s_hx_in"), K.sem("s_b_in"), K.sem("s_g_in")
        bias_t, bias_ok, wa_hi, wa_ok = K.sem("s_bias_t"), K.sem("s_bias_ok"), K.sem("s_wa_hi"), K.sem("s_wa_ok")
        x_t, h_hi, h_lo = K.sem("s_x_t"), K.sem("s_h_hi"), K.sem("s_h_lo")
        lg, lt_ok, lg_t, aff_ok = K.sem("s_lg"), K.sem("s_lt_ok"), K.sem("s_lg_t"), K.sem("s_aff_ok")
        gate, up, ge, y_ok = K.sem("s_gate"), K.sem("s_up"), K.sem("s_ge"), K.sem("s_y_ok")
        y_hi, y_lo, oo, so_ok = K.sem("s_y_hi"), K.sem("s_y_lo"), K.sem("s_oo"), K.sem("s_so_ok")
        dch, sig, hot_ok, named = K.sem("r_dch"), K.sem("r_sig"), K.sem("r_hot_ok"), K.sem("r_named")
        mb_ok, ranks, zero = K.sem("r_mb_ok"), K.sem("r_ranks"), K.sem("r_zero")
        last_base = K.sem("s_last_base")
        N.sems("s_")

        def run(eng, body):
            with eng.Fori(0, B // 2 - 1) as j:
                body(j, False)
            body(B // 2 - 1, True)

        with nc.Block() as block:

            @block.sync
            def _(sp):
                def weights(e):
                    sp.dma_start(st1[:, :, 0], K.ins["L0_ffn_sg"][e].rearrange("(c p) f -> p c f", p=P)).then_inc(w_in, 16)
                    sp.dma_start(st1[:, :, 1], K.ins["L0_ffn_sw1"][e].rearrange("(c p) f -> p c f", p=P)).then_inc(w_in, 16)
                    sp.dma_start(st2[:, :, :], K.ins["L0_ffn_sw2"][e].rearrange("(c p) n -> p c n", p=P)).then_inc(w_in, 16)

                def rows(b):
                    sp.dma_start(hx[:, :, :], K.h2_d.rearrange("(b t p) n -> b p t n", b=B, p=P)[bass.ds(b, 1)]
                                 .rearrange("a p t n -> (a p) t n")).then_inc(hx_in, 16)

                rows(0)
                weights(0)
                sp.dma_start(waf[:, :, :], K.ins["L0_ffn_wa"].rearrange("(c p) e -> p c e", p=P)).then_inc(wa_in, 16)
                sp.dma_start(bst[0:SH, :], K.ins["L0_ffn_sgb"]).then_inc(wa_in, 16)
                sp.dma_start(bst[SH:2 * SH, :], K.ins["L0_ffn_sb1"]).then_inc(wa_in, 16)
                sp.wait_ge(w_lo, 2)
                weights(1)
                for b in range(B):
                    sp.dma_start(M.gb[:, b], K.mod_d[b:b + 1, 5 * D:6 * D].broadcast_to([P, D])).then_inc(g_in, 16)
                for b in range(B - 1):
                    sp.dma_start(M.base[:, b * TB:(b + 1) * TB], K.base_d[b].rearrange("t p n -> p t n")).then_inc(b_in, 16)
                sp.wait_ge(x_t, DC)
                rows(1)
                sp.wait_ge(N.acc_used, 1)
                sp.dma_start(small, K.ins["c_small"].broadcast_to([P, NS])).then_inc(c_in, 16)
                sp.dma_start(row[:, :], K.ins["c_row"]).then_inc(c_in, 16)
                sp.dma_start(trif, K.ins["c_const"][2]).then_inc(c_in, 16)

                def body(j, last):
                    for u in range(2):
                        b = j * 2 + u
                        if not last:
                            sp.wait_ge(x_t, b * DC + 2 * DC)
                            if u:
                                sp.wait_ge(N.h2_out, 16)
                            rows(b + 2)

                run(sp, body)

            @block.gpsimd
            def _(pool):
                N.chain = Chain(pool, N.pch)
                nc.gpsimd.memset(ones[:, :], 1.0).then_inc(zero, 1)
                N.steps(pool, B - 1, 0, M.base[:, (B - 1) * TB:NT])
                pool.sem_inc(last_base, 1)
                pool.wait_ge(N.h2_out, 16)

            @block.scalar
            def _(act):
                def h_high(b, v, c):
                    act.wait_ge(x_t, b * DC + c + 1)
                    nc.scalar.activation(hT[:, v, c, 0], px[:, :], ACT.Copy).then_inc(h_hi, 1)

                def weights(e):
                    act.wait_ge(w_in, 48 * (e + 1))
                    nc.scalar.activation(w1[:, e, :, 0].rearrange("p c (a f) -> p c a f", a=2), st1, ACT.Copy).then_inc(w_hi, 1)
                    nc.scalar.activation(w2[:, e, :, 0], st2[:, :, :], ACT.Copy).then_inc(w_hi, 1)

                def logits(b):
                    act.wait_ge(lg, b + 1)
                    nc.scalar.activation(lt[:, :], pl[0:E, :], ACT.Copy).then_inc(lt_ok, 1)

                def logits_by_token(b):
                    act.wait_ge(lg_t, b + 1)
                    nc.scalar.activation(M.aff[:, bass.ds(b * TB, TB)], pl[:, 0:TB * E].rearrange("p (t e) -> p t e", e=E),
                                         ACT.Copy).then_inc(aff_ok, 1)

                h_high(0, 0, 0)
                weights(0)
                act.wait_ge(wa_in, 48)
                nc.scalar.activation(wa[:, 0], waf[:, :, :], ACT.Copy).then_inc(wa_hi, 1)
                for c in range(1, DC):
                    h_high(0, 0, c)
                weights(1)
                logits(0)
                act.wait_ge(bias_ok, 1)
                act.wait_ge(w_lo, 4)

                def body(j, last):
                    for u in range(2):
                        b = j * 2 + u
                        more = not (last and u)
                        for m in range(NU):
                            e, f = m // FC, m % FC
                            n = b * NU + m
                            act.wait_ge(gate, n + 1)
                            act.wait_ge(y_lo, n + 1)
                            nc.scalar.activation(y[:, m % 2], pg[:, m % 2, 0], ACT.Gelu, bias=bT[:, f, e:e + 1]).then_inc(ge, 1)
                            if m == 0:
                                logits_by_token(b)
                                if not more:
                                    act.wait_ge(aff_ok, B)
                                    act.wait_ge(last_base, 1)
                                    nc.scalar.activation(af, M.aff[:, :, :], ACT.Sigmoid).then_inc(sig, 1)
                            if more:
                                h_high(b + 1, 1 - u, m)
                            act.wait_ge(y_ok, n + 3)
                            nc.scalar.activation(yT[:, m, 0], y[:, m % 2], ACT.Copy).then_inc(y_hi, 1)
                        if more:
                            logits(b + 1)

                run(act, body)

            @block.vector
            def _(dve):
                def h_low(b, v, c):
                    dve.wait_ge(h_hi, b * DC + c + 1)
                    nc.vector.tensor_tensor(hT[:, v, c, 1], px[:, :], hT[:, v, c, 0].bitcast(F32), ALU.subtract).then_inc(h_lo, 1)

                def weights(e):
                    dve.wait_ge(w_hi, 2 * e + 1)
                    nc.vector.tensor_tensor(w1[:, e, :, 1].rearrange("p c (a f) -> p c a f", a=2), st1,
                                            w1[:, e, :, 0].rearrange("p c (a f) -> p c a f", a=2).bitcast(F32),
                                            ALU.subtract).then_inc(w_lo, 1)
                    dve.wait_ge(w_hi, 2 * e + 2)
                    nc.vector.tensor_tensor(w2[:, e, :, 1], st2[:, :, :], w2[:, e, :, 0].bitcast(F32), ALU.subtract).then_inc(w_lo, 1)

                def update(b, t, k):
                    n = b * TB + t
                    row = M.gb[:, bass.ds(b, 1)].rearrange("p a n -> p (a n)")
                    bt = M.base[:, bass.ds(n, 1)].rearrange("p a n -> p (a n)")
                    dve.wait_ge(oo, n + 1)
                    nc.vector.tensor_tensor(so[:, k], po[:, k], row, ALU.mult).then_inc(so_ok, 1)
                    dve.wait_ge(so_ok, n + 3)
                    nc.vector.tensor_tensor(bt, bt, so[:, k], ALU.add)

                over = lambda a: a.unsqueeze(2).broadcast_to([P, NT, E])
                under = lambda a: a.unsqueeze(1).broadcast_to([P, NT, E])
                tt_, v = nc.vector.tensor_tensor, nc.vector
                ch = Chain(dve, dch)

                def best():
                    dve.wait_ge(c_in, 48)
                    dve.wait_ge(sig, 1)
                    ch.after(v.tensor_copy(tri[:, :], trif))
                    for m, oh in ((m1, oh1), (m2, oh2)):
                        ch.after(v.tensor_reduce(m[:, :], af, AX.X, ALU.max))
                        ch.after(tt_(t1, af, over(m[:, :]), ALU.is_equal))
                        ch.after(tt_(t1, t1, under(rev), ALU.mult))
                        ch.after(v.tensor_reduce(mt[:, :], t1, AX.X, ALU.max))
                        ch.after(tt_(oh, t1, over(mt[:, :]), ALU.is_equal))
                        if oh is oh1:
                            flat = lambda a: a.rearrange("p t e -> p (t e)")
                            ch.after(v.scalar_tensor_tensor(out=flat(af), in0=flat(oh), scalar=-2.0, in1=flat(af),
                                                            op0=ALU.mult, op1=ALU.add))
                    tt_(mb[:, :, :], oh1, oh2, ALU.add).then_inc(mb_ok, 1)

                def places():
                    dve.wait_ge(ranks, 1)
                    ch.after(v.tensor_scalar(cnti[:, 0], pn, float(PB - 1), None, ALU.add))
                    ch.after(v.tensor_scalar(cnti[:, 1], cnti[:, 0], PB.bit_length() - 1, None, ALU.logical_shift_right))
                    ch.after(v.tensor_copy(nb[:, :], cnti[:, 1]))
                    ch.after(tt_(tt, before, nb[:, :].unsqueeze(1).broadcast_to([P, E, E]), ALU.mult))
                    ch.after(v.tensor_reduce(first[:, :], tt, AX.X, ALU.add))
                    ch.after(v.tensor_scalar(base[:, :], first[:, :], float(PB), None, ALU.mult))
                    ch.after(tt_(rank, pr.rearrange("p (t e) -> p t e", e=E), under(base[:, :]), ALU.add))
                    for k, oh in enumerate((oh1, oh2)):
                        ch.after(tt_(t1, rank, oh, ALU.mult))
                        ch.after(v.tensor_reduce(mt[:, :], t1, AX.X, ALU.add))
                        ch.after(v.tensor_copy(M.pos[:, k], mt[:, :]))
                    ch.after(v.tensor_scalar(part[:, 0], M.pos[:, :, :], P.bit_length() - 1, None, ALU.logical_shift_right))
                    ch.after(v.tensor_scalar(part[:, 1], M.pos[:, :, :], P - 1, None, ALU.bitwise_and))
                    ch.after(v.tensor_copy(partf, part))

                def names(k):
                    wide = lambda a, w: a.unsqueeze(2).broadcast_to([P, NT, w])
                    upto = lambda w: count[:, 0:w].unsqueeze(1).broadcast_to([P, NT, w])
                    tt_(hot_row[:, k], wide(partf[:, 1, k], P), upto(P), ALU.is_equal).then_inc(hot_ok, 1)
                    ch.after(tt_(hot, wide(partf[:, 0, k], NP), upto(NP), ALU.is_equal))
                    v.tensor_scalar(hot_tile[:, k, :, 0], hot, row[:, 0:1], None, ALU.mult).then_inc(hot_ok, 1)
                    ch.after(tt_(hot_tile[:, k, :, 1], hot, wide(count[:, 0:NT], NP), ALU.mult))
                    dve.sem_inc(hot_ok, 1)

                def name_places():
                    dve.wait_ge(named, 1)
                    ch.after(v.tensor_copy(rowsum, px[:, 0:NP]))
                    ch.after(v.scalar_tensor_tensor(out=rowsum, in0=px[:, NP:2 * NP], scalar=float(P), in1=rowsum,
                                                    op0=ALU.mult, op1=ALU.add))
                    ch.after(v.tensor_copy(M.token[:, :], rowsum))

                def tables():
                    ch.after(tt_(mt[:, :], m1[:, :], m2[:, :], ALU.add))
                    ch.after(v.reciprocal(mt[:, :], mt[:, :]))
                    ch.after(tt_(M.wt[:, 0], m1[:, :], mt[:, :], ALU.mult))
                    ch.after(tt_(M.wt[:, 1], m2[:, :], mt[:, :], ALU.mult))
                    ch.after(tt_(M.cmb[:, :, :], oh1, over(M.wt[:, 0]), ALU.mult))
                    ch.after(tt_(t1, oh2, over(M.wt[:, 1]), ALU.mult))
                    ch.after(tt_(M.cmb[:, :, :], M.cmb[:, :, :], t1, ALU.add))
                    ch.after(tt_(first[:, :], first[:, :], nb[:, :], ALU.add))
                    ch.after(tt_(cmp, first[:, :].unsqueeze(1).broadcast_to([P, NBLK, E]),
                                 blk.unsqueeze(2).broadcast_to([P, NBLK, E]), ALU.is_le))
                    ch.after(v.tensor_reduce(bef[:, :], cmp, AX.X, ALU.add))
                    ch.after(v.tensor_scalar(M.be[:, :], bef[:, :], float(E - 1), None, ALU.min))

                dve.sem_inc(y_lo, 2)
                dve.sem_inc(so_ok, 2)
                dve.sem_inc(y_ok, 2)
                h_low(0, 0, 0)
                weights(0)
                dve.wait_ge(wa_hi, 1)
                nc.vector.tensor_tensor(wa[:, 1], waf[:, :, :], wa[:, 0].bitcast(F32), ALU.subtract).then_inc(wa_ok, 1)
                for c in range(1, DC):
                    h_low(0, 0, c)
                dve.wait_ge(bias_t, 1)
                nc.vector.tensor_copy(bT[:, :, :], po[:, 0, 0:FC * 2 * SH].rearrange("p (f a) -> p f a", f=FC)).then_inc(bias_ok, 1)
                weights(1)
                N.stats(dve, 0)
                dve.wait_ge(g_in, 16 * B)
                dve.wait_ge(b_in, 16 * (B - 1))
                dve.wait_ge(bias_ok, 1)

                def body(j, last):
                    for u in range(2):
                        b = j * 2 + u
                        more = not (last and u)
                        for m in range(NU):
                            e, f = m // FC, m % FC
                            n = b * NU + m
                            dve.wait_ge(up, n + 1)
                            dve.wait_ge(ge, n + 1)
                            nc.vector.scalar_tensor_tensor(out=y[:, m % 2], in0=pg[:, m % 2, 1], scalar=bT[:, f, SH + e:SH + e + 1],
                                                           in1=y[:, m % 2], op0=ALU.add, op1=ALU.mult).then_inc(y_ok, 1)
                            if more:
                                h_low(b + 1, 1 - u, m)
                            dve.wait_ge(y_hi, n + 1)
                            nc.vector.tensor_tensor(yT[:, m, 1], y[:, m % 2], yT[:, m, 0].bitcast(F32), ALU.subtract).then_inc(y_lo, 1)
                            if not more:
                                if m == 0:
                                    best()
                                elif m == 1:
                                    places()
                                elif m - 2 < TOP:
                                    names(m - 2)
                        if not more:
                            name_places()
                            tables()
                            dve.wait_ge(last_base, 1)
                        for t in range(TB):
                            update(b, t, t % 2)

                assert NU == 2 + TOP
                run(dve, body)

            @block.tensor
            def _(pe):
                def x_trans(b, c, begin=False):
                    if not begin:
                        pe.wait_ge(h_lo, b * DC + c)
                    for t in range(TB):
                        m = nc.tensor.transpose(px[:, t * P:(t + 1) * P], hx[:, t, c * P:(c + 1) * P], K.ident[:, :])
                    m.then_inc(x_t, 1)

                def router(b, u):
                    pe.wait_ge(h_lo, b * DC + DC)
                    split3(nc, pl[0:E, :], [(wa[:, 0, c], wa[:, 1, c], hT[:, u, c, 0], hT[:, u, c, 1])
                                            for c in range(DC)]).then_inc(lg, 1)

                pe.wait_ge(hx_in, 16)
                for c in range(DC):
                    x_trans(0, c, c == 0)
                pe.wait_ge(wa_in, 48)
                for f in range(FC):
                    m = nc.tensor.transpose(po[:, 0, f * 2 * SH:(f + 1) * 2 * SH], bst[:, f * P:(f + 1) * P],
                                            K.ident[0:2 * SH, 0:2 * SH])
                m.then_inc(bias_t, 1)
                pe.wait_ge(wa_ok, 1)
                router(0, 0)
                pe.wait_ge(w_lo, 2)

                def body(j, last):
                    for u in range(2):
                        b = j * 2 + u
                        more = not (last and u)
                        for m in range(NU):
                            e, f = m // FC, m % FC
                            pe.wait_ge(y_ok, b * NU + m + 1)
                            if e:
                                pe.wait_ge(w_lo, 4)
                            for a, done in ((0, gate), (1, up)):
                                o = slice(a * F + f * P, a * F + (f + 1) * P)
                                split3(nc, pg[:, m % 2, a], [(w1[:, e, c, 0, o], w1[:, e, c, 1, o], hT[:, u, c, 0], hT[:, u, c, 1])
                                                             for c in range(DC)]).then_inc(done, 1)
                            if m == 0:
                                pe.wait_ge(lt_ok, b + 1)
                                for t in range(TB):
                                    k = nc.tensor.transpose(pl[:, t * E:(t + 1) * E], lt[:, t * P:(t + 1) * P], K.ident[0:E, 0:E])
                                k.then_inc(lg_t, 1)
                            if more:
                                if m == 0:
                                    pe.wait_ge(hx_in, b * 16 + 32)
                                x_trans(b + 1, m)
                            if not more and m == 1:
                                pe.wait_ge(mb_ok, 1)
                                pe.wait_ge(zero, 1)
                                nc.tensor.matmul(pr, tri[:, :], mb[:, :, :].rearrange("p t e -> p (t e)"), start=True, stop=False)
                                for t in range(NT - 1):
                                    nc.tensor.matmul(pr[:, (t + 1) * E:].rearrange("p (t e) -> p t e", e=E), ones[:, :],
                                                     mb[:, t:t + 1].broadcast_to([P, NT - 1 - t, E]), start=False, stop=t == NT - 2)
                                for t in range(NT):
                                    r = nc.tensor.matmul(pn, ones[:, :], mb[:, t], start=t == 0, stop=t == NT - 1)
                                r.then_inc(ranks, 1)
                            if not more and m == NU - 1:
                                for k in range(TOP):
                                    pe.wait_ge(hot_ok, 3 * k + 3)
                                    for t in range(NT):
                                        r = nc.tensor.matmul(px[:, 0:2 * NP], hot_row[:, k, t],
                                                             hot_tile[:, k, t].rearrange("p a n -> p (a n)"),
                                                             start=k == 0 and t == 0, stop=k == TOP - 1 and t == NT - 1)
                                r.then_inc(named, 1)
                        for t in range(TB):
                            q = slice(t * P, (t + 1) * P)
                            pe.wait_ge(so_ok, b * TB + t + 1)
                            n = 0
                            for m in range(NU):
                                if t == 0:
                                    pe.wait_ge(y_lo, b * NU + m + 3)
                                for s_, w in ((0, 0), (0, 1), (1, 0)):
                                    k = nc.tensor.matmul(po[:, t % 2], yT[:, m, s_, q], w2[:, m // FC, m % FC, w],
                                                         start=n == 0, stop=n == 3 * NU - 1)
                                    n += 1
                            k.then_inc(oo, 1)
                        if more:
                            pe.wait_ge(aff_ok, b + 1)
                            router(b + 1, 1 - u)

                run(pe, body)


def stage_routed(K, M):
    nc = K.nc
    LB = NBLK // 2
    PT = PB // P
    PW = 2
    NF = 2 * FC
    with ExitStack() as ctx:
        sb = lambda n, s, d: K.sb(n, s, d, ctx)
        st1 = sb("e_st1", [P, 2, DC, 2, F], F32)
        st2 = sb("e_st2", [P, 2, FC, D], F32)
        w1 = sb("e_w1", [P, 2, DC, 2, 2 * F], F32R)
        w2 = sb("e_w2", [P, 2, FC, 2, D], F32R)
        bst = sb("e_bst", [E, 2, F], F32)
        bT = sb("e_bT", [P, E, NF], F32)
        bias = sb("e_bias", [P, 2, NF], F32)
        idx = sb("e_idx", [P, 2, PT], I32)
        xg = sb("e_xg", [P, 2, PT, D], F32)
        xT = sb("e_xT", [P, 2, 2, DC, PB], F32R)
        y = sb("e_y", [P, 2, FC, PB], F32)
        yT = sb("e_yT", [P, 2, 2, FC, PB], F32R)
        yo = sb("e_yo", [P, 2, PT, D], F32)
        px = K.ps("e_px", [P, DC, PB], F32, ctx)
        pg = K.ps("e_pg", [P, 2, NF, PB], F32, ctx)
        po = K.ps("e_po", [P, PT, D], F32, ctx)
        two = lambda n: [K.sem(n + "0"), K.sem(n + "1")]
        b_st, b_tr, tab_ok = K.sem("e_b_st"), K.sem("e_b_tr"), K.sem("e_tab_ok")
        w1_in, w2_in, b_in, x_in, y_out = two("e_w1_in"), two("e_w2_in"), two("e_b_in"), two("e_x_in"), two("e_y_out")
        step_p, step_s = K.sem("e_step_p"), K.sem("e_step_s")
        w1_hi, w1_lo, w1_lop = K.sem("e_w1_hi"), K.sem("e_w1_lo"), K.sem("e_w1_lop")
        w2_hi, w2_lo, idx_ok = K.sem("e_w2_hi"), K.sem("e_w2_lo"), K.sem("e_idx_ok")
        tr, x_hi, x_lo = K.sem("e_tr"), K.sem("e_x_hi"), K.sem("e_x_lo")
        gate, up, ge, y_ok = K.sem("e_gate"), K.sem("e_up"), K.sem("e_ge"), K.sem("e_y_ok")
        y_hi, y_lo, oo = K.sem("e_y_hi"), K.sem("e_y_lo"), K.sem("e_oo")
        yo_a, yo_v = K.sem("e_yo_a"), K.sem("e_yo_v")

        def run(eng, head, body, tail):
            head()
            body(0, True, LB)
            with eng.Fori(1, LB - 2) as j:
                body(j, False, LB)
            body(LB - 2, False, 1)
            body(LB - 1, False, 0)
            tail()

        with nc.Block() as block:

            @block.sync
            def _(sp):
                rg = K.ins["L0_ffn_rg"].rearrange("e (c p) f -> e p c f", p=P)
                rw1 = K.ins["L0_ffn_rw1"].rearrange("e (c p) f -> e p c f", p=P)
                rw2 = K.ins["L0_ffn_rw2"].rearrange("e (c p) n -> e p c n", p=P)

                def expert(k):
                    sp.sem_inc(step_s, 1)
                    return bass.ds(sp.value_load(M.be[0:1, bass.ds(k, 1)], min_val=0, max_val=E - 1), 1)

                def load1(k, u):
                    one = expert(k)
                    sp.dma_start(st1[:, u, :, 0], rg[one].rearrange("a p c f -> (a p) c f")).then_inc(w1_in[u], 16)
                    sp.dma_start(st1[:, u, :, 1], rw1[one].rearrange("a p c f -> (a p) c f")).then_inc(w1_in[u], 16)

                def load2(k, u):
                    one = expert(k)
                    sp.dma_start(st2[:, u], rw2[one].rearrange("a p c n -> (a p) c n")).then_inc(w2_in[u], 16)

                def load_bias(k, u):
                    one = expert(k)
                    sp.dma_start(bias[:, u], bT[:, one].rearrange("p a n -> p (a n)")).then_inc(b_in[u], 16)

                def store(k, u):
                    sp.wait_ge(yo_a, k + 1)
                    sp.wait_ge(yo_v, k + 1)
                    sp.dma_start(K.y_d[bass.ds(k * PB, PB), :].rearrange("(i p) n -> p i n", p=P), yo[:, u]).then_inc(y_out[u], 16)

                def head():
                    sp.dma_start(bst[:, 0], K.ins["L0_ffn_rgb"]).then_inc(b_st, 16)
                    sp.dma_start(bst[:, 1], K.ins["L0_ffn_rb1"]).then_inc(b_st, 16)
                    load1(0, 0)
                    load1(1, 1)
                    load2(0, 0)
                    load2(1, 1)
                    sp.wait_ge(tab_ok, 1)
                    load_bias(0, 0)
                    load_bias(1, 1)
                    sp.wait_ge(w1_lo, 1)
                    sp.wait_ge(w1_lop, 1)
                    load1(2, 0)

                def body(j, first, left):
                    for u in range(2):
                        k = j * 2 + u
                        if left * 2 - u >= 2:
                            sp.wait_ge(w1_lo, k + 2)
                            sp.wait_ge(w1_lop, k + 2)
                            load1(k + 3, 1 - u)
                        if left:
                            sp.wait_ge(w2_lo, k + 1)
                            load2(k + 2, u)
                        if not first:
                            store(k - 2, u)
                        if left:
                            sp.wait_ge(y_ok, k * 2 + 2)
                            load_bias(k + 2, u)

                def tail():
                    for u in range(2):
                        store(NBLK - 2 + u, u)
                    for u in range(2):
                        sp.wait_ge(y_out[u], 16 * LB + 16)

                run(sp, head, body, tail)

            @block.gpsimd
            def _(pool):
                def gather(k, u):
                    pool.wait_ge(idx_ok, k + 1)
                    pool.sem_inc(step_p, 1)
                    for i in range(PT):
                        pool.indirect_dma_start(out=xg[:, u, i], out_offset=None, in_=K.h2_d,
                                                in_offset=bass.IndirectOffsetOnAxis(ap=idx[:, u, i:i + 1], axis=0)
                                                ).then_inc(x_in[u], 16)

                def w1_low(k, u):
                    pool.wait_ge(w1_hi, k + 1)
                    nc.gpsimd.tensor_tensor(w1[:, u, 0:PW, 1].rearrange("p c (a f) -> p c a f", a=2), st1[:, u, 0:PW],
                                            w1[:, u, 0:PW, 0].rearrange("p c (a f) -> p c a f", a=2).bitcast(F32),
                                            ALU.subtract).then_inc(w1_lop, 1)

                def head():
                    gather(0, 0)
                    gather(1, 1)
                    w1_low(0, 0)
                    gather(2, 0)

                def body(j, first, left):
                    for u in range(2):
                        k = j * 2 + u
                        if left or not u:
                            w1_low(k + 1, 1 - u)
                        if left * 2 - u >= 2:
                            gather(k + 3, 1 - u)

                run(pool, head, body, lambda: None)

            @block.scalar
            def _(act):
                def w1_high(k, j, u, free=True):
                    act.wait_ge(w1_in[u], j * 32 + 32)
                    if free:
                        act.wait_ge(up, k - 1)
                    nc.scalar.activation(w1[:, u, :, 0].rearrange("p c (a f) -> p c a f", a=2), st1[:, u], ACT.Copy).then_inc(w1_hi, 1)

                def w2_high(k, j, u, first):
                    act.wait_ge(w2_in[u], j * 16 + 16)
                    if not first:
                        act.wait_ge(oo, k - 1)
                    nc.scalar.activation(w2[:, u, :, 0], st2[:, u], ACT.Copy).then_inc(w2_hi, 1)

                def x_high(k, u):
                    act.wait_ge(tr, k + 1)
                    for c in range(0, DC, 2):
                        nc.scalar.activation(xT[:, u, 0, c:c + 2], px[:, c:c + 2], ACT.Copy).then_inc(x_hi, 1)

                def gelu(k, j, u, first):
                    act.wait_ge(b_in[u], j * 16 + 16)
                    act.wait_ge(gate, k + 1)
                    if not first:
                        act.wait_ge(y_lo, k - 1)
                    for f in range(FC):
                        nc.scalar.activation(y[:, u, f], pg[:, u, f], ACT.Gelu, bias=bias[:, u, f:f + 1]).then_inc(ge, 1)

                def y_high(k, u):
                    act.wait_ge(y_ok, k * 2 + 2)
                    nc.scalar.activation(yT[:, u, 0], y[:, u], ACT.Copy).then_inc(y_hi, 1)

                def rows(k, j, u):
                    act.wait_ge(oo, k + 1)
                    act.wait_ge(y_out[u], j * 16 + 16)
                    nc.scalar.activation(yo[:, u, 0], po[:, 0], ACT.Copy).then_inc(yo_a, 1)

                def head():
                    w1_high(0, 0, 0, False)
                    x_high(0, 0)

                def body(j, first, left):
                    for u in range(2):
                        k = j * 2 + u
                        if u or not first:
                            y_high(k - 1, 1 - u)
                        if left or not u:
                            w1_high(k + 1, j + u, 1 - u, u or not first)
                        w2_high(k, j, u, first)
                        if not first:
                            rows(k - 2, j - 1, u)
                        gelu(k, j, u, first)
                        if left or not u:
                            x_high(k + 1, 1 - u)

                def tail():
                    rows(NBLK - 2, LB - 1, 0)
                    y_high(NBLK - 1, 1)
                    rows(NBLK - 1, LB - 1, 1)

                run(act, head, body, tail)

            @block.vector
            def _(dve):
                def w1_low(k, u):
                    dve.wait_ge(w1_hi, k + 1)
                    nc.vector.tensor_tensor(w1[:, u, PW:DC, 1].rearrange("p c (a f) -> p c a f", a=2), st1[:, u, PW:DC],
                                            w1[:, u, PW:DC, 0].rearrange("p c (a f) -> p c a f", a=2).bitcast(F32),
                                            ALU.subtract).then_inc(w1_lo, 1)

                def w2_low(k, u):
                    dve.wait_ge(w2_hi, k + 1)
                    nc.vector.tensor_tensor(w2[:, u, :, 1], st2[:, u], w2[:, u, :, 0].bitcast(F32), ALU.subtract).then_inc(w2_lo, 1)

                def name(k, u):
                    nc.vector.tensor_copy(idx[:, u], M.token[:, bass.ds(k * PT, PT)]).then_inc(idx_ok, 1)

                def x_low(k, u):
                    for n, c in enumerate(range(0, DC, 2)):
                        dve.wait_ge(x_hi, k * 2 + n + 1)
                        nc.vector.tensor_tensor(xT[:, u, 1, c:c + 2], px[:, c:c + 2], xT[:, u, 0, c:c + 2].bitcast(F32),
                                                ALU.subtract).then_inc(x_lo, 1)

                def times(k, u):
                    dve.wait_ge(up, k + 1)
                    for f in range(FC):
                        dve.wait_ge(ge, k * 2 + f + 1)
                        nc.vector.scalar_tensor_tensor(out=y[:, u, f], in0=pg[:, u, FC + f], scalar=bias[:, u, FC + f:FC + f + 1],
                                                       in1=y[:, u, f], op0=ALU.add, op1=ALU.mult).then_inc(y_ok, 1)

                def y_low(k, u):
                    dve.wait_ge(y_hi, k + 1)
                    nc.vector.tensor_tensor(yT[:, u, 1], y[:, u], yT[:, u, 0].bitcast(F32), ALU.subtract).then_inc(y_lo, 1)

                def rows(k, j, u):
                    dve.wait_ge(oo, k + 1)
                    dve.wait_ge(y_out[u], j * 16 + 16)
                    nc.vector.tensor_copy(yo[:, u, 1], po[:, 1]).then_inc(yo_v, 1)

                def head():
                    for u in range(2):
                        dve.sem_inc(y_out[u], 16)
                    name(0, 0)
                    name(1, 1)
                    dve.wait_ge(b_tr, 1)
                    nc.vector.tensor_copy(bT[:, :, :], po[:, 1, 0:NF * E].rearrange("p (a e) -> p e a", e=E)).then_inc(tab_ok, 1)
                    w1_low(0, 0)
                    x_low(0, 0)
                    name(2, 0)

                def body(j, first, left):
                    for u in range(2):
                        k = j * 2 + u
                        if u or not first:
                            y_low(k - 1, 1 - u)
                        if left or not u:
                            w1_low(k + 1, 1 - u)
                        w2_low(k, u)
                        if not first:
                            rows(k - 2, j - 1, u)
                        times(k, u)
                        if left or not u:
                            x_low(k + 1, 1 - u)
                        if left * 2 - u >= 2:
                            name(k + 3, 1 - u)

                def tail():
                    rows(NBLK - 2, LB - 1, 0)
                    y_low(NBLK - 1, 1)
                    rows(NBLK - 1, LB - 1, 1)

                run(dve, head, body, tail)

            @block.tensor
            def _(pe):
                def x_trans(k, j, u):
                    pe.wait_ge(x_in[u], j * 16 * PT + 16 * PT)
                    for c in range(DC):
                        for i in range(PT):
                            m = nc.tensor.transpose(px[:, c, i * P:(i + 1) * P], xg[:, u, i, c * P:(c + 1) * P], K.ident[:, :])
                    m.then_inc(tr, 1)

                def first_(k, u):
                    pe.wait_ge(x_lo, k * 2 + 2)
                    pe.wait_ge(w1_lo, k + 1)
                    pe.wait_ge(w1_lop, k + 1)
                    for n in range(NF):
                        f_ = slice(n * P, (n + 1) * P)
                        m = split3(nc, pg[:, u, n], [(w1[:, u, c, 0, f_], w1[:, u, c, 1, f_], xT[:, u, 0, c], xT[:, u, 1, c])
                                                     for c in range(DC)])
                        if n == FC - 1:
                            m.then_inc(gate, 1)
                    m.then_inc(up, 1)

                def second(k, u, first):
                    pe.wait_ge(y_lo, k + 1)
                    pe.wait_ge(w2_lo, k + 1)
                    if not first:
                        pe.wait_ge(yo_a, k)
                        pe.wait_ge(yo_v, k)
                    for i in range(PT):
                        t_ = slice(i * P, (i + 1) * P)
                        m = split3(nc, po[:, i], [(yT[:, u, 0, f, t_], yT[:, u, 1, f, t_], w2[:, u, f, 0], w2[:, u, f, 1])
                                                  for f in range(FC)])
                    m.then_inc(oo, 1)

                def head():
                    pe.wait_ge(b_st, 32)
                    for n in range(NF):
                        m = nc.tensor.transpose(po[:, 1, n * E:(n + 1) * E], bst[:, n // FC, (n % FC) * P:(n % FC + 1) * P],
                                                K.ident[0:E, 0:E])
                    m.then_inc(b_tr, 1)
                    x_trans(0, 0, 0)

                def body(j, first, left):
                    for u in range(2):
                        k = j * 2 + u
                        first_(k, u)
                        if left or not u:
                            x_trans(k + 1, j + u, 1 - u)
                        if u or not first:
                            second(k - 1, 1 - u, first)

                run(pe, head, body, lambda: second(NBLK - 1, 1, False))


def stage_combine(K, M):
    nc = K.nc
    NS = TB
    with ExitStack() as ctx:
        sb = lambda n, s, d: K.sb(n, s, d, ctx)
        at = sb("f_at", [P, NS, TOP], I32)
        b2 = sb("f_b2", [E, D], F32)
        cm = sb("f_cm", [P, NS, E], F32)
        cT = sb("f_cT", [E, NS, P], F32)
        r = sb("f_r", [P, NS, TOP, D], F32)
        o = sb("f_o", [P, NS, D], F32)
        pc = K.ps("f_pc", [E, NS, 512], F32, ctx)
        pb = K.ps("f_pb", [P, NS, D], F32, ctx)
        step_p = K.sem("f_step_p")
        at_ok, dch, o_ok, b2_in = K.sem("f_at_ok"), K.sem("f_dch"), K.sem("f_o_ok"), K.sem("f_b2_in")
        ct, ct_ok, bb = K.sem("f_ct"), K.sem("f_ct_ok"), K.sem("f_bb")
        r_in = [K.sem(f"f_r_in{u}") for u in range(NS)]
        o_out = [K.sem(f"f_o_out{u}") for u in range(NS)]

        with nc.Block() as block:

            @block.sync
            def _(sp):
                ov = K.out.rearrange("b (t p) n -> (b t) p n", p=P)
                sp.dma_start(b2[:, :], K.ins["L0_ffn_rb2"]).then_inc(b2_in, 16)
                with sp.Fori(0, NT // NS) as j:
                    for u in range(NS):
                        t = j * NS + u
                        sp.wait_ge(o_ok, t + 1)
                        sp.dma_start(ov[bass.ds(t, 1)].rearrange("a p n -> p (a n)"), o[:, u]).then_inc(o_out[u], 16)
                for u in range(NS):
                    sp.wait_ge(o_out[u], 16 * (NT // NS) + 16)

            @block.gpsimd
            def _(pool):
                with pool.Fori(0, NT // NS) as j:
                    for u in range(NS):
                        t = j * NS + u
                        pool.wait_ge(at_ok, t * 2 + 1)
                        pool.sem_inc(step_p, 1)
                        for k in range(TOP):
                            pool.indirect_dma_start(out=r[:, u, k], out_offset=None, in_=K.y_d,
                                                    in_offset=bass.IndirectOffsetOnAxis(ap=at[:, u, k:k + 1], axis=0)
                                                    ).then_inc(r_in[u], 16)

            @block.scalar
            def _(act):
                with act.Fori(0, NT // NS) as j:
                    for u in range(NS):
                        act.wait_ge(ct, j * NS + u + 1)
                        nc.scalar.activation(cT[:, u], pc[:, u, 0:P], ACT.Copy).then_inc(ct_ok, 1)

            @block.tensor
            def _(pe):
                pe.wait_ge(b2_in, 16)
                with pe.Fori(0, NT // NS) as j:
                    for u in range(NS):
                        t = j * NS + u
                        pe.wait_ge(at_ok, t * 2 + 2)
                        nc.tensor.transpose(pc[:, u, 0:P], cm[:, u], K.ident[:, :]).then_inc(ct, 1)
                        pe.wait_ge(ct_ok, t + 1)
                        nc.tensor.matmul(pb[:, u], cT[:, u], b2[:, :], start=True, stop=True).then_inc(bb, 1)

            @block.vector
            def _(dve):
                def places(t, u):
                    nc.vector.tensor_copy(at[:, u], M.pos[:, :, bass.ds(t, 1)].rearrange("p k a -> p (k a)")).then_inc(at_ok, 1)
                    nc.vector.tensor_copy(cm[:, u], M.cmb[:, bass.ds(t, 1)].rearrange("p a e -> p (a e)")).then_inc(at_ok, 1)

                def tiles(j, more):
                    for u0 in range(0, NS, 2):
                        both = [(j * NS + u, u) for u in (u0, u0 + 1)]
                        done = (j * NS + u0) * 3
                        row = M.gb[:, bass.ds(j, 1)].rearrange("p a n -> p (a n)")
                        for k in range(TOP):
                            for i, (t, u) in enumerate(both):
                                if k:
                                    dve.wait_ge(dch, done + i + 1)
                                else:
                                    dve.wait_ge(r_in[u], j * 32 + 32)
                                    dve.wait_ge(bb, t + 1)
                                nc.vector.scalar_tensor_tensor(out=r[:, u, 0], in0=r[:, u, k], scalar=M.wt[:, k, bass.ds(t, 1)],
                                                               in1=r[:, u, 0] if k else pb[:, u],
                                                               op0=ALU.mult, op1=ALU.add).then_inc(dch, 1)
                        for i, (t, u) in enumerate(both):
                            dve.wait_ge(dch, done + 2 + i + 1)
                            nc.vector.tensor_tensor(r[:, u, 0], r[:, u, 0], row, ALU.mult).then_inc(dch, 1)
                        for i, (t, u) in enumerate(both):
                            dve.wait_ge(dch, done + 4 + i + 1)
                            dve.wait_ge(o_out[u], j * 16 + 16)
                            nc.vector.tensor_tensor(o[:, u], r[:, u, 0], M.base[:, bass.ds(t, 1)].rearrange("p a n -> p (a n)"),
                                                    ALU.add).then_inc(o_ok, 1)
                        if more:
                            for t, u in both:
                                dve.wait_ge(o_ok, t + 1)
                                places(t + NS, u)

                for u in range(NS):
                    dve.sem_inc(o_out[u], 16)
                for u in range(NS):
                    places(u, u)
                with dve.Fori(0, NT // NS - 1) as j:
                    tiles(j, True)
                tiles(NT // NS - 1, False)


class Kept:

    def __init__(self, K, ctx):
        self.gb = K.sb("gb", [P, B, D], F32, ctx)
        self.base = K.sb("base", [P, NT, D], F32, ctx)
        self.aff = K.sb("aff", [P, NT, E], F32, ctx)
        self.wt = K.sb("wt", [P, TOP, NT], F32, ctx)
        self.cmb = K.sb("cmb", [P, NT, E], F32, ctx)
        self.pos = K.sb("pos", [P, TOP, NT], I32, ctx)
        self.token = K.sb("token", [P, NBLK * PB // P], I32, ctx)
        self.be = K.sb("be", [P, NBLK], I32, ctx)


def program(nc, ins, out):
    with ExitStack() as ctx:
        K = Kernel(nc, ctx, ins, out)
        with ExitStack() as kept:
            N = SecondNorm(K, kept)
            with ExitStack() as att:
                Mhl = K.sb("Mhl", [P, H, 2, D], F32R, att)
                modcol = K.sb("modcol", [P, B, 2, DC], F32, att)
                stage_weights(K, N, Mhl, modcol)
                stage_project(K, N, modcol)
                stage_attention(K, N, Mhl)
            K.free_sems()
            M = Kept(K, kept)
            stage_shared(K, N, M)
            stage_routed(K, M)
            stage_combine(K, M)


_INS = ["L0_attn_x", "L0_attn_wq", "L0_attn_wkv_a", "L0_attn_wkv_b", "L0_attn_wo", "L0_ffn_wa", "L0_ffn_rg",
        "L0_ffn_rgb", "L0_ffn_rw1", "L0_ffn_rb1", "L0_ffn_rw2", "L0_ffn_rb2", "L0_ffn_sg", "L0_ffn_sgb",
        "L0_ffn_sw1", "L0_ffn_sb1", "L0_ffn_sw2", "L0_ffn_sb2", "L0_c", "L0_wmod"]


def constants():
    inv = (np.float32(1.0) / np.float32(10000.0) ** (np.arange(HALF, dtype=np.float32) * np.float32(2.0)
                                                     / np.float32(ROPE))).astype(np.float32)
    ang = (np.arange(S, dtype=np.float32)[:, None] * inv[None, :]).astype(np.float32)
    cos, sin = np.tile(np.cos(ang).T, (P // HALF, 1)), np.tile(np.sin(ang).T, (P // HALF, 1))
    sign = np.where(np.arange(P) < ROPE, 1.0, -1.0)[:, None]
    rope = np.stack([cos * SCALE, sin * SCALE, cos, sin * sign]).astype(np.float32)
    k, m = np.arange(P)[:, None], np.arange(P)[None, :]
    const = np.stack([k == m, np.where(m > k, -1e30, 0.0), k < m]).astype(np.float32)
    e, f = np.arange(E)[:, None], np.arange(E)[None, :]
    small = np.concatenate([E - np.arange(E), (f < e).ravel(), np.arange(NBLK), np.arange(P)]).astype(np.float32)[None, :]
    row = np.arange(P, dtype=np.float32)[:, None]
    return {"c_rope": rope, "c_const": const, "c_small": small, "c_row": row}


def kernel(**inputs):
    import concourse.bacc as _bacc
    from concourse.bass_utils import run_bass_kernel_spmd as _run

    nc = _bacc.Bacc("TRN2", target_bir_lowering=False, num_devices=1)
    arrays, ins = {}, {}
    for name, a in [(n, inputs[n]) for n in _INS] + list(constants().items()):
        a = np.ascontiguousarray(a)
        arrays[f"in_{name}"] = a
        ins[name] = nc.dram_tensor(f"in_{name}", a.shape, mybir.dt.from_np(a.dtype), kind="ExternalInput").ap()
    out = nc.dram_tensor("out_0", (B, S, D), F32, kind="ExternalOutput").ap()
    program(nc, ins, out)
    r = _run(nc, [arrays], core_ids=[0])
    return r.results[0]["out_0"]
```
